# Optimizing a Trainium2 kernel written in Bass

```python
import numpy as np
import jax
import jax.numpy as jnp

def _softmax(x, axis=-1):
    return jax.nn.softmax(x, axis=axis)

def _gelu(x):
    return jax.nn.gelu(x, approximate=True)

def _silu(x):
    return jax.nn.silu(x)

def _sigmoid(x):
    return jax.nn.sigmoid(x)

def _layernorm(x, axis=-1, eps=1e-05):
    m = jnp.mean(x, axis=axis, keepdims=True)
    v = jnp.var(x, axis=axis, keepdims=True)
    return (x - m) / jnp.sqrt(v + eps)

def _scatter_add(tgt, idx, src, axis=0):
    return tgt.at[idx].add(src)

def _segment_sum(src, seg, n):
    return jax.ops.segment_sum(src, seg, n)
kernel_name = 'mk_xattn_ffn_d2_seqx_r4_27d458'

def setup_inputs(seed: int=0):
    np.random.seed(seed)
    _w = jnp.asarray

    def _rec_inputs():
        import jax
        import jax.numpy as jnp
        _rk = jax.random.key(seed)
        x = -0.000125 + 0.9999 * jax.random.normal(jax.random.fold_in(_rk, 1), (8, 256, 256), jnp.float32)
        _lenS = 256 - jax.random.randint(jax.random.fold_in(_rk, 7), (8,), 0, max(1, 256 // 4) + 1, jnp.int32)
        _lenS2 = 256 - jax.random.randint(jax.random.fold_in(_rk, 8), (8,), 0, max(1, 256 // 4) + 1, jnp.int32)
        _ctx_768P = jax.random.normal(jax.random.fold_in(_rk, 11), (8, 16, 192), jnp.float32)
        _ctx_768c = jax.random.dirichlet(jax.random.fold_in(_rk, 511), 0.3 * jnp.ones((16,), jnp.float32), (8, 256))
        _ctx_768t = jnp.einsum('bsk,bkd->bsd', _ctx_768c, _ctx_768P)
        _ctx_768t = _ctx_768t * jax.lax.rsqrt(jnp.mean(jnp.square(_ctx_768t)) + 1e-12) * 0.953939
        ctx_768 = 0.00272024 + 0.999456 * (_ctx_768t + 0.3 * jax.random.normal(jax.random.fold_in(_rk, 611), (8, 256, 192), jnp.float32))
        return (x, ctx_768)
    x, ctx_768 = _rec_inputs()

    def _L0_xattn_setup():
        import jax, jax.numpy as jnp
        import numpy as np
        QUERY_DIM = 256
        CONTEXT_DIM = 192
        HEADS = 8
        DIM_HEAD = 64
        INNER = HEADS * DIM_HEAD
        key = jax.random.key(seed)
        ks = jax.random.split(key, 7)
        B, S, L = (8, 1024, 77)
        x = jax.random.normal(ks[0], (B, S, QUERY_DIM), dtype=jnp.float32)
        context = jax.random.normal(ks[1], (B, L, CONTEXT_DIM), dtype=jnp.float32)
        Wq = jax.random.normal(ks[2], (QUERY_DIM, INNER), dtype=jnp.float32) * QUERY_DIM ** (-0.5)
        Wk = jax.random.normal(ks[3], (CONTEXT_DIM, INNER), dtype=jnp.float32) * CONTEXT_DIM ** (-0.5)
        Wv = jax.random.normal(ks[4], (CONTEXT_DIM, INNER), dtype=jnp.float32) * CONTEXT_DIM ** (-0.5)
        Wo = jax.random.normal(ks[5], (INNER, QUERY_DIM), dtype=jnp.float32) * INNER ** (-0.5)
        bo = jax.random.normal(ks[6], (QUERY_DIM,), dtype=jnp.float32) * 0.01
        return {'x': x, 'context': context, 'Wq': Wq, 'Wk': Wk, 'Wv': Wv, 'Wo': Wo, 'bo': bo}
    _L0_xattn_all = _L0_xattn_setup()
    _L0_xattn_in = {k: v for k, v in _L0_xattn_all.items() if k in ('Wq', 'Wk', 'Wv', 'Wo', 'bo')}
    del _L0_xattn_all

    def _L0_ffn_setup():
        import jax, jax.numpy as jnp
        import numpy as np
        B, N, D, H, E = (4, 256, 256, 16, 8)
        DK = D // H
        HID = 4 * D
        EPS = 1e-05

        def _layernorm(x, w, b):
            m = jnp.mean(x, axis=-1, keepdims=True)
            v = jnp.mean(jnp.square(x - m), axis=-1, keepdims=True)
            return (x - m) * jax.lax.rsqrt(v + EPS) * w + b

        def _msa(x, w_qkv, w_proj):
            b, n, d = x.shape
            qkv = (x @ w_qkv).reshape(b, n, 3, H, DK)
            q = qkv[:, :, 0].transpose(0, 2, 1, 3)
            k = qkv[:, :, 1].transpose(0, 2, 1, 3)
            v = qkv[:, :, 2].transpose(0, 2, 1, 3)
            attn = jnp.einsum('bhnd,bhmd->bhnm', q, k) * (1.0 / np.sqrt(DK))
            attn = jax.nn.softmax(attn, axis=-1)
            y = jnp.einsum('bhnm,bhmd->bhnd', attn, v)
            y = y.transpose(0, 2, 1, 3).reshape(b, n, d)
            return y @ w_proj

        def _moe_mlp(x, gate_w, gate_b, w1, w2):
            b, n, d = x.shape
            xf = x.reshape(b * n, d)
            logits = xf @ gate_w + gate_b
            one_hot = jax.nn.one_hot(jnp.argmax(logits, axis=-1), E, dtype=xf.dtype)
            h = jax.nn.gelu(jnp.einsum('td,edh->teh', xf, w1), approximate=True)
            y = jnp.einsum('teh,ehd->ted', h, w2)
            out = jnp.einsum('te,ted->td', one_hot, y)
            return out.reshape(b, n, d)
        key = jax.random.key(seed)
        ks = jax.random.split(key, 8)
        s = 0.02
        return {'x': jax.random.normal(ks[0], (B, N, D), jnp.float32), 'ln1_w': jnp.ones((D,), jnp.float32), 'ln1_b': jnp.zeros((D,), jnp.float32), 'w_qkv': jax.random.normal(ks[1], (D, 3 * D), jnp.float32) * s, 'w_proj': jax.random.normal(ks[2], (D, D), jnp.float32) * s, 'ln2_w': jnp.ones((D,), jnp.float32), 'ln2_b': jnp.zeros((D,), jnp.float32), 'gate_w': jax.random.normal(ks[3], (D, E), jnp.float32) * s, 'gate_b': jnp.zeros((E,), jnp.float32), 'w1': jax.random.normal(ks[4], (E, D, HID), jnp.float32) * s, 'w2': jax.random.normal(ks[5], (E, HID, D), jnp.float32) * s}
    _L0_ffn_all = _L0_ffn_setup()
    _L0_ffn_in = {k: v for k, v in _L0_ffn_all.items() if k in ('ln1_w', 'ln1_b', 'w_qkv', 'w_proj', 'ln2_w', 'ln2_b', 'gate_w', 'gate_b', 'w1', 'w2')}
    del _L0_ffn_all

    def _L1_xattn_setup():
        import jax, jax.numpy as jnp
        import numpy as np
        IMG_DIM, TXT_DIM, HID = (256, 192, 256)
        B, LQ, LK = (8, 512, 512)
        key = jax.random.key(seed)
        ks = jax.random.split(key, 8)
        s_img = 1.0 / np.sqrt(IMG_DIM)
        s_txt = 1.0 / np.sqrt(TXT_DIM)
        return {'image_features': jax.random.normal(ks[0], (B, LQ, IMG_DIM), jnp.float32), 'text_features': jax.random.normal(ks[1], (B, LK, TXT_DIM), jnp.float32), 'Wq': jax.random.uniform(ks[2], (IMG_DIM, HID), jnp.float32, -s_img, s_img), 'bq': jax.random.uniform(ks[3], (HID,), jnp.float32, -s_img, s_img), 'Wk': jax.random.uniform(ks[4], (TXT_DIM, HID), jnp.float32, -s_txt, s_txt), 'bk': jax.random.uniform(ks[5], (HID,), jnp.float32, -s_txt, s_txt), 'Wv': jax.random.uniform(ks[6], (TXT_DIM, HID), jnp.float32, -s_txt, s_txt), 'bv': jax.random.uniform(ks[7], (HID,), jnp.float32, -s_txt, s_txt)}
    _L1_xattn_all = _L1_xattn_setup()
    _L1_xattn_in = {k: v for k, v in _L1_xattn_all.items() if k in ('Wq', 'bq', 'Wk', 'bk', 'Wv', 'bv')}
    del _L1_xattn_all

    def _L1_ffn_setup():
        import jax, jax.numpy as jnp
        import numpy as np
        B, L, D = (2, 512, 256)
        E = 15
        H = D * 1
        K = 3
        T = 1.0
        key = jax.random.key(seed)
        ks = jax.random.split(key, 12)
        s = 0.02
        return {'x': jax.random.normal(ks[0], (B, L, D), dtype=jnp.float32), 'router_W': jax.random.normal(ks[1], (D, E), dtype=jnp.float32) * s, 'router_b': jnp.zeros((E,), dtype=jnp.float32), 'sW1': jax.random.normal(ks[2], (D, H), dtype=jnp.float32) * s, 'sb1': jnp.zeros((H,), dtype=jnp.float32), 'sW2': jax.random.normal(ks[3], (H, D), dtype=jnp.float32) * s, 'sb2': jnp.zeros((D,), dtype=jnp.float32), 'eW1': jax.random.normal(ks[4], (E, D, H), dtype=jnp.float32) * s, 'eb1': jnp.zeros((E, H), dtype=jnp.float32), 'eW2': jax.random.normal(ks[5], (E, H, D), dtype=jnp.float32) * s, 'eb2': jnp.zeros((E, D), dtype=jnp.float32)}
    _L1_ffn_all = _L1_ffn_setup()
    _L1_ffn_in = {k: v for k, v in _L1_ffn_all.items() if k in ('router_W', 'router_b', 'sW1', 'sb1', 'sW2', 'sb2', 'eW1', 'eb1', 'eW2', 'eb2')}
    del _L1_ffn_all
    return {'x': x, 'ctx_768': ctx_768, 'L0_xattn_Wq': _L0_xattn_in['Wq'], 'L0_xattn_Wk': _L0_xattn_in['Wk'], 'L0_xattn_Wv': _L0_xattn_in['Wv'], 'L0_xattn_Wo': _L0_xattn_in['Wo'], 'L0_xattn_bo': _L0_xattn_in['bo'], 'L0_ffn_ln1_w': _L0_ffn_in['ln1_w'], 'L0_ffn_ln1_b': _L0_ffn_in['ln1_b'], 'L0_ffn_w_qkv': _L0_ffn_in['w_qkv'], 'L0_ffn_w_proj': _L0_ffn_in['w_proj'], 'L0_ffn_ln2_w': _L0_ffn_in['ln2_w'], 'L0_ffn_ln2_b': _L0_ffn_in['ln2_b'], 'L0_ffn_gate_w': _L0_ffn_in['gate_w'], 'L0_ffn_gate_b': _L0_ffn_in['gate_b'], 'L0_ffn_w1': _L0_ffn_in['w1'], 'L0_ffn_w2': _L0_ffn_in['w2'], 'L1_xattn_Wq': _L1_xattn_in['Wq'], 'L1_xattn_bq': _L1_xattn_in['bq'], 'L1_xattn_Wk': _L1_xattn_in['Wk'], 'L1_xattn_bk': _L1_xattn_in['bk'], 'L1_xattn_Wv': _L1_xattn_in['Wv'], 'L1_xattn_bv': _L1_xattn_in['bv'], 'L1_ffn_router_W': _L1_ffn_in['router_W'], 'L1_ffn_router_b': _L1_ffn_in['router_b'], 'L1_ffn_sW1': _L1_ffn_in['sW1'], 'L1_ffn_sb1': _L1_ffn_in['sb1'], 'L1_ffn_sW2': _L1_ffn_in['sW2'], 'L1_ffn_sb2': _L1_ffn_in['sb2'], 'L1_ffn_eW1': _L1_ffn_in['eW1'], 'L1_ffn_eb1': _L1_ffn_in['eb1'], 'L1_ffn_eW2': _L1_ffn_in['eW2'], 'L1_ffn_eb2': _L1_ffn_in['eb2']}

def reference(x, ctx_768, L0_xattn_Wq, L0_xattn_Wk, L0_xattn_Wv, L0_xattn_Wo, L0_xattn_bo, L0_ffn_ln1_w, L0_ffn_ln1_b, L0_ffn_w_qkv, L0_ffn_w_proj, L0_ffn_ln2_w, L0_ffn_ln2_b, L0_ffn_gate_w, L0_ffn_gate_b, L0_ffn_w1, L0_ffn_w2, L1_xattn_Wq, L1_xattn_bq, L1_xattn_Wk, L1_xattn_bk, L1_xattn_Wv, L1_xattn_bv, L1_ffn_router_W, L1_ffn_router_b, L1_ffn_sW1, L1_ffn_sb1, L1_ffn_sW2, L1_ffn_sb2, L1_ffn_eW1, L1_ffn_eb1, L1_ffn_eW2, L1_ffn_eb2):
    import jax
    import jax.numpy as jnp

    def _L0_xattn_ref(x, context, Wq, Wk, Wv, Wo, bo):
        import jax, jax.numpy as jnp
        import numpy as np
        QUERY_DIM = 256
        CONTEXT_DIM = 192
        HEADS = 8
        DIM_HEAD = 64
        INNER = HEADS * DIM_HEAD
        B, S, _ = x.shape
        L = context.shape[1]
        scale = DIM_HEAD ** (-0.5)
        q = (x @ Wq).reshape(B, S, HEADS, DIM_HEAD).transpose(0, 2, 1, 3)
        k = (context @ Wk).reshape(B, L, HEADS, DIM_HEAD).transpose(0, 2, 1, 3)
        v = (context @ Wv).reshape(B, L, HEADS, DIM_HEAD).transpose(0, 2, 1, 3)
        attn = jnp.einsum('bhsd,bhld->bhsl', q, k) * scale
        attn = jax.nn.softmax(attn, axis=-1)
        out = jnp.einsum('bhsl,bhld->bhsd', attn, v)
        out = out.transpose(0, 2, 1, 3).reshape(B, S, INNER)
        return out @ Wo + bo

    def _L0_ffn_ref(x, ln1_w, ln1_b, w_qkv, w_proj, ln2_w, ln2_b, gate_w, gate_b, w1, w2):
        import jax, jax.numpy as jnp
        import numpy as np
        B, N, D, H, E = (4, 256, 256, 16, 8)
        DK = D // H
        HID = 4 * D
        EPS = 1e-05

        def _layernorm(x, w, b):
            m = jnp.mean(x, axis=-1, keepdims=True)
            v = jnp.mean(jnp.square(x - m), axis=-1, keepdims=True)
            return (x - m) * jax.lax.rsqrt(v + EPS) * w + b

        def _msa(x, w_qkv, w_proj):
            b, n, d = x.shape
            qkv = (x @ w_qkv).reshape(b, n, 3, H, DK)
            q = qkv[:, :, 0].transpose(0, 2, 1, 3)
            k = qkv[:, :, 1].transpose(0, 2, 1, 3)
            v = qkv[:, :, 2].transpose(0, 2, 1, 3)
            attn = jnp.einsum('bhnd,bhmd->bhnm', q, k) * (1.0 / np.sqrt(DK))
            attn = jax.nn.softmax(attn, axis=-1)
            y = jnp.einsum('bhnm,bhmd->bhnd', attn, v)
            y = y.transpose(0, 2, 1, 3).reshape(b, n, d)
            return y @ w_proj

        def _moe_mlp(x, gate_w, gate_b, w1, w2):
            b, n, d = x.shape
            xf = x.reshape(b * n, d)
            logits = xf @ gate_w + gate_b
            one_hot = jax.nn.one_hot(jnp.argmax(logits, axis=-1), E, dtype=xf.dtype)
            h = jax.nn.gelu(jnp.einsum('td,edh->teh', xf, w1), approximate=True)
            y = jnp.einsum('teh,ehd->ted', h, w2)
            out = jnp.einsum('te,ted->td', one_hot, y)
            return out.reshape(b, n, d)
        x = x + _msa(_layernorm(x, ln1_w, ln1_b), w_qkv, w_proj)
        x = x + _moe_mlp(_layernorm(x, ln2_w, ln2_b), gate_w, gate_b, w1, w2)
        return x

    def _L1_xattn_ref(image_features, text_features, Wq, bq, Wk, bk, Wv, bv):
        import jax, jax.numpy as jnp
        import numpy as np
        IMG_DIM, TXT_DIM, HID = (256, 192, 256)
        B, LQ, LK = (8, 512, 512)
        query = jnp.einsum('bqi,ih->bqh', image_features, Wq) + bq
        key = jnp.einsum('bkt,th->bkh', text_features, Wk) + bk
        value = jnp.einsum('bkt,th->bkh', text_features, Wv) + bv
        scale = 1.0 / jnp.sqrt(jnp.asarray(HID, query.dtype))
        scores = jnp.einsum('bqh,bkh->bqk', query, key) * scale
        weights = jax.nn.softmax(scores, axis=-1)
        attended = jnp.einsum('bqk,bkh->bqh', weights, value)
        return attended

    def _L1_ffn_ref(x, router_W, router_b, sW1, sb1, sW2, sb2, eW1, eb1, eW2, eb2):
        import jax, jax.numpy as jnp
        import numpy as np
        B, L, D = (2, 512, 256)
        E = 15
        H = D * 1
        K = 3
        T = 1.0
        b, l, d = x.shape
        n = b * l
        xt = x.reshape(n, d)
        shared = jax.nn.relu(xt @ sW1 + sb1) @ sW2 + sb2
        logits = xt @ router_W + router_b
        probs = jax.nn.softmax(logits / T, axis=-1)
        top_p, top_i = jax.lax.top_k(probs, K)
        cw = jnp.zeros((n, E), dtype=probs.dtype)
        cw = cw.at[jnp.arange(n)[:, None], top_i].set(top_p)
        h = jax.nn.relu(jnp.einsum('nd,edh->neh', xt, eW1) + eb1)
        ye = jnp.einsum('neh,ehd->ned', h, eW2) + eb2
        routed = jnp.einsum('ned,ne->nd', ye, cw)
        return (shared + routed).reshape(b, l, d)
    x = x + _L0_xattn_ref(_layernorm(x, axis=-1), ctx_768, L0_xattn_Wq, L0_xattn_Wk, L0_xattn_Wv, L0_xattn_Wo, L0_xattn_bo)
    x = x + _L0_ffn_ref(_layernorm(x, axis=-1), L0_ffn_ln1_w, L0_ffn_ln1_b, L0_ffn_w_qkv, L0_ffn_w_proj, L0_ffn_ln2_w, L0_ffn_ln2_b, L0_ffn_gate_w, L0_ffn_gate_b, L0_ffn_w1, L0_ffn_w2)
    x = x + _L1_xattn_ref(_layernorm(x, axis=-1), ctx_768, L1_xattn_Wq, L1_xattn_bq, L1_xattn_Wk, L1_xattn_bk, L1_xattn_Wv, L1_xattn_bv)
    x = x + _L1_ffn_ref(_layernorm(x, axis=-1), L1_ffn_router_W, L1_ffn_router_b, L1_ffn_sW1, L1_ffn_sb1, L1_ffn_sW2, L1_ffn_sb2, L1_ffn_eW1, L1_ffn_eb1, L1_ffn_eW2, L1_ffn_eb2)
    return x

_drawn_inputs = setup_inputs


def setup_inputs(seed=0):
    import zlib

    import numpy as np

    out = dict(_drawn_inputs(seed))
    spreads = {'L0_ffn_ln1_w': (1.0, 0.6),
     'L0_ffn_ln1_b': (0.0, 0.8),
     'L0_ffn_ln2_w': (1.0, 0.561),
     'L0_ffn_ln2_b': (0.0, 0.395),
     'L0_ffn_gate_b': (0.0, 0.1),
     'L1_ffn_router_b': (0.0, 0.8),
     'L1_ffn_sb1': (0.0, 0.8),
     'L1_ffn_sb2': (0.0, 0.303),
     'L1_ffn_eb1': (0.0, 0.8),
     'L1_ffn_eb2': (0.0, 0.8)}
    factors = {'L0_xattn_bo': 5.708,
     'L1_xattn_Wq': 3.438,
     'L1_xattn_bq': 8.0,
     'L1_xattn_Wk': 3.393,
     'L1_xattn_bk': 64.0,
     'L1_xattn_bv': 2.89,
     'L1_ffn_router_W': 6.203,
     'L1_ffn_eW1': 8.0,
     'L1_ffn_eW2': 8.0,
     'L1_ffn_sW1': 3.225}
    for name, (base, spread) in spreads.items():
        noise = np.random.default_rng([zlib.crc32(name.encode()), seed]).standard_normal(out[name].shape)
        drawn = base * np.exp(spread * noise) if base else spread * noise
        out[name] = jnp.asarray(drawn.astype(out[name].dtype))
    for name, factor in factors.items():
        out[name] = (out[name] * factor).astype(out[name].dtype)
    return out
```

```python
from contextlib import ExitStack

import concourse.bass as bass
from concourse import mybir

F32 = mybir.dt.float32
BF16 = mybir.dt.bfloat16
I32 = mybir.dt.int32
ALU = mybir.AluOpType
ACT = mybir.ActivationFunctionType
AX = mybir.AxisListType.X

P = 128
B, S, D = 8, 256, 256
NT = B * S // P
QT = S // P
KD = D // P
CP, KC = 96, 2
H0, DH0 = 8, 64
H1, DH1, PAD1 = 16, 16, 32
EPS = 1e-5
E0, HID0 = 8, 1024
M0 = HID0 // P
E1, HID1, TOP1 = 15, 256, 3
M1 = HID1 // P
TILES0 = (NT * P + E0 * (P - 1)) // P
TILES1 = (TOP1 * NT * P + E1 * (P - 1)) // P
NC = 16


class Chain:

    def __init__(self, eng, sem, base):
        self.eng, self.sem, self.base, self.k = eng, sem, base, 0

    def done(self, ins):
        self.k += 1
        ins.then_inc(self.sem, 1)

    def wait(self):
        self.eng.wait_ge(self.sem, self.base + self.k)


class Carve:

    def __init__(self, region, words):
        self.region, self.words, self.at = region, words, 0

    def take(self, parts, *shape, dt=F32):
        n = 1
        for s in shape:
            n *= s
        w = n if dt != BF16 else (n + 1) // 2
        v = self.region[0:parts, self.at:self.at + w]
        self.at += (w + 7) // 8 * 8
        assert self.at <= self.words, (self.at, self.words)
        if dt != F32:
            v = v.bitcast(dt)
        names = "abcd"[:len(shape)]
        if len(shape) > 1:
            v = v.rearrange("p (" + " ".join(names) + ") -> p " + " ".join(names), **dict(zip(names, shape)))
        return v


def tile2(t, b):
    return t[:, bass.ds(b * (QT * D), QT * D)]


def tile1(t, b, q):
    return t[:, bass.ds(b * (QT * D) + q * D, D)]


def layernorm(dve, ch, src, dst, ln, nth, done=None):
    stats, mv, var, rstd = ln["stats"], ln["mv"], ln["var"], ln["rstd"]
    for q in range(QT):
        ch.done(dve.bn_stats(stats[:, q, :], src(q)))
    ch.wait()
    dve.memset(ln["spare"], 0.0)
    for q in range(QT):
        ch.done(dve.bn_aggr(mv[:, q, :], stats[:, q, :]))
    ch.wait()
    dve.tensor_scalar(var, mv[:, :, 1], EPS, None, ALU.add).then_inc(ln["var_ready"], 1)
    dve.wait_ge(ln["rstd_ready"], nth + 1)
    for q in range(QT):
        ins = dve.tensor_scalar(dst(q), src(q), mv[:, q, 0:1], rstd[:, q:q + 1], ALU.subtract, ALU.mult)
        if done is None:
            ch.done(ins)
    if done is not None:
        ins.then_inc(done, 1)


LN_STEPS = 4


def ln_buffers(m, cv, tag):
    return dict(stats=cv.take(P, QT, 6), mv=cv.take(P, QT, 2), var=cv.take(P, QT), rstd=cv.take(P, QT),
                var_ready=m["sem"](tag + "var_ready"), rstd_ready=m["sem"](tag + "rstd_ready"), power=m["power"][:, :], spare=cv.take(P, 1))


def ln_power(pool, ln, nth):
    pool.wait_ge(ln["var_ready"], nth + 1)
    pool.tensor_tensor(ln["rstd"], ln["var"], ln["power"], ALU.pow).then_inc(ln["rstd_ready"], 1)


def build(nc, a, out):
    ctx = ExitStack()
    with ctx:
        def sb(name, shape, dt=F32):
            return ctx.enter_context(nc.sbuf_tensor(name, shape, dt))

        def sem(name):
            return ctx.enter_context(nc.semaphore(name))

        def scratch(name, shape):
            return nc.dram_tensor(name, shape, F32, kind="Internal").ap()

        m = {}
        m["x"] = sb("x_all", [P, NT * D])
        m["z"] = sb("z_all", [P, NT * D])
        W1WORDS = E0 * KD * HID0
        m["w1"] = sb("w1_all", [P, W1WORDS])
        m["w2"] = sb("w2_all", [P, W1WORDS])
        RW = 11000
        m["r"] = sb("r_all", [P, RW])
        m["RW"], m["W1WORDS"] = RW, W1WORDS
        m["ident"] = sb("ident", [P, P])
        m["power"] = sb("power", [P, QT])
        m["upper"] = sb("upper", [P, P], BF16)
        m["ones"] = sb("ones", [P, P], BF16)
        m["oh_bf"] = sb("oh_bf", [P, NT * E1], BF16)
        m["logits"] = sb("logits", [P, NT * 16])
        m["slots"] = sb("slots", [P, TOP1, NT], I32)
        m["owner"] = sb("owner", [P, 64], I32)
        m["top_p"] = sb("top_p", [P, TOP1, NT])
        m["cw"] = sb("cw", [P, NT, E1 + 1])
        m["psum"] = [ctx.enter_context(nc.psum_tensor(f"bank{i}", [P, 512], F32)) for i in range(8)]
        m["zs0"] = scratch("zs0", [TILES0 * P, D])
        m["ys0"] = scratch("ys0", [TILES0 * P, D])
        m["zs1"] = scratch("zs1", [TILES1 * P, D])
        m["ys1"] = scratch("ys1", [TILES1 * P, D])
        for s in ("const_in", "w1_in", "w2_in", "w_self_in", "zero_fill", "w_cross1_in", "we_in"):
            m[s] = sem(s)
        m["sem"] = sem
        cross0(nc, a, m)
        self0(nc, a, m)
        route(nc, a, m, 0)
        moe(nc, a, m, 0)
        join0(nc, a, m)
        cross1(nc, a, m)
        route(nc, a, m, 1)
        moe(nc, a, m, 1)
        join1(nc, a, m, out)



def heads_pe(pe, c, g, b):
    n = g["heads"]
    for s in range(n + 2):
        if s < n:
            h = s
            if h >= 2:
                pe.wait_ge(c["exp_done"], b * n + h - 1)
            lo, mt = g["rows"](h)
            for q in range(QT):
                ins = pe.matmul(c["s_ps"][h % 2][:, q * S:(q + 1) * S],
                                c["qT"][lo:lo + g["dh"], mt, q * P:(q + 1) * P],
                                c["kT"][lo:lo + g["dh"], mt, :], start=True, stop=True)
            ins.then_inc(c["s_full"], 1)
        if 1 <= s <= n:
            h = s - 1
            pe.wait_ge(c["exp_done"], b * n + h + 1)
            if h >= 2:
                evac = c["pt_act"] if h % 2 == 0 else c["pt_dve"]
                pe.wait_ge(evac, b * (n // 2) + h // 2)
            for kt in range(QT):
                for q in range(QT):
                    at = kt * S + q * P
                    ins = pe.transpose(c["pt_ps"][h % 2][:, at:at + P],
                                       c["p"][:, h % 2, q, kt * P:(kt + 1) * P], c["ident"])
            ins.then_inc(c["pt_full"], 1)
        if s >= 2:
            h = s - 2
            evac = c["pt_act"] if h % 2 == 0 else c["pt_dve"]
            pe.wait_ge(evac, b * (n // 2) + h // 2 + 1)
            if h >= 2:
                pe.wait_ge(c["att_done"], b * n + h - 1)
            w = g["dv"] + 1
            for q in range(QT):
                for kt in range(QT):
                    ins = pe.matmul(c["o_ps"][h % 2][:, q * w:(q + 1) * w],
                                    c["pT"][:, h % 2, kt, q * P:(q + 1) * P],
                                    c["v"][:, kt, h, :], start=(kt == 0), stop=(kt == QT - 1))
            ins.then_inc(c["o_full"], 1)


def heads_act(act, c, g, b):
    n = g["heads"]
    for s in range(n + 1):
        if s < n:
            h = s
            act.wait_ge(c["max_done"], b * n + h + 1)
            if h >= 2:
                act.wait_ge(c["pt_full"], b * n + h - 1)
            for q in range(QT):
                ins = act.activation(c["p"][:, h % 2, q, :], c["s_ps"][h % 2][:, q * S:(q + 1) * S],
                                     ACT.Exp, bias=c["nmax"][:, h % 2, q:q + 1])
            ins.then_inc(c["exp_done"], 1)
        if s >= 1 and (s - 1) % 2 == 0:
            h = s - 1
            act.wait_ge(c["pt_full"], b * n + h + 1)
            if h >= 2:
                act.wait_ge(c["o_full"], b * n + h - 1)
            act.copy(c["pT"][:, 0, :, :].rearrange("p k q -> p (k q)"), c["pt_ps"][0][:, :])\
               .then_inc(c["pt_act"], 1)


def heads_dve(dve, ch, c, g, b):
    n, w = g["heads"], g["dv"] + 1

    def finish(h):
        dve.wait_ge(c["o_full"], b * n + h + 1)
        o = c["o_ps"][h % 2][:, 0:QT * w].rearrange("p (q w) -> p q w", q=QT)
        ch.done(dve.reciprocal(c["rec"][:, h % 2, :], o[:, :, w - 1]))
        ch.wait()
        dve.tensor_tensor(c["att"][:, :, h * g["dv"]:(h + 1) * g["dv"]], o[:, :, 0:w - 1],
                          c["rec"][:, h % 2, :].unsqueeze(2).to_broadcast([P, QT, w - 1]),
                          ALU.mult).then_inc(c["att_done"], 1)

    for s in range(n + 2):
        if s < n:
            h = s
            dve.wait_ge(c["s_full"], b * n + h + 1)
            dve.tensor_reduce(c["nmax"][:, h % 2, :], c["s_ps"][h % 2][:, :].rearrange("p (q k) -> p q k", q=QT),
                              AX, ALU.max, negate=True).then_inc(c["max_done"], 1)
        if 1 <= s <= n and (s - 1) % 2 == 1:
            h = s - 1
            dve.wait_ge(c["pt_full"], b * n + h + 1)
            if h >= 2:
                dve.wait_ge(c["o_full"], b * n + h - 1)
            dve.tensor_copy(c["pT"][:, 1, :, :].rearrange("p k q -> p (k q)"), c["pt_ps"][1][:, :])\
               .then_inc(c["pt_dve"], 1)
        if s >= 3:
            finish(s - 3)
    finish(n - 1)


def head_buffers(m, cv, heads, dv, tag):
    sem, ps = m["sem"], m["psum"]
    return dict(
        p=cv.take(P, 2, QT, S), pT=cv.take(P, 2, QT, S), v=cv.take(P, QT, heads, dv + 1),
        att=cv.take(P, QT, heads * dv), nmax=cv.take(P, 2, QT), rec=cv.take(P, 2, QT),
        s_ps=ps[0:2], pt_ps=ps[2:4], o_ps=ps[4:6], ident=m["ident"][:, :],
        s_full=sem(tag + "s_full"), max_done=sem(tag + "max_done"), exp_done=sem(tag + "exp_done"),
        pt_full=sem(tag + "pt_full"), pt_act=sem(tag + "pt_act"), pt_dve=sem(tag + "pt_dve"),
        o_full=sem(tag + "o_full"), att_done=sem(tag + "att_done"),
        job=sem(tag + "job"), act_ev=sem(tag + "act_ev"), dve_ev=sem(tag + "dve_ev"),
        xn_ready=sem(tag + "xn_ready"), own=sem(tag + "own"), start=sem(tag + "start"))



def cross0(nc, a, m):
    cv = Carve(m["w2"], m["W1WORDS"])
    c = head_buffers(m, cv, H0, DH0, "c0_")
    wq = cv.take(P, KD, H0 * DH0)
    wk = cv.take(CP, KC, H0 * DH0)
    wv = cv.take(CP, KC, H0 * DH0)
    wo = cv.take(P, H0 * DH0 // P, D)
    bo = cv.take(P, D)
    ctxT = cv.take(CP, KC, S)
    xn = cv.take(P, QT, D)
    xb = cv.take(P, QT * D)
    xnT = cv.take(P, KD, S)
    c["qT"] = cv.take(P, 4, S)
    c["kT"] = cv.take(P, 4, S)
    attT = cv.take(P, 4, S)
    ln = ln_buffers(m, cv, "c0_")
    g = dict(heads=H0, dh=DH0, dv=DH0, rows=lambda h: (DH0 * (h % 2), h // 2))
    sem = m["sem"]
    x_in, wq_in, wkv_in, wo_in, ctx_in = (sem("c0_" + s) for s in ("x_in", "wq_in", "wkv_in", "wo_in", "ctx_in"))
    xb_ready = sem("c0_xb_ready")
    L = m["psum"][6:8]
    x, ident = m["x"], m["ident"]
    NJ, NA, ND = 10, 5, 5
    OWN = LN_STEPS + H0

    with nc.Block() as block:
        @block.sync
        def _(sp):
            sp.dma_start(x[:, :], a["x"]).then_inc(x_in, 16)
            sp.dma_start(wk, a["wk0"]).then_inc(wkv_in, 16)
            sp.dma_start(wv, a["wv0"]).then_inc(wkv_in, 16)
            sp.dma_start(ctxT, a["ctxT"][0]).then_inc(ctx_in, 16)
            sp.dma_start(m["ident"][:, :], a["ident"]).then_inc(m["const_in"], 16)
            sp.dma_start(wq, a["wq0"]).then_inc(wq_in, 16)
            sp.dma_start(wo, a["wo0"]).then_inc(wo_in, 16)
            sp.dma_start(bo, a["bo0"].partition_broadcast(P)).then_inc(wo_in, 16)
            sp.dma_start(m["upper"][:, :], a["upper"]).then_inc(m["const_in"], 16)
            sp.dma_start(m["ones"][:, :], a["ones"]).then_inc(m["const_in"], 16)
            wself = self0_weights(m)
            for name in ("wq", "wk", "wv", "wp", "ln1", "ln2w", "ln2b", "gw", "gb"):
                src = a["s_" + name]
                if name in ("ln2w", "ln2b", "gb"):
                    src = src.partition_broadcast(P)
                sp.dma_start(wself[name], src).then_inc(m["w_self_in"], 16)
            w1v = m["w1"][:, :].rearrange("p (e n) -> p e n", e=E0)
            for b in range(B):
                if b + 1 < B:
                    sp.wait_ge(c["job"], NJ * b + 4)
                    sp.dma_start(ctxT, a["ctxT"][b + 1]).then_inc(ctx_in, 16)
                sp.dma_start(w1v[:, b, :], a["w1"][b]).then_inc(m["w1_in"], 16)

        @block.gpsimd
        def _(pool):
            zero = m["z"][:, 0:D]
            pool.memset(m["z"][:, :], 0.0).then_inc(c["start"], 1)
            pool.memset(c["v"].rearrange("p q h w -> p (q h) w")[:, :, DH0:DH0 + 1], 1.0).then_inc(c["start"], 1)
            pool.wait_ge(c["start"], 2)
            pool.memset(m["cw"][:, :, :], 1.0).then_inc(c["start"], 1)
            pool.memset(m["power"][:, :], -0.5).then_inc(c["start"], 1)
            for name, tiles in (("zs0", TILES0), ("zs1", TILES1)):
                for t in range(0, tiles, NT):
                    k = min(NT, tiles - t)
                    pool.dma_start(m[name][t * P:(t + k) * P, :].rearrange("(t p) d -> p t d", p=P),
                                   m["z"][:, 0:k * D].rearrange("p (t d) -> p t d", d=D))\
                        .then_inc(m["zero_fill"], 16)
            pool.wait_ge(c["start"], 4)
            pool.wait_ge(x_in, 16)
            pool.wait_ge(wo_in, 32)
            with pool.Fori(0, B) as b:
                ln_power(pool, ln, b)
                pool.wait_ge(c["xn_ready"], b + 1)
                pool.tensor_tensor(xb.rearrange("p (q d) -> p q d", q=QT),
                                   tile2(x, b).rearrange("p (q d) -> p q d", q=QT),
                                   bo.unsqueeze(1).to_broadcast([P, QT, D]), ALU.add).then_inc(xb_ready, 1)

        @block.tensor
        def _(pe):
            pe.wait_ge(wkv_in, 32)
            pe.wait_ge(m["const_in"], 48)
            pe.wait_ge(wq_in, 16)
            pe.wait_ge(wo_in, 32)
            pe.wait_ge(c["start"], 4)
            with pe.Fori(0, B) as b:
                pe.wait_ge(ctx_in, 16 * b + 16)
                for j in range(2):
                    if j == 0:
                        pe.wait_ge(c["dve_ev"], ND * b + 1)
                    else:
                        pe.wait_ge(c["dve_ev"], ND * b + 1)
                    for i in range(2):
                        mt = 2 * j + i
                        for k in range(KC):
                            ins = pe.matmul(L[j][:, i * S:(i + 1) * S], wk[:, k, mt * P:(mt + 1) * P],
                                            ctxT[:, k, :], start=(k == 0), stop=(k == KC - 1))
                    ins.then_inc(c["job"], 1)
                for q in range(QT):
                    if q == 0:
                        pe.wait_ge(c["act_ev"], NA * b + 1)
                    else:
                        pe.wait_ge(c["dve_ev"], ND * b + 2)
                    for k in range(KC):
                        ins = pe.matmul(L[q][:, :], ctxT[:, k, q * P:(q + 1) * P], wv[:, k, :],
                                        start=(k == 0), stop=(k == KC - 1))
                    ins.then_inc(c["job"], 1)
                pe.wait_ge(c["xn_ready"], b + 1)
                pe.wait_ge(c["act_ev"], NA * b + 2)
                for k in range(KD):
                    for q in range(QT):
                        ins = pe.transpose(L[0][:, k * S + q * P:k * S + (q + 1) * P],
                                           xn[:, q, k * P:(k + 1) * P], ident[:, :])
                ins.then_inc(c["job"], 1)
                pe.wait_ge(c["act_ev"], NA * b + 3)
                pe.wait_ge(c["dve_ev"], ND * b + 3)
                for j in (1, 0):
                    for i in range(2):
                        mt = 2 * (1 - j) + i
                        for k in range(KD):
                            ins = pe.matmul(L[j][:, i * S:(i + 1) * S], wq[:, k, mt * P:(mt + 1) * P],
                                            xnT[:, k, :], start=(k == 0), stop=(k == KD - 1))
                    ins.then_inc(c["job"], 1)
                pe.wait_ge(c["act_ev"], NA * b + 4)
                pe.wait_ge(c["dve_ev"], ND * b + 4)
                heads_pe(pe, c, g, b)
                pe.wait_ge(c["att_done"], H0 * b + H0)
                for j in (1, 0):
                    for i in range(2):
                        ft = 2 * (1 - j) + i
                        for q in range(QT):
                            ins = pe.transpose(L[j][:, i * S + q * P:i * S + (q + 1) * P],
                                               c["att"][:, q, ft * P:(ft + 1) * P], ident[:, :])
                    ins.then_inc(c["job"], 1)
                pe.wait_ge(c["act_ev"], NA * b + 5)
                pe.wait_ge(c["dve_ev"], ND * b + 5)
                for q in range(QT):
                    for ft in range(4):
                        ins = pe.matmul(L[1][:, q * D:(q + 1) * D], attT[:, ft, q * P:(q + 1) * P], wo[:, ft, :],
                                        start=(ft == 0), stop=(ft == 3))
                ins.then_inc(c["job"], 1)

        @block.scalar
        def _(act):
            act.wait_ge(c["start"], 4)
            with act.Fori(0, B) as b:
                act.wait_ge(c["job"], NJ * b + 1)
                act.copy(c["kT"][:, 0:2, :].rearrange("p m s -> p (m s)"), L[0][:, :]).then_inc(c["act_ev"], 1)
                act.wait_ge(c["job"], NJ * b + 3)
                act.copy(c["v"][:, 0, :, 0:DH0], L[0][:, :].rearrange("p (h w) -> p h w", h=H0)).then_inc(c["act_ev"], 1)
                act.wait_ge(c["job"], NJ * b + 5)
                act.copy(xnT.rearrange("p k s -> p (k s)"), L[0][:, :]).then_inc(c["act_ev"], 1)
                act.wait_ge(c["job"], NJ * b + 7)
                act.mul(c["qT"][:, 2:4, :].rearrange("p m s -> p (m s)"), L[0][:, :], DH0 ** -0.5).then_inc(c["act_ev"], 1)
                heads_act(act, c, g, b)
                act.wait_ge(c["job"], NJ * b + 8)
                act.copy(attT[:, 0:2, :].rearrange("p m s -> p (m s)"), L[1][:, :]).then_inc(c["act_ev"], 1)

        @block.vector
        def _(dve):
            dve.wait_ge(x_in, 16)
            dve.nop().then_inc(c["dve_ev"], 1)
            dve.wait_ge(c["start"], 4)
            with dve.Fori(0, B) as b:
                ch = Chain(dve, c["own"], b * OWN)
                layernorm(dve, ch, lambda q: tile1(x, b, q), lambda q: xn[:, q, :], ln, b, c["xn_ready"])
                dve.wait_ge(c["job"], NJ * b + 2)
                dve.tensor_copy(c["kT"][:, 2:4, :].rearrange("p m s -> p (m s)"), L[1][:, :]).then_inc(c["dve_ev"], 1)
                dve.wait_ge(c["job"], NJ * b + 4)
                dve.tensor_copy(c["v"][:, 1, :, 0:DH0], L[1][:, :].rearrange("p (h w) -> p h w", h=H0)).then_inc(c["dve_ev"], 1)
                dve.wait_ge(c["job"], NJ * b + 6)
                dve.tensor_scalar(c["qT"][:, 0:2, :].rearrange("p m s -> p (m s)"), L[1][:, :], DH0 ** -0.5, None,
                                  ALU.mult).then_inc(c["dve_ev"], 1)
                heads_dve(dve, ch, c, g, b)
                dve.wait_ge(c["job"], NJ * b + 9)
                dve.tensor_copy(attT[:, 2:4, :].rearrange("p m s -> p (m s)"), L[0][:, :]).then_inc(c["dve_ev"], 1)
                dve.wait_ge(c["job"], NJ * b + 10)
                dve.wait_ge(xb_ready, b + 1)
                dve.tensor_tensor(tile2(x, b), L[1][:, :], xb, ALU.add).then_inc(c["dve_ev"], 1)
                assert ch.k == OWN, ch.k



def self0_weights(m):
    cv = Carve(m["r"], m["RW"])
    w = dict(wq=cv.take(P, KD, H1 * PAD1), wk=cv.take(P, KD, H1 * PAD1), wv=cv.take(P, KD, D), wp=cv.take(P, KD, D),
             ln1=cv.take(P, 2, KD), ln2w=cv.take(P, D), ln2b=cv.take(P, D), gw=cv.take(P, KD, E0), gb=cv.take(P, E0))
    w["carve"] = cv
    return w


def self0(nc, a, m):
    w = self0_weights(m)
    cv = w["carve"]
    c = head_buffers(m, cv, H1, DH1, "s0_")
    y0 = cv.take(P, QT, D)
    xn = cv.take(P, QT, D)
    zT = cv.take(P, KD, S)
    c["qT"] = cv.take(P, 4, S)
    c["kT"] = cv.take(P, 4, S)
    attT = cv.take(P, KD, S)
    ln = ln_buffers(m, cv, "s0_")
    g = dict(heads=H1, dh=DH1, dv=DH1, rows=lambda h: (PAD1 * (h % 4), h // 4))
    sem = m["sem"]
    n2_ready, z2_ready, z_kept = sem("s0_n2_ready"), sem("s0_z2_ready"), sem("s0_z_kept")
    L = m["psum"][6:8]
    x, z, ident = m["x"], m["z"], m["ident"]
    lg = m["logits"][:, 0:NT * E0]
    NJ, NA, ND = 10, 6, 4
    OWN = 3 * LN_STEPS + QT + H1 + 1

    with nc.Block() as block:
        @block.sync
        def _(sp):
            w2v = m["w2"][:, :].rearrange("p (e n) -> p e n", e=E0)
            for e in range(E0):
                sp.dma_start(w2v[:, e, :], a["w2"][e]).then_inc(m["w2_in"], 16)

        @block.gpsimd
        def _(pool):
            pool.memset(c["v"].rearrange("p q h w -> p (q h) w")[:, :, DH1:DH1 + 1], 1.0).then_inc(c["start"], 1)
            pool.wait_ge(m["w_self_in"], 16 * 9)
            pool.wait_ge(m["zero_fill"], 16 * 6)
            pool.nop().then_inc(c["start"], 1)
            with pool.Fori(0, B) as b:
                for k in range(3):
                    ln_power(pool, ln, 3 * b + k)
                pool.wait_ge(n2_ready, b + 1)
                pool.tensor_tensor(xn, xn, w["ln2w"].unsqueeze(1).to_broadcast([P, QT, D]), ALU.mult).then_inc(c["start"], 1)
                pool.wait_ge(c["start"], b + 3)
                pool.tensor_tensor(xn, xn, w["ln2b"].unsqueeze(1).to_broadcast([P, QT, D]), ALU.add).then_inc(z2_ready, 1)
                pool.wait_ge(z2_ready, b + 1)
                pool.tensor_copy(tile2(z, b), xn.rearrange("p q d -> p (q d)")).then_inc(z_kept, 1)

        @block.tensor
        def _(pe):
            pe.wait_ge(c["start"], 2)
            pe.wait_ge(m["w_self_in"], 16 * 9)
            with pe.Fori(0, B) as b:
                pe.wait_ge(c["xn_ready"], b + 1)
                pe.wait_ge(c["act_ev"], NA * b + 1)
                for k in range(KD):
                    for q in range(QT):
                        ins = pe.transpose(L[0][:, k * S + q * P:k * S + (q + 1) * P],
                                           xn[:, q, k * P:(k + 1) * P], ident[:, :])
                ins.then_inc(c["job"], 1)
                pe.wait_ge(c["act_ev"], NA * b + 2)
                pe.wait_ge(c["dve_ev"], ND * b + 1)
                for j in range(4):
                    if j == 2:
                        pe.wait_ge(c["dve_ev"], ND * b + 2)
                    if j == 3:
                        pe.wait_ge(c["act_ev"], NA * b + 3)
                    wt = w["wq"] if j < 2 else w["wk"]
                    for i in range(2):
                        mt = 2 * (j % 2) + i
                        for k in range(KD):
                            ins = pe.matmul(L[1 - j % 2][:, i * S:(i + 1) * S], wt[:, k, mt * P:(mt + 1) * P],
                                            zT[:, k, :], start=(k == 0), stop=(k == KD - 1))
                    ins.then_inc(c["job"], 1)
                pe.wait_ge(c["dve_ev"], ND * b + 3)
                for q in range(QT):
                    for k in range(KD):
                        ins = pe.matmul(L[1][:, q * D:(q + 1) * D], zT[:, k, q * P:(q + 1) * P], w["wv"][:, k, :],
                                        start=(k == 0), stop=(k == KD - 1))
                ins.then_inc(c["job"], 1)
                pe.wait_ge(c["act_ev"], NA * b + 5)
                heads_pe(pe, c, g, b)
                pe.wait_ge(c["att_done"], H1 * b + H1)
                for k in range(KD):
                    for q in range(QT):
                        ins = pe.transpose(L[0][:, k * S + q * P:k * S + (q + 1) * P],
                                           c["att"][:, q, k * P:(k + 1) * P], ident[:, :])
                ins.then_inc(c["job"], 1)
                pe.wait_ge(c["act_ev"], NA * b + 6)
                for q in range(QT):
                    for k in range(KD):
                        ins = pe.matmul(L[1][:, q * D:(q + 1) * D], attT[:, k, q * P:(q + 1) * P], w["wp"][:, k, :],
                                        start=(k == 0), stop=(k == KD - 1))
                ins.then_inc(c["job"], 1)
                pe.wait_ge(z2_ready, b + 1)
                for k in range(KD):
                    for q in range(QT):
                        ins = pe.transpose(L[0][:, k * S + q * P:k * S + (q + 1) * P],
                                           xn[:, q, k * P:(k + 1) * P], ident[:, :])
                ins.then_inc(c["job"], 1)
                pe.wait_ge(c["act_ev"], NA * b + 7)
                pe.wait_ge(c["dve_ev"], ND * b + 4)
                for q in range(QT):
                    for k in range(KD):
                        ins = pe.matmul(L[1][:, q * E0:(q + 1) * E0], zT[:, k, q * P:(q + 1) * P], w["gw"][:, k, :],
                                        start=(k == 0), stop=(k == KD - 1))
                ins.then_inc(c["job"], 1)

        @block.scalar
        def _(act):
            act.wait_ge(m["w_self_in"], 16 * 9)
            act.nop().then_inc(c["act_ev"], 1)
            with act.Fori(0, B) as b:
                act.wait_ge(c["job"], NJ * b + 1)
                for k in range(KD):
                    ins = act.activation(zT[:, k, :], L[0][:, k * S:(k + 1) * S], ACT.Identity,
                                         bias=w["ln1"][:, 1, k:k + 1], scale=w["ln1"][:, 0, k:k + 1])
                ins.then_inc(c["act_ev"], 1)
                act.wait_ge(c["job"], NJ * b + 3)
                act.mul(c["qT"][:, 2:4, :].rearrange("p m s -> p (m s)"), L[0][:, :], DH1 ** -0.5).then_inc(c["act_ev"], 1)
                act.wait_ge(c["job"], NJ * b + 5)
                act.copy(c["kT"][:, 2:4, :].rearrange("p m s -> p (m s)"), L[0][:, :]).then_inc(c["act_ev"], 1)
                act.wait_ge(c["job"], NJ * b + 6)
                act.copy(c["v"].rearrange("p q h w -> p (q h) w")[:, :, 0:DH1],
                         L[1][:, :].rearrange("p (g w) -> p g w", w=DH1)).then_inc(c["act_ev"], 1)
                heads_act(act, c, g, b)
                act.wait_ge(c["job"], NJ * b + 7)
                act.copy(attT.rearrange("p k s -> p (k s)"), L[0][:, :]).then_inc(c["act_ev"], 1)
                act.wait_ge(c["job"], NJ * b + 9)
                act.copy(zT.rearrange("p k s -> p (k s)"), L[0][:, :]).then_inc(c["act_ev"], 1)

        @block.vector
        def _(dve):
            dve.nop().then_inc(c["dve_ev"], 1)
            dve.wait_ge(c["start"], 2)
            with dve.Fori(0, B) as b:
                ch = Chain(dve, c["own"], b * OWN)
                layernorm(dve, ch, lambda q: tile1(x, b, q), lambda q: y0[:, q, :], ln, 3 * b)
                ch.wait()
                layernorm(dve, ch, lambda q: y0[:, q, :], lambda q: xn[:, q, :], ln, 3 * b + 1, c["xn_ready"])
                dve.wait_ge(c["job"], NJ * b + 2)
                dve.tensor_scalar(c["qT"][:, 0:2, :].rearrange("p m s -> p (m s)"), L[1][:, :], DH1 ** -0.5, None,
                                  ALU.mult).then_inc(c["dve_ev"], 1)
                dve.wait_ge(c["job"], NJ * b + 4)
                dve.tensor_copy(c["kT"][:, 0:2, :].rearrange("p m s -> p (m s)"), L[1][:, :]).then_inc(c["dve_ev"], 1)
                heads_dve(dve, ch, c, g, b)
                dve.wait_ge(c["job"], NJ * b + 8)
                ych = dve.tensor_tensor(y0.rearrange("p q d -> p (q d)"), L[1][:, :],
                                        y0.rearrange("p q d -> p (q d)"), ALU.add)
                ych.then_inc(c["dve_ev"], 1)
                dve.wait_ge(c["dve_ev"], ND * b + 4)
                layernorm(dve, ch, lambda q: y0[:, q, :], lambda q: xn[:, q, :], ln, 3 * b + 2, n2_ready)
                ch.done(dve.tensor_tensor(tile2(x, b), tile2(x, b), y0.rearrange("p q d -> p (q d)"), ALU.add))
                dve.wait_ge(c["job"], NJ * b + 10)
                dve.tensor_tensor(lg[:, bass.ds(b * (QT * E0), QT * E0)].rearrange("p (q e) -> p q e", q=QT),
                                  L[1][:, 0:QT * E0].rearrange("p (q e) -> p q e", q=QT),
                                  w["gb"].unsqueeze(1).to_broadcast([P, QT, E0]), ALU.add).then_inc(c["dve_ev"], 1)
                dve.wait_ge(z_kept, b + 1)
                assert ch.k == OWN, ch.k



def route(nc, a, m, which):
    E, top, tiles = (E0, 1, TILES0) if which == 0 else (E1, TOP1, TILES1)
    tag = f"r{which}_"
    cv = Carve(m["r"], m["RW"])
    if which == 0:
        cv.at = 4000
    mask, rank, steps, jx = (cv.take(P, E, E), cv.take(P, E), cv.take(P, NC), cv.take(P, tiles))
    val, mx, eq, any_oh = cv.take(P, NT, E), cv.take(P, NT), cv.take(P, NT, E), cv.take(P, NT, E)
    oh = [cv.take(P, NT, E) for _ in range(top)]
    slotf, cnt, cmp, padded = cv.take(P, NT), cv.take(P, E), cv.take(P, E, NC), cv.take(P, E)
    lt, end, base = cv.take(P, E, E), cv.take(P, E), cv.take(P, E)
    own_cmp, own_f = cv.take(P, tiles, E), cv.take(P, tiles)
    sem = m["sem"]
    own, oh_ready, rank_ready = sem(tag + "own"), sem(tag + "oh_ready"), sem(tag + "rank_ready")
    mask_in, slots_ready, sent = sem(tag + "mask_in"), sem(tag + "slots_ready"), sem(tag + "sent")
    lg = m["logits"][:, 0:NT * E].rearrange("p (t e) -> p t e", t=NT)
    ohb = m["oh_bf"][:, 0:NT * E]
    ranks, counts = m["psum"][0][:, 0:NT * E], m["psum"][1][:, 0:NT * E]
    zs = m[f"zs{which}"]
    src = m["z"]

    def over_e(v):
        return v.unsqueeze(2).to_broadcast([P, NT, E])

    def over_t(v):
        return v.unsqueeze(1).to_broadcast([P, NT, E])

    with nc.Block() as block:
        @block.sync
        def _(sp):
            for dst, name in ((mask, "incl"), (rank, "rank"), (steps, "steps"), (jx, "jx")):
                n = dst.free_size()
                flat = dst if len(dst.shape) == 2 else dst.rearrange("p a b -> p (a b)")
                sp.dma_start(flat, a[name + str(which)].partition_broadcast(P)).then_inc(mask_in, 16)

        @block.tensor
        def _(pe):
            pe.wait_ge(oh_ready, 1)
            pe.matmul(ranks, m["upper"][:, :], ohb, start=True, stop=False)
            v = ranks.rearrange("p (t e) -> p t e", t=NT)
            for t in range(NT - 1):
                pe.matmul(v[:, t + 1:NT, :], m["ones"][:, :],
                          ohb[:, t * E:(t + 1) * E].unsqueeze(1).to_broadcast([P, NT - 1 - t, E]),
                          start=False, stop=(t == NT - 2))
            pe.matmul(counts, m["ones"][:, :], ohb, start=True, stop=True).then_inc(rank_ready, 1)

        @block.vector
        def _(dve):
            ch = Chain(dve, own, 0)

            def step(ins):
                ch.done(ins)
                ch.wait()

            dve.wait_ge(mask_in, 64)
            if which == 1:
                step(dve.tensor_reduce(mx, lg, AX, ALU.max))
                step(dve.tensor_tensor(val, lg, over_e(mx), ALU.subtract))
                dve.nop().then_inc(m["r1_shifted"], 1)
                dve.wait_ge(m["r1_exp"], 1)
                step(dve.tensor_reduce(mx, val, AX, ALU.add))
                step(dve.reciprocal(slotf, mx))
                step(dve.tensor_tensor(val, val, over_e(slotf), ALU.mult))
            else:
                step(dve.tensor_copy(val, lg))
            for k in range(top):
                step(dve.tensor_reduce(mx, val, AX, ALU.max))
                if which == 1:
                    step(dve.tensor_copy(m["top_p"][:, k, :], mx))
                step(dve.tensor_tensor(eq, val, over_e(mx), ALU.is_equal))
                step(dve.tensor_tensor(eq, eq, over_t(rank), ALU.mult))
                step(dve.tensor_reduce(mx, eq, AX, ALU.max))
                step(dve.tensor_tensor(oh[k], over_t(rank), over_e(mx), ALU.is_equal))
                if k + 1 < top:
                    step(dve.scalar_tensor_tensor(val, oh[k], -4.0, val, ALU.mult, ALU.add))
            total = oh[0]
            if which == 1:
                step(dve.tensor_tensor(any_oh, oh[0], oh[1], ALU.add))
                step(dve.tensor_tensor(any_oh, any_oh, oh[2], ALU.add))
                total = any_oh
                step(dve.scalar_tensor_tensor(val, oh[2], -4.0, val, ALU.mult, ALU.add))
                step(dve.scalar_tensor_tensor(val, any_oh, 4.0, val, ALU.mult, ALU.add))
                step(dve.tensor_tensor(m["cw"][:, :, 0:E], oh[0],
                                       over_e(m["top_p"][:, 0, :]), ALU.mult))
                for k in (1, 2):
                    step(dve.tensor_tensor(eq, oh[k], over_e(m["top_p"][:, k, :]), ALU.mult))
                    step(dve.tensor_tensor(m["cw"][:, :, 0:E], m["cw"][:, :, 0:E], eq, ALU.add))
            dve.tensor_copy(ohb, total.rearrange("p t e -> p (t e)")).then_inc(oh_ready, 1)
            dve.wait_ge(rank_ready, 1)
            step(dve.tensor_reduce(cnt, counts.rearrange("p (t e) -> p e t", t=NT), AX, ALU.add))
            step(dve.tensor_tensor(cmp, cnt.unsqueeze(2).to_broadcast([P, E, NC]),
                                   steps.unsqueeze(1).to_broadcast([P, E, NC]), ALU.is_gt))
            step(dve.tensor_reduce(padded, cmp, AX, ALU.add))
            step(dve.tensor_tensor(lt, mask, padded.unsqueeze(1).to_broadcast([P, E, E]), ALU.mult))
            step(dve.tensor_reduce(end, lt, AX, ALU.add))
            step(dve.tensor_tensor(base, end, padded, ALU.subtract))
            step(dve.scalar_tensor_tensor(eq, over_t(base), float(P), ranks.rearrange("p (t e) -> p t e", t=NT),
                                          ALU.mult, ALU.add))
            for k in range(top):
                step(dve.tensor_tensor(val, eq, oh[k], ALU.mult))
                step(dve.tensor_reduce(slotf, val, AX, ALU.add))
                step(dve.tensor_copy(m["slots"][:, k, :], slotf))
                dve.nop().then_inc(slots_ready, 1)
            step(dve.tensor_tensor(own_cmp, jx.unsqueeze(2).to_broadcast([P, tiles, E]),
                                   end.unsqueeze(1).to_broadcast([P, tiles, E]), ALU.is_ge))
            step(dve.tensor_reduce(own_f, own_cmp, AX, ALU.add))
            step(dve.tensor_scalar(own_f, own_f, float(E - 1), None, ALU.min))
            step(dve.tensor_copy(m["owner"][:, 0:tiles], own_f))

        if which == 1:
            @block.scalar
            def _(act):
                act.wait_ge(m["r1_shifted"], 1)
                act.activation(val, val, ACT.Exp).then_inc(m["r1_exp"], 1)

        @block.gpsimd
        def _(pool):
            pool.wait_ge(m["zero_fill"], 16 * 6)
            for k in range(top):
                pool.wait_ge(slots_ready, k + 1)
                for t in range(NT):
                    pool.indirect_dma_start(zs, bass.IndirectOffsetOnAxis(m["slots"][:, k, t:t + 1], 0),
                                            src[:, t * D:(t + 1) * D], None).then_inc(sent, 16)
            pool.wait_ge(sent, 16 * NT * top)



def moe(nc, a, m, which):
    E, HID, tiles = (E0, HID0, TILES0) if which == 0 else (E1, HID1, TILES1)
    MK = HID // P
    HB = (HID + 511) // 512
    HW = min(HID, 512)
    tag = f"m{which}_"
    cv = Carve(m["r"], m["RW"])
    zt = cv.take(P, 2, D)
    zT = cv.take(P, 2, KD, P)
    hid = cv.take(P, 2, HID)
    hT = cv.take(P, 2, MK, P)
    y = cv.take(P, 2, D)
    if which == 0:
        w1, w2 = m["w1"][:, 0:E * KD * HID], m["w2"][:, 0:E * MK * D]
    else:
        w1, w2 = m["w1"][:, 0:E * KD * HID], m["w1"][:, E * KD * HID:E * KD * HID + E * MK * D]
        b1T = cv.take(P, E, MK)
    sem = m["sem"]
    z_in = [sem(tag + f"z_in{i}") for i in range(2)]
    y_out = [sem(tag + f"y_out{i}") for i in range(2)]
    t_full, zT_ready, h_full, hid_ready, g_full, hT_ready, y_full, y_ready, b_in = (
        sem(tag + s) for s in ("t_full", "zT_ready", "h_full", "hid_ready", "g_full", "hT_ready", "y_full", "y_ready", "b_in"))
    ps = m["psum"]
    t_ps, h_ps, g_ps, y_ps = ps[0], ps[1:3], ps[3:5], ps[5:7]
    zs, ys = m[f"zs{which}"], m[f"ys{which}"]


    def T(pe, j, p, behind):
        pe.wait_ge(z_in[p], 16 * ((j - p) // 2) + 16 if isinstance(j, int) else j * 8 + (16 - 8 * p))
        if behind:
            pe.wait_ge(zT_ready, j)
        for k in range(KD):
            ins = pe.transpose(t_ps[:, k * P:(k + 1) * P], zt[:, p, k * P:(k + 1) * P], m["ident"][:, :])
        ins.then_inc(t_full, 1)

    def H(pe, j, p, behind):
        e = pe.value_load(m["owner"][0:1, bass.ds(j, 1)], min_val=0, max_val=E - 1)
        pe.wait_ge(zT_ready, j + 1)
        if behind:
            pe.wait_ge(hid_ready, j)
        for n in range(HB):
            for k in range(KD):
                ins = pe.matmul(h_ps[n][:, 0:HW], zT[:, p, k, :], w1[:, bass.ds(e * (KD * HID) + (k * HID + n * HW), HW)],
                                start=(k == 0), stop=(k == KD - 1))
        ins.then_inc(h_full, 1)

    def G(pe, j, p, behind):
        pe.wait_ge(hid_ready, j + 1)
        if behind:
            pe.wait_ge(hT_ready, j)
        for i in range(MK):
            ins = pe.transpose(g_ps[i // 4][:, i % 4 * P:(i % 4 + 1) * P], hid[:, p, i * P:(i + 1) * P], m["ident"][:, :])
        ins.then_inc(g_full, 1)

    def Y(pe, j, p, behind):
        e = pe.value_load(m["owner"][0:1, bass.ds(j, 1)], min_val=0, max_val=E - 1)
        pe.wait_ge(hT_ready, j + 1)
        if behind:
            pe.wait_ge(y_ready, j - 1)
        for i in range(MK):
            ins = pe.matmul(y_ps[p][:, 0:D], hT[:, p, i, :], w2[:, bass.ds(e * (MK * D) + i * D, D)],
                            start=(i == 0), stop=(i == MK - 1))
        ins.then_inc(y_full, 1)

    def act_T(act, j, p):
        act.wait_ge(t_full, j + 1)
        act.copy(zT[:, p, :, :].rearrange("p k s -> p (k s)"), t_ps[:, 0:KD * P]).then_inc(zT_ready, 1)

    def act_H(act, j, p):
        act.wait_ge(h_full, j + 1)
        for n in range(HB):
            ins = act.activation(hid[:, p, n * HW:(n + 1) * HW], h_ps[n][:, 0:HW],
                                 ACT.Gelu_apprx_tanh if which == 0 else ACT.Copy)
        ins.then_inc(hid_ready, 1)

    def dve_G(dve, j, p):
        dve.wait_ge(g_full, j + 1)
        if which == 0:
            for n in range(2):
                ins = dve.tensor_copy(hT[:, p, 4 * n:4 * n + 4, :].rearrange("p k s -> p (k s)"), g_ps[n][:, :])
        else:
            e = dve.value_load(m["owner"][0:1, bass.ds(j, 1)], min_val=0, max_val=E - 1)
            for i in range(MK):
                ins = dve.tensor_scalar(hT[:, p, i, :], g_ps[0][:, i * P:(i + 1) * P],
                                        b1T.rearrange("p e k -> p (e k)")[:, bass.ds(e * MK + i, 1)], 0.0,
                                        ALU.add, ALU.max)
        ins.then_inc(hT_ready, 1)

    def dve_Y(dve, j, p, behind):
        dve.wait_ge(y_full, j + 1)
        if behind:
            dve.wait_ge(y_out[p], 8 * j - 8 * p)
        dve.tensor_copy(y[:, p, :], y_ps[p][:, 0:D]).then_inc(y_ready, 1)

    def load(sp, j, p):
        sp.dma_start(zt[:, p, :], zs[bass.ds(j * P, P), :]).then_inc(z_in[p], 16)

    def store(sp, j, p):
        sp.wait_ge(y_ready, j + 1)
        sp.dma_start(ys[bass.ds(j * P, P), :], y[:, p, :]).then_inc(y_out[p], 16)

    TURNS = (tiles - 3) // 2
    LEFT = tiles - 2 * TURNS

    with nc.Block() as block:
        @block.sync
        def _(sp):
            if which == 1:
                sp.dma_start(b1T.rearrange("p e k -> p (e k)"), a["eb1T"]).then_inc(b_in, 16)
            load(sp, 0, 0)
            load(sp, 1, 1)
            for j in (2, 3, 4):
                if j < tiles:
                    sp.wait_ge(t_full, j - 1)
                    load(sp, j, j % 2)
            with sp.Fori(0, TURNS - 1) as i:
                for p in range(2):
                    j = i * 2 + p
                    sp.wait_ge(t_full, j + 4)
                    load(sp, j + 5, 1 - p)
                    store(sp, j, p)
            for j in range(2 * TURNS - 2, tiles):
                if j + 5 < tiles:
                    sp.wait_ge(t_full, j + 4)
                    load(sp, j + 5, (j + 5) % 2)
                store(sp, j, j % 2)
            for p in range(2):
                sp.wait_ge(y_out[p], 16 * ((tiles + 1 - p) // 2))

        @block.tensor
        def _(pe):
            if which == 0:
                pe.wait_ge(m["w1_in"], 16 * E0)
                pe.wait_ge(m["w2_in"], 16 * E0)
            else:
                pe.wait_ge(m["we_in"], 32)
            T(pe, 0, 0, False)
            T(pe, 1, 1, True)
            H(pe, 0, 0, False)
            T(pe, 2, 0, True)
            H(pe, 1, 1, True)
            G(pe, 0, 0, False)
            for j in range(2):
                T(pe, j + 3, (j + 1) % 2, True)
                H(pe, j + 2, j, True)
                G(pe, j + 1, 1 - j, True)
                Y(pe, j, j, False)
            with pe.Fori(1, TURNS) as i:
                for p in range(2):
                    j = i * 2 + p
                    T(pe, j + 3, 1 - p, True)
                    H(pe, j + 2, p, True)
                    G(pe, j + 1, 1 - p, True)
                    Y(pe, j, p, True)
            for j in range(2 * TURNS, tiles):
                if j + 3 < tiles:
                    T(pe, j + 3, (j + 3) % 2, True)
                if j + 2 < tiles:
                    H(pe, j + 2, j % 2, True)
                if j + 1 < tiles:
                    G(pe, j + 1, (j + 1) % 2, True)
                Y(pe, j, j % 2, True)

        @block.scalar
        def _(act):
            act_T(act, 0, 0)
            act_T(act, 1, 1)
            act_H(act, 0, 0)
            act_T(act, 2, 0)
            act_H(act, 1, 1)
            with act.Fori(0, TURNS) as i:
                for p in range(2):
                    j = i * 2 + p
                    act_T(act, j + 3, 1 - p)
                    act_H(act, j + 2, p)
            for j in range(2 * TURNS, tiles):
                if j + 3 < tiles:
                    act_T(act, j + 3, (j + 3) % 2)
                if j + 2 < tiles:
                    act_H(act, j + 2, j % 2)

        @block.vector
        def _(dve):
            if which == 1:
                dve.wait_ge(b_in, 16)
            dve_G(dve, 0, 0)
            for j in range(2):
                dve_G(dve, j + 1, 1 - j)
                dve_Y(dve, j, j, False)
            with dve.Fori(1, TURNS) as i:
                for p in range(2):
                    j = i * 2 + p
                    dve_G(dve, j + 1, 1 - p)
                    dve_Y(dve, j, p, True)
            for j in range(2 * TURNS, tiles):
                if j + 1 < tiles:
                    dve_G(dve, j + 1, (j + 1) % 2)
                dve_Y(dve, j, j % 2, True)


def join0(nc, a, m):
    cv = Carve(m["w1"], m["W1WORDS"])
    got = cv.take(P, NT, D)
    sem = m["sem"]
    row_in, joined = sem("j0_row_in"), sem("j0_joined")
    with nc.Block() as block:
        @block.gpsimd
        def _(pool):
            for t in range(NT):
                pool.indirect_dma_start(got[:, t, :], None, m["ys0"],
                                        bass.IndirectOffsetOnAxis(m["slots"][:, 0, t:t + 1], 0)).then_inc(row_in, 16)

        @block.vector
        def _(dve):
            dve.wait_ge(row_in, 16 * NT)
            dve.tensor_tensor(m["x"][:, :], m["x"][:, :], got.rearrange("p t d -> p (t d)"), ALU.add).then_inc(joined, 1)



def cross1(nc, a, m):
    cv = Carve(m["w2"], m["W1WORDS"])
    wq, wk, wv = cv.take(P, KD, D), cv.take(CP, KC, D), cv.take(CP, KC, D)
    sw1, sw2, rw = cv.take(P, KD, D), cv.take(P, KD, D), cv.take(P, KD, E1)
    bqk, bv, rb, sb1 = cv.take(P, 2, KD), cv.take(P, D), cv.take(P, E1), cv.take(P, KD)
    ctxT, xn, xnT = cv.take(CP, KC, S), cv.take(P, QT, D), cv.take(P, KD, S)
    qT, kT, v = cv.take(P, KD, S), cv.take(P, KD, S), cv.take(P, QT, D + 1)
    p, pT, x3T, shT = cv.take(P, QT, S), cv.take(P, QT, S), cv.take(P, KD, S), cv.take(P, KD, S)
    nmax, rec = cv.take(P, QT), cv.take(P, QT)
    x3 = cv.take(P, QT, D)
    ln = ln_buffers(m, cv, "c1_")
    sem = m["sem"]
    (job, act_ev, dve_ev, own, xn_ready, w_in, ctx_in, start, x_ready) = (sem("c1_" + s) for s in (
        "job", "act_ev", "dve_ev", "own", "xn_ready", "w_in", "ctx_in", "start", "x_ready"))
    m["r1_shifted"], m["r1_exp"] = sem("r1_shifted"), sem("r1_exp")
    ps, ident, x, z = m["psum"], m["ident"], m["x"], m["z"]
    lg = m["logits"][:, 0:NT * E1]
    NJ, NA, ND = 11, 7, 3
    OWN = 2 * LN_STEPS + 1 + QT
    n3_ready, z_kept = sem("c1_n3_ready"), sem("c1_z_kept")

    with nc.Block() as block:
        @block.sync
        def _(sp):
            for dst, name in ((wk, "wk1"), (wv, "wv1"), (wq, "wq1"), (bqk, "bqk1"), (sw1, "sw1"), (sw2, "sw2"), (rw, "rw"), (sb1, "sb1")):
                sp.dma_start(dst, a[name]).then_inc(w_in, 16)
            sp.dma_start(bv, a["bv1"].partition_broadcast(P)).then_inc(w_in, 16)
            sp.dma_start(rb, a["rb"].partition_broadcast(P)).then_inc(w_in, 16)
            sp.dma_start(ctxT, a["ctxT"][0]).then_inc(ctx_in, 16)
            n = E1 * KD * HID1
            sp.dma_start(m["w1"][:, 0:n], a["ew1"]).then_inc(m["we_in"], 16)
            sp.dma_start(m["w1"][:, n:2 * n], a["ew2"]).then_inc(m["we_in"], 16)
            with sp.Fori(0, B - 1) as b:
                sp.wait_ge(job, NJ * b + 2)
                sp.dma_start(ctxT, a["ctxT"][bass.ds(b + 1, 1)].rearrange("o p k s -> (o p) k s")).then_inc(ctx_in, 16)

        @block.gpsimd
        def _(pool):
            pool.memset(v[:, :, D:D + 1], 1.0).then_inc(start, 1)
            with pool.Fori(0, B) as b:
                ln_power(pool, ln, 2 * b)
                ln_power(pool, ln, 2 * b + 1)
                pool.wait_ge(n3_ready, b + 1)
                pool.tensor_copy(tile2(z, b), xn.rearrange("p q d -> p (q d)")).then_inc(z_kept, 1)

        @block.tensor
        def _(pe):
            pe.wait_ge(w_in, 160)
            pe.wait_ge(start, 1)
            with pe.Fori(0, B) as b:
                pe.wait_ge(ctx_in, 16 * b + 16)
                for i in range(KD):
                    for k in range(KC):
                        ins = pe.matmul(ps[0][:, i * S:(i + 1) * S], wk[:, k, i * P:(i + 1) * P], ctxT[:, k, :],
                                        start=(k == 0), stop=(k == KC - 1))
                ins.then_inc(job, 1)
                pe.wait_ge(dve_ev, ND * b + 1)
                for q in range(QT):
                    for k in range(KC):
                        ins = pe.matmul(ps[1][:, q * D:(q + 1) * D], ctxT[:, k, q * P:(q + 1) * P], wv[:, k, :],
                                        start=(k == 0), stop=(k == KC - 1))
                ins.then_inc(job, 1)
                pe.wait_ge(xn_ready, b + 1)
                for k in range(KD):
                    for q in range(QT):
                        ins = pe.transpose(ps[2][:, k * S + q * P:k * S + (q + 1) * P], xn[:, q, k * P:(k + 1) * P],
                                           ident[:, :])
                ins.then_inc(job, 1)
                pe.wait_ge(act_ev, NA * b + 2)
                for i in range(KD):
                    for k in range(KD):
                        ins = pe.matmul(ps[3][:, i * S:(i + 1) * S], wq[:, k, i * P:(i + 1) * P], xnT[:, k, :],
                                        start=(k == 0), stop=(k == KD - 1))
                ins.then_inc(job, 1)
                pe.wait_ge(act_ev, NA * b + 3)
                for q in range(QT):
                    for k in range(KD):
                        ins = pe.matmul(ps[4][:, q * S:(q + 1) * S], qT[:, k, q * P:(q + 1) * P], kT[:, k, :],
                                        start=(k == 0), stop=(k == KD - 1))
                ins.then_inc(job, 1)
                pe.wait_ge(act_ev, NA * b + 4)
                for kt in range(QT):
                    for q in range(QT):
                        ins = pe.transpose(ps[5][:, kt * S + q * P:kt * S + (q + 1) * P], p[:, q, kt * P:(kt + 1) * P],
                                           ident[:, :])
                ins.then_inc(job, 1)
                pe.wait_ge(act_ev, NA * b + 5)
                pe.wait_ge(dve_ev, ND * b + 2)
                for q in range(QT):
                    for kt in range(QT):
                        ins = pe.matmul(ps[6 + q][:, 0:D + 1], pT[:, kt, q * P:(q + 1) * P], v[:, kt, :],
                                        start=(kt == 0), stop=(kt == QT - 1))
                ins.then_inc(job, 1)
                pe.wait_ge(n3_ready, b + 1)
                for k in range(KD):
                    for q in range(QT):
                        ins = pe.transpose(ps[0][:, k * S + q * P:k * S + (q + 1) * P], xn[:, q, k * P:(k + 1) * P],
                                           ident[:, :])
                ins.then_inc(job, 1)
                pe.wait_ge(act_ev, NA * b + 6)
                for q in range(QT):
                    for k in range(KD):
                        ins = pe.matmul(ps[1][:, q * E1:(q + 1) * E1], x3T[:, k, q * P:(q + 1) * P], rw[:, k, :],
                                        start=(k == 0), stop=(k == KD - 1))
                ins.then_inc(job, 1)
                for i in range(KD):
                    for k in range(KD):
                        ins = pe.matmul(ps[2][:, i * S:(i + 1) * S], sw1[:, k, i * P:(i + 1) * P], x3T[:, k, :],
                                        start=(k == 0), stop=(k == KD - 1))
                ins.then_inc(job, 1)
                pe.wait_ge(act_ev, NA * b + 7)
                for q in range(QT):
                    for k in range(KD):
                        ins = pe.matmul(ps[3][:, q * D:(q + 1) * D], shT[:, k, q * P:(q + 1) * P], sw2[:, k, :],
                                        start=(k == 0), stop=(k == KD - 1))
                ins.then_inc(job, 1)

        @block.scalar
        def _(act):
            act.wait_ge(w_in, 160)
            with act.Fori(0, B) as b:
                act.wait_ge(job, NJ * b + 1)
                for i in range(KD):
                    ins = act.activation(kT[:, i, :], ps[0][:, i * S:(i + 1) * S], ACT.Identity, bias=bqk[:, 1, i:i + 1])
                ins.then_inc(act_ev, 1)
                act.wait_ge(job, NJ * b + 3)
                act.copy(xnT.rearrange("p k s -> p (k s)"), ps[2][:, :]).then_inc(act_ev, 1)
                act.wait_ge(job, NJ * b + 4)
                for i in range(KD):
                    ins = act.activation(qT[:, i, :], ps[3][:, i * S:(i + 1) * S], ACT.Identity, bias=bqk[:, 0, i:i + 1])
                ins.then_inc(act_ev, 1)
                act.wait_ge(start, b + 2)
                for q in range(QT):
                    ins = act.activation(p[:, q, :], ps[4][:, q * S:(q + 1) * S], ACT.Exp, bias=nmax[:, q:q + 1],
                                         scale=D ** -0.5)
                ins.then_inc(act_ev, 1)
                act.wait_ge(job, NJ * b + 6)
                act.copy(pT.rearrange("p k s -> p (k s)"), ps[5][:, :]).then_inc(act_ev, 1)
                act.wait_ge(job, NJ * b + 8)
                act.copy(x3T.rearrange("p k s -> p (k s)"), ps[0][:, :]).then_inc(act_ev, 1)
                act.wait_ge(job, NJ * b + 10)
                for i in range(KD):
                    ins = act.activation(shT[:, i, :], ps[2][:, i * S:(i + 1) * S], ACT.Relu, bias=sb1[:, i:i + 1])
                ins.then_inc(act_ev, 1)

        @block.vector
        def _(dve):
            dve.wait_ge(w_in, 160)
            dve.nop().then_inc(dve_ev, 1)
            with dve.Fori(0, B) as b:
                ch = Chain(dve, own, OWN * b)
                layernorm(dve, ch, lambda q: tile1(x, b, q), lambda q: xn[:, q, :], ln, 2 * b, xn_ready)
                dve.wait_ge(job, NJ * b + 2)
                dve.tensor_tensor(v[:, :, 0:D], ps[1][:, :].rearrange("p (q d) -> p q d", q=QT),
                                  bv.unsqueeze(1).to_broadcast([P, QT, D]), ALU.add).then_inc(dve_ev, 1)
                dve.wait_ge(job, NJ * b + 5)
                ch.done(dve.tensor_reduce(rec, ps[4][:, :].rearrange("p (q k) -> p q k", q=QT), AX, ALU.max))
                ch.wait()
                dve.tensor_scalar(nmax, rec, -(D ** -0.5), None, ALU.mult).then_inc(start, 1)
                dve.wait_ge(job, NJ * b + 7)
                for q in range(QT):
                    ch.done(dve.reciprocal(rec[:, q:q + 1], ps[6 + q][:, D:D + 1]))
                ch.wait()
                for q in range(QT):
                    ins = dve.scalar_tensor_tensor(x3[:, q, :], ps[6 + q][:, 0:D], rec[:, q:q + 1], tile1(x, b, q),
                                                   ALU.mult, ALU.add)
                ins.then_inc(x_ready, 1)
                dve.wait_ge(x_ready, b + 1)
                layernorm(dve, ch, lambda q: x3[:, q, :], lambda q: xn[:, q, :], ln, 2 * b + 1, n3_ready)
                dve.wait_ge(job, NJ * b + 9)
                dve.tensor_tensor(lg[:, bass.ds(b * (QT * E1), QT * E1)].rearrange("p (q e) -> p q e", q=QT),
                                  ps[1][:, 0:QT * E1].rearrange("p (q e) -> p q e", q=QT),
                                  rb.unsqueeze(1).to_broadcast([P, QT, E1]), ALU.add).then_inc(dve_ev, 1)
                dve.wait_ge(job, NJ * b + 11)
                dve.tensor_tensor(tile2(x, b), ps[3][:, :], x3.rearrange("p q d -> p (q d)"), ALU.add).then_inc(dve_ev, 1)
                dve.wait_ge(z_kept, b + 1)
                assert ch.k == OWN, ch.k


def join1(nc, a, m, out):
    cv = Carve(m["w2"], m["W1WORDS"])
    got = cv.take(P, TOP1, NT, D)
    b2 = cv.take(E1 + 1, D)
    cwT = cv.take(E1 + 1, NT, P)
    sem = m["sem"]
    row_in, b_in, cw_full, cwT_ready, bias_full, joined, stored = (
        sem("j1_" + s) for s in ("row_in", "b_in", "cw_full", "cwT_ready", "bias_full", "joined", "stored"))
    ps, x = m["psum"], m["x"]
    with nc.Block() as block:
        @block.sync
        def _(sp):
            sp.dma_start(b2, a["b2"]).then_inc(b_in, 16)
            for b in range(B):
                sp.wait_ge(joined, (QT * TOP1) * (b + 1))
                sp.dma_start(out[:, b * QT * D:(b + 1) * QT * D], tile2(x, b)).then_inc(stored, 16)
            sp.wait_ge(stored, 16 * B)

        @block.gpsimd
        def _(pool):
            for t in range(NT):
                for k in range(TOP1):
                    pool.indirect_dma_start(got[:, k, t, :], None, m["ys1"],
                                            bass.IndirectOffsetOnAxis(m["slots"][:, k, t:t + 1], 0)).then_inc(row_in, 16)

        @block.tensor
        def _(pe):
            for j in range(4):
                for t in range(4):
                    ins = pe.transpose(ps[j][0:E1 + 1, t * P:(t + 1) * P], m["cw"][:, 4 * j + t, :], m["ident"][:, :])
                ins.then_inc(cw_full, 1)
            pe.wait_ge(b_in, 16)
            pe.wait_ge(cwT_ready, 4)
            for b in range(B):
                if b >= 4:
                    pe.wait_ge(joined, QT * TOP1 * (b - 3))
                for q in range(QT):
                    ins = pe.matmul(ps[4 + b % 4][:, q * D:(q + 1) * D], cwT[:, QT * b + q, :], b2, start=True, stop=True)
                ins.then_inc(bias_full, 1)

        @block.scalar
        def _(act):
            for j in range(4):
                act.wait_ge(cw_full, j + 1)
                act.copy(cwT[:, 4 * j:4 * j + 4, :].rearrange("p t s -> p (t s)"), ps[j][0:E1 + 1, :]).then_inc(cwT_ready, 1)

        @block.vector
        def _(dve):
            own = sem("j1_own")
            for b in range(B):
                dve.wait_ge(bias_full, b + 1)
                dve.tensor_tensor(tile2(x, b), tile2(x, b), ps[4 + b % 4][:, :], ALU.add).then_inc(own, 1)
                dve.wait_ge(own, b + 1)
                dve.wait_ge(row_in, 16 * NT * TOP1)
                for k in range(TOP1):
                    for q in range(QT):
                        t = QT * b + q
                        if k:
                            dve.wait_ge(joined, QT * TOP1 * b + QT * k - (QT - 1 - q))
                        dve.scalar_tensor_tensor(x[:, t * D:(t + 1) * D], got[:, k, t, :], m["top_p"][:, k, t:t + 1],
                                                 x[:, t * D:(t + 1) * D], ALU.mult, ALU.add).then_inc(joined, 1)



def kernel(**inputs):
    import numpy as np
    import concourse.bacc as bacc
    from concourse import mybir as mb
    from concourse.bass_utils import run_bass_kernel_spmd as run
    import ml_dtypes

    x = {k: np.asarray(v) for k, v in inputs.items()}

    def part(w, p=P):
        return np.ascontiguousarray(w.reshape(w.shape[0] // p, p, -1).transpose(1, 0, 2))

    def cols(v):
        return np.ascontiguousarray(v.reshape(-1, P).T)

    def padded_heads(w):
        w = w.reshape(D, H1, DH1)
        return part(np.concatenate([w, np.zeros((D, H1, PAD1 - DH1), w.dtype)], axis=2).reshape(D, H1 * PAD1))

    qkv = x["L0_ffn_w_qkv"]
    arrays = {
        "x": part(x["x"].reshape(B * S, D)).reshape(P, NT * D),
        "ctxT": np.ascontiguousarray(x["ctx_768"].reshape(B, S, KC, CP).transpose(0, 3, 2, 1)),
        "wq0": part(x["L0_xattn_Wq"]), "wk0": part(x["L0_xattn_Wk"], CP), "wv0": part(x["L0_xattn_Wv"], CP),
        "wo0": part(x["L0_xattn_Wo"]), "bo0": x["L0_xattn_bo"],
        "s_wq": padded_heads(qkv[:, 0:D]), "s_wk": padded_heads(qkv[:, D:2 * D]), "s_wv": part(qkv[:, 2 * D:]),
        "s_wp": part(x["L0_ffn_w_proj"]),
        "s_ln1": np.ascontiguousarray(np.stack([cols(x["L0_ffn_ln1_w"]), cols(x["L0_ffn_ln1_b"])], axis=1)),
        "s_ln2w": x["L0_ffn_ln2_w"], "s_ln2b": x["L0_ffn_ln2_b"],
        "s_gw": part(x["L0_ffn_gate_w"]), "s_gb": x["L0_ffn_gate_b"],
        "w1": np.stack([part(w).reshape(P, -1) for w in x["L0_ffn_w1"]]),
        "w2": np.stack([part(w).reshape(P, -1) for w in x["L0_ffn_w2"]]),
        "wq1": part(x["L1_xattn_Wq"]), "wk1": part(x["L1_xattn_Wk"], CP), "wv1": part(x["L1_xattn_Wv"], CP),
        "bqk1": np.ascontiguousarray(np.stack([cols(x["L1_xattn_bq"]), cols(x["L1_xattn_bk"])], axis=1)),
        "bv1": x["L1_xattn_bv"], "rw": part(x["L1_ffn_router_W"]), "rb": x["L1_ffn_router_b"],
        "sw1": part(x["L1_ffn_sW1"]), "sw2": part(x["L1_ffn_sW2"]), "sb1": cols(x["L1_ffn_sb1"]),
        "ew1": np.ascontiguousarray(np.stack([part(w).reshape(P, -1) for w in x["L1_ffn_eW1"]], axis=1)).reshape(P, -1),
        "ew2": np.ascontiguousarray(np.stack([part(w).reshape(P, -1) for w in x["L1_ffn_eW2"]], axis=1)).reshape(P, -1),
        "eb1T": np.ascontiguousarray(x["L1_ffn_eb1"].reshape(E1 * M1, P).T),
        "b2": np.ascontiguousarray(np.concatenate([x["L1_ffn_eb2"], x["L1_ffn_sb2"][None]], axis=0)),
        "ident": np.eye(P, dtype=np.float32),
        "upper": np.triu(np.ones((P, P)), 1).astype(ml_dtypes.bfloat16),
        "ones": np.ones((P, P)).astype(ml_dtypes.bfloat16),
    }
    for i, (e, tiles) in enumerate(((E0, TILES0), (E1, TILES1))):
        arrays[f"incl{i}"] = np.tril(np.ones((e, e), np.float32)).reshape(-1)
        arrays[f"rank{i}"] = (e - np.arange(e)).astype(np.float32)
        arrays[f"steps{i}"] = (P * np.arange(NC)).astype(np.float32)
        arrays[f"jx{i}"] = np.arange(tiles).astype(np.float32)

    nc = bacc.Bacc("TRN2", target_bir_lowering=False, num_devices=1)
    args = {k: nc.dram_tensor("in_" + k, v.shape, mb.dt.from_np(v.dtype), kind="ExternalInput").ap()
            for k, v in arrays.items()}
    out = nc.dram_tensor("out", (P, NT * D), mb.dt.float32, kind="ExternalOutput").ap()
    build(nc, args, out)
    r = run(nc, [{"in_" + k: v for k, v in arrays.items()}], core_ids=[0])
    got = np.asarray(r.results[0]["out"])
    return np.ascontiguousarray(got.reshape(P, NT, D).transpose(1, 0, 2)).reshape(B, S, D)
```

```python
from contextlib import ExitStack

import concourse.bass as bass
from concourse import mybir

F32 = mybir.dt.float32
BF16 = mybir.dt.bfloat16
F16 = mybir.dt.float16
I32 = mybir.dt.int32
ALU = mybir.AluOpType
ACT = mybir.ActivationFunctionType
AX = mybir.AxisListType.X

P = 128
B, S, D = 8, 256, 256
NT = B * S // P
QT = S // P
KD = D // P
CP, KC = 96, 2
H0, DH0 = 8, 64
H1, DH1 = 16, 16
EPS = 1e-5
E0, HID0 = 8, 1024
M0 = HID0 // P
E1, HID1, TOP1 = 15, 256, 3
M1 = HID1 // P
TILES0 = (NT * P + E0 * (P - 1)) // P
TILES1 = (TOP1 * NT * P + E1 * (P - 1)) // P
U = 4
NC = 16


class Chain:

    def __init__(self, eng, sem, base):
        self.eng, self.sem, self.base, self.k = eng, sem, base, 0

    def done(self, ins):
        self.k += 1
        ins.then_inc(self.sem, 1)

    def wait(self):
        self.eng.wait_ge(self.sem, self.base + self.k)


def ge(eng, sem, value):
    if not isinstance(value, int) or value > 0:
        eng.wait_ge(sem, value)


class Carve:

    def __init__(self, region, words):
        self.region, self.words, self.at = region, words, 0

    def take(self, parts, *shape, dt=F32):
        n = 1
        for s in shape:
            n *= s
        w = n if dt in (F32, I32) else (n + 1) // 2
        v = self.region[0:parts, self.at:self.at + w]
        self.at += (w + 7) // 8 * 8
        assert self.at <= self.words, (self.at, self.words)
        if dt != F32:
            v = v.bitcast(dt)
        names = "abcd"[:len(shape)]
        if len(shape) > 1:
            v = v.rearrange("p (" + " ".join(names) + ") -> p " + " ".join(names), **dict(zip(names, shape)))
        return v


def tile2(t, b):
    return t[:, bass.ds(b * (QT * D), QT * D)]


def tile1(t, b, q):
    return t[:, bass.ds(b * (QT * D) + q * D, D)]


def layernorm(dve, ch, src, dst, ln, nth, done=None):
    stats, mv, var, rstd = ln["stats"], ln["mv"], ln["var"], ln["rstd"]
    for q in range(QT):
        ch.done(dve.bn_stats(stats[:, q, :], src(q)))
    ch.wait()
    dve.memset(ln["spare"], 0.0)
    for q in range(QT):
        ch.done(dve.bn_aggr(mv[:, q, :], stats[:, q, :]))
    ch.wait()
    dve.tensor_scalar(var, mv[:, :, 1], EPS, None, ALU.add).then_inc(ln["var_ready"], 1)
    dve.wait_ge(ln["rstd_ready"], nth + 1)
    for q in range(QT):
        ins = dve.tensor_scalar(dst(q), src(q), mv[:, q, 0:1], rstd[:, q:q + 1], ALU.subtract, ALU.mult)
        if done is None:
            ch.done(ins)
    if done is not None:
        ins.then_inc(done, 1)


LN_STEPS = 4



def ln_stats(dve, ln, src, nth):
    for q in range(QT):
        dve.bn_stats(ln["stats"][:, q, :], src(q)).then_inc(ln["own"], 1)


def ln_variance(dve, ln, nth):
    dve.wait_ge(ln["own"], nth * 4 + 2)
    dve.memset(ln["spare"], 0.0)
    for q in range(QT):
        dve.bn_aggr(ln["mv"][:, q, :], ln["stats"][:, q, :]).then_inc(ln["own"], 1)
    dve.wait_ge(ln["own"], nth * 4 + 4)
    dve.tensor_scalar(ln["var"], ln["mv"][:, :, 1], EPS, None, ALU.add).then_inc(ln["var_ready"], 1)


def ln_apply(dve, ln, src, dst, nth):
    dve.wait_ge(ln["rstd_ready"], nth + 1)
    for q in range(QT):
        ins = dve.tensor_scalar(dst(q), src(q), ln["mv"][:, q, 0:1], ln["rstd"][:, q:q + 1], ALU.subtract, ALU.mult)
    return ins


def ln_buffers(m, cv, tag):
    return dict(stats=cv.take(P, QT, 6), mv=cv.take(P, QT, 2), var=cv.take(P, QT), rstd=cv.take(P, QT),
                var_ready=m["sem"](tag + "var_ready"), rstd_ready=m["sem"](tag + "rstd_ready"), power=m["power"][:, :], spare=cv.take(P, 1), own=m["sem"](tag + "ln_own"))


def ln_power(pool, ln, nth):
    pool.wait_ge(ln["var_ready"], nth + 1)
    pool.tensor_tensor(ln["rstd"], ln["var"], ln["power"], ALU.pow).then_inc(ln["rstd_ready"], 1)


def build(nc, a, out):
    ctx = ExitStack()
    with ctx:
        def sb(name, shape, dt=F32):
            return ctx.enter_context(nc.sbuf_tensor(name, shape, dt))

        def sem(name):
            return ctx.enter_context(nc.semaphore(name))

        def scratch(name, shape):
            return nc.dram_tensor(name, shape, F32, kind="Internal").ap()

        m = {}
        m["x"] = sb("x_all", [P, NT * D])
        m["z"] = sb("z_all", [P, NT * D])
        W1WORDS = E0 * KD * HID0
        m["w1"] = sb("w1_all", [P, W1WORDS])
        m["w2"] = sb("w2_all", [P, W1WORDS])
        RW = 11000
        m["r"] = sb("r_all", [P, RW])
        m["RW"], m["W1WORDS"] = RW, W1WORDS
        m["ident"] = sb("ident", [P, P])
        m["power"] = sb("power", [P, QT])
        m["upper"] = sb("upper", [P, P], BF16)
        m["ones"] = sb("ones", [P, P], BF16)
        m["oh_bf"] = sb("oh_bf", [P, NT * E1], BF16)
        m["logits"] = sb("logits", [P, NT * 16])
        m["slots"] = sb("slots", [P, TOP1, NT], I32)
        m["owner"] = sb("owner", [P, 64], I32)
        m["top_p"] = sb("top_p", [P, TOP1, NT])
        m["cw"] = sb("cw", [P, NT, E1 + 1])
        m["psum"] = [ctx.enter_context(nc.psum_tensor(f"bank{i}", [P, 512], F32)) for i in range(8)]
        m["q_parts"] = nc.dram_tensor("q_parts", [2, 3, DH1, H1 // 2, 2 * S], BF16, kind="Internal").ap()
        m["k_parts"] = nc.dram_tensor("k_parts", [2, 6, DH1, H1 // 2, 2 * S], BF16, kind="Internal").ap()
        m["zs0"] = scratch("zs0", [TILES0 * P, D])
        m["ys0"] = scratch("ys0", [TILES0 * P, D])
        m["zs1"] = scratch("zs1", [TILES1 * P, D])
        m["ys1"] = scratch("ys1", [TILES1 * P, D])
        for s in ("const_in", "w1_in", "w2_in", "w_self_in", "zero_fill", "we_in"):
            m[s] = sem(s)
        m["sem"] = sem
        cross0(nc, a, m)
        self0(nc, a, m)
        route(nc, a, m, 0)
        moe(nc, a, m, 0)
        cross1(nc, a, m)
        route(nc, a, m, 1)
        moe(nc, a, m, 1)
        join1(nc, a, m, out)



def cross0(nc, a, m):
    cv, cr = Carve(m["w2"], m["W1WORDS"]), self0_weights(m)["carve"]
    n, W, FT = H0, DH0 + 1, H0 * DH0 // P
    wq, wo, bo = cv.take(P, KD, n * DH0), cv.take(P, FT, D), cv.take(P, D)
    wk, wv, ctxT = cv.take(CP, KC, n * DH0), cv.take(CP, KC, n * DH0), cv.take(CP, 2, KC, S)
    xn, xnT, qT, kT = cv.take(P, QT, D), cv.take(P, KD, S), cv.take(P, FT, S), cv.take(P, 2, FT, S)
    att, attT = cv.take(P, QT, n * DH0), cv.take(P, FT, S)
    p = cv.take(P, 2, QT, S)
    pT = cr.take(P, 2, QT * S)
    p1 = pT.rearrange("p s n -> p (s n)").bitcast(BF16).rearrange("p (s k n two) -> p s k n two", s=2, k=QT, two=2)
    p2 = cr.take(P, 2, QT * S, dt=F16)
    v1, v2 = cr.take(P, 2, QT * n, W, dt=BF16), cr.take(P, 2, QT * n, W, dt=F16)
    nmax, rec, spare = cr.take(P, 2, QT), cr.take(P, 2, QT * 2), cr.take(P, 1)
    ln = ln_buffers(m, cr, "c0_")
    sem = m["sem"]
    (s_full, max_done, exp_done, pt_full, pt_ev, p2_done, o_done, att_done, rec_ready, f_job, f_act, f_dve, t_job,
     t_dve, xn_ready, bo_added, start, x_in, w_in) = (sem("c0_" + s) for s in (
         "s_full", "max_done", "exp_done", "pt_full", "pt_ev", "p2_done", "o_done", "att_done", "rec_ready", "f_job",
         "f_act", "f_dve", "t_job", "t_dve", "xn_ready", "bo_added", "start", "x_in", "w_in"))
    ctx_in = [sem(f"c0_ctx_in{i}") for i in range(2)]
    ps, x, ident = m["psum"], m["x"], m["ident"]
    s_ps, pt_ps, o_ps, f_ps, t_ps = ps[0:2], ps[2], ps[3:5], ps[5:7], ps[7]
    NF, NTL = 7, 3

    def transposes(pe, bank, src):
        for k in range(2):
            for q in range(QT):
                ins = pe.transpose(bank[:, k * S + q * P:k * S + (q + 1) * P], src(k, q), ident[:, :])
        return ins

    def project(pe, bank, w, kn, mt, xT):
        for i in range(2):
            for k in range(kn):
                ins = pe.matmul(bank[:, i * S:(i + 1) * S], w[:, k, (mt + i) * P:(mt + i + 1) * P], xT[:, k, :],
                                start=(k == 0), stop=(k == kn - 1))
        return ins

    def pe_S(pe, b, par, h):
        if h % 4 == 0:
            ge(pe, f_act, NF * b + 6 + h // 4)
        ge(pe, exp_done, n * b + h - 1)
        lo, mt = DH0 * (h % 2), h // 2
        for q in range(QT):
            ins = pe.matmul(s_ps[h % 2][:, q * S:(q + 1) * S], qT[lo:lo + DH0, mt, q * P:(q + 1) * P],
                            kT[lo:lo + DH0, par, mt, :], start=True, stop=True)
        ins.then_inc(s_full, 1)

    def pe_T(pe, b, h):
        ge(pe, exp_done, n * b + h + 1)
        ge(pe, pt_ev, n * b + h)
        transposes(pe, pt_ps, lambda kt, q: p[:, h % 2, q, kt * P:(kt + 1) * P]).then_inc(pt_full, 1)

    def pe_PV(pe, b, par, h):
        if h == 0:
            ge(pe, f_act, NF * b + 4)
            ge(pe, f_dve, 2 * b + 2)
        if h % 2 == 0:
            ge(pe, att_done, (n // 2) * b + h // 2 - 1)
        ge(pe, p2_done, n * b + h + 1)
        for q in range(QT):
            c = (q * 2 + h % 2) * W
            k = 0
            for kt in range(QT):
                for lhsT in (p1[:, h % 2, kt, q * P:(q + 1) * P, 1], p2[:, h % 2, kt * S + q * P:kt * S + (q + 1) * P]):
                    for v in (v1, v2):
                        ins = pe.matmul(o_ps[h // 2 % 2][:, c:c + W], lhsT, v[:, par, kt * n + h, :],
                                        start=(k == 0), stop=(k == 4 * QT - 1))
                        k += 1
        ins.then_inc(o_done, 1)

    def pe_side(pe, s, b, par, front, tail):
        f, t = b + 1, b - 1
        cx = ctxT[:, 1 - par]
        if front and s == 0:
            ge(pe, ctx_in[1 - par], 16 * ((f - (1 - par)) // 2) + 16 if isinstance(f, int) else 8 * (f - (1 - par)) + 16)
            ge(pe, f_act, NF * f)
            project(pe, f_ps[0], wk, KC, 0, cx).then_inc(f_job, 1)
        if front and s == 1:
            project(pe, f_ps[1], wk, KC, 2, cx).then_inc(f_job, 1)
        if front and s in (2, 3):
            ge(pe, f_act, NF * f + s - 1)
            for k in range(KC):
                ins = pe.matmul(f_ps[s - 2][:, :], cx[:, k, (s - 2) * P:(s - 1) * P], wv[:, k, :],
                                start=(k == 0), stop=(k == KC - 1))
            ins.then_inc(f_job, 1)
        if front and s == 5:
            ge(pe, xn_ready, f + 1)
            ge(pe, f_act, NF * f + 3)
            ge(pe, f_dve, 2 * f + 1)
            transposes(pe, f_ps[0], lambda k, q: xn[:, q, k * P:(k + 1) * P]).then_inc(f_job, 1)
        if front and s in (6, 7):
            ge(pe, f_act, NF * f + 5)
            ge(pe, f_dve, 2 * f + 2)
            project(pe, f_ps[7 - s], wq, KD, 2 * (s - 6), xnT).then_inc(f_job, 1)
        if tail and s in (0, 2):
            ge(pe, att_done, (n // 2) * t + 2 + s)
            ge(pe, t_dve, NTL * t + s // 2)
            transposes(pe, t_ps, lambda k, q: att[:, q, (s + k) * P:(s + k + 1) * P]).then_inc(t_job, 1)
        if tail and s in (4, 5):
            if s == 4:
                ge(pe, t_dve, NTL * t + 2)
            q = s - 4
            for k in range(FT):
                ins = pe.matmul(t_ps[:, q * D:(q + 1) * D], attT[:, k, q * P:(q + 1) * P], wo[:, k, :],
                                start=(k == 0), stop=(k == FT - 1))
            if s == 5:
                ins.then_inc(t_job, 1)

    def pe_turn(pe, b, par, front, heads, tail):
        for s in range(n):
            if heads:
                pe_S(pe, b, par, s)
            if s == 0 and tail:
                pe_T(pe, b - 1, n - 1)
            if s > 0 and heads:
                pe_T(pe, b, s - 1)
            if s < 2 and tail:
                pe_PV(pe, b - 1, 1 - par, n + s - 2)
            if s >= 2 and heads:
                pe_PV(pe, b, par, s - 2)
            pe_side(pe, s, b, par, front, tail)

    def act_E(act, b, h):
        ge(act, max_done, n * b + h + 1)
        ge(act, pt_full, n * b + h - 1)
        for q in range(QT):
            ins = act.activation(p[:, h % 2, q, :], s_ps[h % 2][:, q * S:(q + 1) * S], ACT.Exp,
                                 bias=nmax[:, h % 2, q:q + 1])
        ins.then_inc(exp_done, 1)

    def act_C(act, b, h):
        ge(act, pt_full, n * b + h + 1)
        ge(act, o_done, n * b + h - 1)
        act.copy(pT[:, h % 2, :], pt_ps[:, :]).then_inc(pt_ev, 1)

    def flat(t):
        return t.rearrange("p k s -> p (k s)")

    def act_side(act, s, b, par, front, heads):
        f = b + 1
        if heads and s == 0:
            ge(act, f_job, NF * b + 7)
            act.mul(flat(qT[:, 2:4, :]), f_ps[0][:, :], DH0 ** -0.5).then_inc(f_act, 1)
        if front and s in (1, 2):
            ge(act, f_job, NF * f + s)
            act.copy(flat(kT[:, 1 - par, 2 * (s - 1):2 * s, :]), f_ps[s - 1][:, :]).then_inc(f_act, 1)
        if front and s in (3, 4):
            ge(act, f_job, NF * f + s)
            act.copy(v1[:, 1 - par, (s - 3) * n:(s - 2) * n, 0:DH0],
                     f_ps[s - 3][:, :].rearrange("p (h w) -> p h w", h=n)).then_inc(f_act, 1)
        if front and s == 5:
            ge(act, f_job, NF * f + 5)
            act.copy(flat(xnT), f_ps[0][:, :]).then_inc(f_act, 1)
        if front and s == 7:
            ge(act, f_job, NF * f + 6)
            act.mul(flat(qT[:, 0:2, :]), f_ps[1][:, :], DH0 ** -0.5).then_inc(f_act, 1)

    def act_turn(act, b, par, front, heads, tail):
        for s in range(n):
            act_side(act, s, b, par, front, heads) if s < 5 else None
            if s == 0 and tail:
                act_C(act, b - 1, n - 1)
            if s > 0 and heads:
                act_C(act, b, s - 1)
            if heads:
                act_E(act, b, s)
            act_side(act, s, b, par, front, heads) if s >= 5 else None

    def dve_M(dve, b, h):
        ge(dve, s_full, n * b + h + 1)
        dve.tensor_reduce(nmax[:, h % 2, :], s_ps[h % 2][:, :].rearrange("p (q k) -> p q k", q=QT),
                          AX, ALU.max, negate=True).then_inc(max_done, 1)

    def dve_R(dve, b, h):
        ge(dve, pt_ev, n * b + h + 1)
        dve.tensor_tensor(p2[:, h % 2, :], pT[:, h % 2, :], p1[:, h % 2, :, :, 1].rearrange("p k n -> p (k n)"),
                          ALU.subtract).then_inc(p2_done, 1)

    def dve_F(dve, b, g):
        ge(dve, o_done, n * b + 2 * g + 2)
        ge(dve, t_job, NTL * (b - 1) + 1 + g // 2)
        o = o_ps[g % 2][:, 0:QT * 2 * W].rearrange("p (c w) -> p c w", w=W)
        dve.reciprocal(rec[:, g % 2, :], o[:, :, DH0]).then_inc(rec_ready, 1)
        ge(dve, rec_ready, (n // 2) * b + g + 1)
        for q in range(QT):
            ins = dve.tensor_tensor(att[:, q, g * P:(g + 1) * P].rearrange("p (h w) -> p h w", w=DH0),
                                    o[:, q * 2:(q + 1) * 2, 0:DH0],
                                    rec[:, g % 2, q * 2:(q + 1) * 2].unsqueeze(2).to_broadcast([P, 2, DH0]), ALU.mult)
        ins.then_inc(att_done, 1)

    def dve_side(dve, s, b, par, front, tail):
        f, t = b + 1, b - 1
        if front and s == 0:
            ln_stats(dve, ln, lambda q: tile1(x, f, q), f)
            ln_variance(dve, ln, f)
        if front and s == 1:
            ge(dve, f_job, NF * f - 2)
            ln_apply(dve, ln, lambda q: tile1(x, f, q), lambda q: xn[:, q, :], f).then_inc(xn_ready, 1)
        if front and s in (3, 4):
            i = s - 3
            ge(dve, f_act, NF * f + s)
            dve.tensor_tensor(v2[:, 1 - par, i * n:(i + 1) * n, 0:DH0], f_ps[i][:, :].rearrange("p (h w) -> p h w", h=n),
                              v1[:, 1 - par, i * n:(i + 1) * n, 0:DH0], ALU.subtract).then_inc(f_dve, 1)
        if tail and s in (1, 3):
            ge(dve, t_job, NTL * t + 1 + s // 2)
            dve.tensor_scalar(flat(attT[:, s - 1:s + 1, :]), t_ps[:, :], 1.0, None, ALU.mult).then_inc(t_dve, 1)
        if tail and s == 6:
            ge(dve, t_job, NTL * t + 3)
            ge(dve, bo_added, t + 1)
            dve.tensor_tensor(tile2(x, t), t_ps[:, :], tile2(x, t), ALU.add).then_inc(t_dve, 1)

    def dve_turn(dve, b, par, front, heads, tail):
        for s in range(n):
            if heads:
                dve_M(dve, b, s)
            if s % 2 == 0 and s < 4 and tail:
                dve_F(dve, b - 1, 2 + s // 2)
            if s % 2 == 0 and s >= 4 and heads:
                dve_F(dve, b, s // 2 - 2)
            if s == 0 and tail:
                dve_R(dve, b - 1, n - 1)
            if s > 0 and heads:
                dve_R(dve, b, s - 1)
            dve_side(dve, s, b, par, front, tail)

    def pool_turn(pool, b, par, front, heads, tail):
        if front:
            ln_power(pool, ln, b + 1)
            ge(pool, xn_ready, b + 2)
            pool.tensor_tensor(tile2(x, b + 1).rearrange("p (q d) -> p q d", q=QT),
                               tile2(x, b + 1).rearrange("p (q d) -> p q d", q=QT),
                               bo.unsqueeze(1).to_broadcast([P, QT, D]), ALU.add).then_inc(bo_added, 1)

    def turns(eng, turn):
        turn(eng, -1, 1, True, False, False)
        turn(eng, 0, 0, True, True, False)
        turn(eng, 1, 1, True, True, True)
        turn(eng, 2, 0, True, True, True)
        with eng.Fori(1, B // 2 - 1) as i:
            turn(eng, i * 2 + 1, 1, True, True, True)
            turn(eng, i * 2 + 2, 0, True, True, True)
        turn(eng, B - 1, 1, False, True, True)
        turn(eng, B, 0, False, False, True)

    with nc.Block() as block:
        @block.sync
        def _(sp):
            sp.dma_start(wk, a["wk0"]).then_inc(w_in, 16)
            sp.dma_start(ctxT[:, 0], a["ctxT"][0]).then_inc(ctx_in[0], 16)
            sp.dma_start(wv, a["wv0"]).then_inc(w_in, 16)
            sp.dma_start(x[:, :], a["x"]).then_inc(x_in, 16)
            sp.dma_start(m["ident"][:, :], a["ident"]).then_inc(m["const_in"], 16)
            sp.dma_start(wq, a["wq0"]).then_inc(w_in, 16)
            sp.dma_start(wo, a["wo0"]).then_inc(w_in, 16)
            sp.dma_start(bo, a["bo0"].partition_broadcast(P)).then_inc(w_in, 16)
            sp.dma_start(ctxT[:, 1], a["ctxT"][1]).then_inc(ctx_in[1], 16)
            sp.dma_start(m["upper"][:, :], a["upper"]).then_inc(m["const_in"], 16)
            sp.dma_start(m["ones"][:, :], a["ones"]).then_inc(m["const_in"], 16)
            wself = self0_weights(m)
            for name in ("wq", "wk", "wv", "wp", "ln1", "ln2", "ln2w", "ln2b", "gw", "gb"):
                src = a["s_" + name]
                if name in ("ln2w", "ln2b", "gb"):
                    src = src.partition_broadcast(P)
                sp.dma_start(wself[name], src).then_inc(m["w_self_in"], 16)
            w1v = m["w1"][:, :].rearrange("p (e n) -> p e n", e=E0)
            for b in range(B):
                if b + 2 < B:
                    sp.wait_ge(f_job, NF * b + 4)
                    sp.dma_start(ctxT[:, b % 2], a["ctxT"][b + 2]).then_inc(ctx_in[b % 2], 16)
                sp.dma_start(w1v[:, b, :], a["w1"][b]).then_inc(m["w1_in"], 16)

        @block.gpsimd
        def _(pool):
            pool.memset(v1.rearrange("p a g w -> p (a g) w")[:, :, DH0:W], 1.0).then_inc(start, 1)
            pool.memset(v2.rearrange("p a g w -> p (a g) w")[:, :, DH0:W], 0.0).then_inc(start, 1)
            pool.memset(m["power"][:, :], -0.5).then_inc(start, 1)
            pool.memset(m["cw"][:, :, :], 1.0).then_inc(start, 1)
            pool.memset(m["z"][:, :], 0.0).then_inc(start, 1)
            pool.wait_ge(start, 5)
            for name, tiles in (("zs0", TILES0), ("zs1", TILES1)):
                for t in range(0, tiles, NT):
                    k = min(NT, tiles - t)
                    pool.dma_start(m[name][t * P:(t + k) * P, :].rearrange("(t p) d -> p t d", p=P),
                                   m["z"][:, 0:k * D].rearrange("p (t d) -> p t d", d=D))\
                        .then_inc(m["zero_fill"], 16)
            pool.wait_ge(w_in, 16 * 5)
            turns(pool, pool_turn)

        @block.tensor
        def _(pe):
            pe.wait_ge(w_in, 16 * 5)
            pe.wait_ge(m["const_in"], 48)
            pe.wait_ge(start, 5)
            turns(pe, pe_turn)

        @block.scalar
        def _(act):
            turns(act, act_turn)

        @block.vector
        def _(dve):
            dve.wait_ge(x_in, 16)
            turns(dve, dve_turn)



def self0_weights(m):
    cv = Carve(m["r"], m["RW"])
    w = dict(wq=cv.take(P, KD, D), wk=cv.take(P, KD, D), wv=cv.take(P, KD, D), wp=cv.take(P, KD, D),
             ln1=cv.take(P, 2, KD), ln2=cv.take(P, 2, KD), ln2w=cv.take(P, D), ln2b=cv.take(P, D),
             gw=cv.take(P, KD, E0), gb=cv.take(P, E0))
    w["carve"] = cv
    return w


def self0(nc, a, m):
    w = self0_weights(m)
    cv, cw = w["carve"], Carve(m["w2"], m["W1WORDS"])
    cw.at = m["W1WORDS"] // 2
    G, W = H1 // 2, DH1 + 1
    TERMS = 6
    p = cv.take(P, 2, QT, S)
    pT = cv.take(P, 4, QT * S)
    p1 = pT.rearrange("p s n -> p (s n)").bitcast(BF16).rearrange("p (s k n two) -> p s k n two", s=4, k=QT, two=2)
    p2 = cv.take(P, 4, QT * S, dt=F16)
    v1 = cv.take(P, 2, QT * H1, W, dt=BF16)
    v2 = cv.take(P, 2, QT * H1, W, dt=F16)
    att = cv.take(P, 2, QT, D)
    xn, zT, attT = cv.take(P, QT, D), cv.take(P, KD, S), cv.take(P, KD, S)
    pool_spare = cv.take(P, 1)
    nmax, rec = cv.take(P, 2, QT), cv.take(P, 2, QT * G)
    z2T = attT
    qS, kS = cw.take(TERMS * DH1, H1, S, dt=BF16), cw.take(TERMS * DH1, H1, S, dt=BF16)
    qp, kp = [[cw.take(P, 2 * S, dt=BF16) for _ in range(3)] for _ in range(2)]
    rq, rk, y1, n2, tmp = cw.take(P, 2 * S), cw.take(P, 2 * S), cw.take(P, QT * D), cw.take(P, QT, D), cw.take(P, QT, D)
    sem = m["sem"]
    ln = [ln_buffers(m, cv, f"s0_ln{i}_") for i in range(3)]
    (s_full, max_done, exp_done, pt_full, pt_ev, p2_dve, p2_pool, o_done, att_done, rec_ready, ones_set,
     f_job, f_act, f_dve, f_pool, t_job, t_act, t_dve, y0_ready, xn_ready, n2_ready, x_added, t_pool) = (
        sem("s0_" + s) for s in (
            "s_full", "max_done", "exp_done", "pt_full", "pt_ev", "p2_dve", "p2_pool", "o_done", "att_done",
            "rec_ready", "ones_set", "f_job", "f_act", "f_dve", "f_pool", "t_job", "t_act", "t_dve", "y0_ready",
            "xn_ready", "n2_ready", "x_added", "t_pool"))
    q_out, k_out = sem("s0_q_out"), sem("s0_k_out")
    half_in = [sem(f"s0_half_in{i}") for i in range(2)]
    qD, kD = m["q_parts"], m["k_parts"]
    s_ps, pt_ps, o_ps, f_ps, t_ps = m["psum"][0:2], m["psum"][2:4], m["psum"][4:6], m["psum"][6], m["psum"][7]
    x, z, ident = m["x"], m["z"], m["ident"]
    lg = m["logits"][:, 0:NT * E0]
    NW = 10
    n = H1
    LAG_T, LAG_R, LAG_PV = 2, 3, 5


    def pe_S(pe, b, h):
        if h % G == 0:
            ge(pe, half_in[h // G], 64 * b + 64)
        ge(pe, exp_done, n * b + h - 1)
        for q in range(QT):
            ins = pe.matmul(s_ps[h % 2][:, q * S:(q + 1) * S], qS[:, h, q * P:(q + 1) * P], kS[:, h, :],
                            start=True, stop=True)
        ins.then_inc(s_full, 1)

    def pe_T(pe, b, h):
        ge(pe, exp_done, n * b + h + 1)
        ge(pe, pt_ev, n * b + h - 1)
        for kt in range(QT):
            for q in range(QT):
                at = kt * S + q * P
                ins = pe.transpose(pt_ps[h % 2][:, at:at + P], p[:, h % 2, q, kt * P:(kt + 1) * P], ident[:, :])
        ins.then_inc(pt_full, 1)

    def pe_PV(pe, b, par, h):
        if h == 0:
            ge(pe, f_act, 4 * b + 4)
            ge(pe, f_dve, 3 * b + 3)
        if h % G == 0:
            ge(pe, att_done, 2 * b + h // G - 1)
        if h % 2 == 0:
            ge(pe, p2_dve, (n // 2) * b + h // 2 + 1)
        else:
            ge(pe, p2_pool, (n // 2) * b + h // 2 + 1)
        for q in range(QT):
            o = o_ps[h // G][:, (q * G + h % G) * W:(q * G + h % G + 1) * W]
            k = 0
            for kt in range(QT):
                cols = slice(kt * S + q * P, kt * S + (q + 1) * P)
                for lhsT in (p1[:, h % 4, kt, q * P:(q + 1) * P, 1], p2[:, h % 4, cols]):
                    for v in (v1, v2):
                        ins = pe.matmul(o, lhsT, v[:, par, kt * H1 + h, :], start=(k == 0), stop=(k == 4 * QT - 1))
                        k += 1
        ins.then_inc(o_done, 1)

    def pe_side(pe, s, b, par, front, tail):
        f, t = b + 1, b - 1
        if front and s == 5:
            ge(pe, xn_ready, f + 1)
            ge(pe, f_act, 4 * f)
            ge(pe, f_dve, 3 * f)
            for k in range(KD):
                for q in range(QT):
                    ins = pe.transpose(f_ps[:, k * S + q * P:k * S + (q + 1) * P], xn[:, q, k * P:(k + 1) * P],
                                       ident[:, :])
            ins.then_inc(f_job, 1)
        if front and s in (6, 8):
            ge(pe, f_act, 4 * f + (1 if s == 6 else 2))
            if s == 8:
                ge(pe, f_dve, 3 * f + 1)
            wt = w["wq"] if s == 6 else w["wk"]
            for i in range(2):
                for k in range(KD):
                    ins = pe.matmul(f_ps[:, i * S:(i + 1) * S], wt[:, k, i * P:(i + 1) * P], zT[:, k, :],
                                    start=(k == 0), stop=(k == KD - 1))
            ins.then_inc(f_job, 1)
        if front and s == 10:
            ge(pe, f_act, 4 * f + 3)
            ge(pe, f_dve, 3 * f + 2)
            for q in range(QT):
                for k in range(KD):
                    ins = pe.matmul(f_ps[:, q * D:(q + 1) * D], zT[:, k, q * P:(q + 1) * P], w["wv"][:, k, :],
                                    start=(k == 0), stop=(k == KD - 1))
            ins.then_inc(f_job, 1)
        if tail and s == 6:
            ge(pe, att_done, 2 * t + 2)
            ge(pe, t_dve, 2 * t)
            for k in range(KD):
                for q in range(QT):
                    ins = pe.transpose(t_ps[:, k * S + q * P:k * S + (q + 1) * P],
                                       att[:, 1 - par, q, k * P:(k + 1) * P], ident[:, :])
            ins.then_inc(t_job, 1)
        if tail and s == 8:
            ge(pe, t_act, 2 * t + 1)
            for q in range(QT):
                for k in range(KD):
                    ins = pe.matmul(t_ps[:, q * D:(q + 1) * D], attT[:, k, q * P:(q + 1) * P], w["wp"][:, k, :],
                                    start=(k == 0), stop=(k == KD - 1))
            ins.then_inc(t_job, 1)
        if tail and s == 13:
            ge(pe, n2_ready, t + 1)
            ge(pe, t_dve, 2 * t + 1)
            for k in range(KD):
                for q in range(QT):
                    ins = pe.transpose(t_ps[:, k * S + q * P:k * S + (q + 1) * P], n2[:, q, k * P:(k + 1) * P],
                                       ident[:, :])
            ins.then_inc(t_job, 1)
        if tail and s == 15:
            ge(pe, t_act, 2 * t + 2)
            for q in range(QT):
                for k in range(KD):
                    ins = pe.matmul(t_ps[:, q * E0:(q + 1) * E0], z2T[:, k, q * P:(q + 1) * P], w["gw"][:, k, :],
                                    start=(k == 0), stop=(k == KD - 1))
            ins.then_inc(t_job, 1)

    def pe_turn(pe, b, par, front, heads, tail):
        for s in range(n):
            if heads:
                pe_S(pe, b, s)
            if s < LAG_T and tail:
                pe_T(pe, b - 1, n + s - LAG_T)
            if s >= LAG_T and heads:
                pe_T(pe, b, s - LAG_T)
            if s < LAG_PV and tail:
                pe_PV(pe, b - 1, 1 - par, n + s - LAG_PV)
            if s >= LAG_PV and heads:
                pe_PV(pe, b, par, s - LAG_PV)
            pe_side(pe, s, b, par, front, tail)

    def act_E(act, b, h):
        ge(act, max_done, n * b + h + 1)
        ge(act, pt_full, n * b + h - 1)
        for q in range(QT):
            ins = act.activation(p[:, h % 2, q, :], s_ps[h % 2][:, q * S:(q + 1) * S], ACT.Exp,
                                 bias=nmax[:, h % 2, q:q + 1])
        ins.then_inc(exp_done, 1)

    def act_C(act, b, h):
        ge(act, pt_full, n * b + h + 1)
        ge(act, o_done, n * b + h - 3)
        act.copy(pT[:, h % 4, :], pt_ps[h % 2][:, :]).then_inc(pt_ev, 1)

    def act_side(act, s, b, par, front, tail):
        f, t = b + 1, b - 1
        if front and s == 5:
            ge(act, f_job, 4 * f + 1)
            for k in range(KD):
                ins = act.activation(zT[:, k, :], f_ps[:, k * S:(k + 1) * S], ACT.Identity,
                                     bias=w["ln1"][:, 1, k:k + 1], scale=w["ln1"][:, 0, k:k + 1])
            ins.then_inc(f_act, 1)
        if front and s == 6:
            ge(act, f_job, 4 * f + 2)
            ge(act, q_out, 48 * f)
            act.mul(qp[0], f_ps[:, :], DH1 ** -0.5).then_inc(f_act, 1)
        if front and s == 8:
            ge(act, f_job, 4 * f + 3)
            ge(act, k_out, 48 * f)
            act.copy(kp[0], f_ps[:, :]).then_inc(f_act, 1)
        if front and s == 10:
            ge(act, f_job, 4 * f + 4)
            ge(act, o_done, n * (f - 1))
            act.copy(v1[:, 1 - par, :, 0:DH1], f_ps[:, :].rearrange("p (g w) -> p g w", w=DH1)).then_inc(f_act, 1)
        if tail and s == 6:
            ge(act, t_job, 4 * t + 1)
            act.copy(attT.rearrange("p k s -> p (k s)"), t_ps[:, :]).then_inc(t_act, 1)
        if tail and s == 13:
            ge(act, t_job, 4 * t + 3)
            for k in range(KD):
                ins = act.activation(z2T[:, k, :], t_ps[:, k * S:(k + 1) * S], ACT.Identity,
                                     bias=w["ln2"][:, 1, k:k + 1], scale=w["ln2"][:, 0, k:k + 1])
            ins.then_inc(t_act, 1)

    def act_turn(act, b, par, front, heads, tail):
        for s in range(n):
            if s < LAG_T and tail:
                act_C(act, b - 1, n + s - LAG_T)
            if s >= LAG_T and heads:
                act_C(act, b, s - LAG_T)
            if heads:
                act_E(act, b, s)
            act_side(act, s, b, par, front, tail)

    def dve_M(dve, b, h):
        ge(dve, s_full, n * b + h + 1)
        dve.tensor_reduce(nmax[:, h % 2, :], s_ps[h % 2][:, :].rearrange("p (q k) -> p q k", q=QT),
                          AX, ALU.max, negate=True).then_inc(max_done, 1)

    def rest(eng, b, h, done):
        ge(eng, pt_ev, n * b + h + 1)
        eng.tensor_tensor(p2[:, h % 4, :], pT[:, h % 4, :], p1[:, h % 4, :, :, 1].rearrange("p k n -> p (k n)"),
                          ALU.subtract).then_inc(done, 1)

    def dve_F(dve, b, par, g):
        ge(dve, o_done, n * b + G * (g + 1))
        ge(dve, t_job, 4 * (b - 2) + 1)
        o = o_ps[g][:, 0:QT * G * W].rearrange("p (c w) -> p c w", w=W)
        dve.reciprocal(rec[:, g, :], o[:, :, DH1]).then_inc(rec_ready, 1)
        ge(dve, rec_ready, 2 * b + g + 1)
        for q in range(QT):
            ins = dve.tensor_tensor(att[:, par, q, g * P:(g + 1) * P].rearrange("p (h w) -> p h w", w=DH1),
                                    o[:, q * G:(q + 1) * G, 0:DH1],
                                    rec[:, g, q * G:(q + 1) * G].unsqueeze(2).to_broadcast([P, G, DH1]), ALU.mult)
        ins.then_inc(att_done, 1)

    def dve_side(dve, s, b, par, front, tail):
        f, t = b + 1, b - 1
        if front and s == 0:
            ln_stats(dve, ln[0], lambda q: tile1(x, f, q), f)
            ln_variance(dve, ln[0], f)
        if front and s == 2:
            ln_apply(dve, ln[0], lambda q: tile1(x, f, q), lambda q: tile1(z, f, q), f).then_inc(y0_ready, 1)
            ge(dve, y0_ready, f + 1)
            dve.memset(ln[1]["spare"], 0.0)
            ln_stats(dve, ln[1], lambda q: tile1(z, f, q), f)
        if front and s == 3:
            ln_variance(dve, ln[1], f)
        if front and s == 4:
            ge(dve, f_job, 4 * f - 3)
            ln_apply(dve, ln[1], lambda q: tile1(z, f, q), lambda q: xn[:, q, :], f).then_inc(xn_ready, 1)
        if front and s == 6:
            ge(dve, f_act, 4 * f + 2)
            ge(dve, f_pool, 4 * f - 2)
            dve.scalar_tensor_tensor(rq, f_ps[:, :], DH1 ** -0.5, qp[0], ALU.mult, ALU.subtract).then_inc(f_dve, 1)
        if front and s == 8:
            ge(dve, f_act, 4 * f + 3)
            ge(dve, f_pool, 4 * f)
            dve.tensor_tensor(rk, f_ps[:, :], kp[0], ALU.subtract).then_inc(f_dve, 1)
        if front and s == 10:
            ge(dve, f_act, 4 * f + 4)
            dve.tensor_tensor(v2[:, 1 - par, :, 0:DH1], f_ps[:, :].rearrange("p (g w) -> p g w", w=DH1),
                              v1[:, 1 - par, :, 0:DH1], ALU.subtract).then_inc(f_dve, 1)
        if tail and s == 5:
            dve_F(dve, t, 1 - par, 1)
        if tail and s == 8:
            ge(dve, t_job, 4 * t + 2)
            ge(dve, x_added, t)
            dve.tensor_tensor(y1, t_ps[:, :], tile2(z, t), ALU.add).then_inc(t_dve, 1)
        if tail and s == 9:
            ge(dve, t_dve, 2 * t + 1)
            dve.memset(ln[1]["spare"], 0.0)
            ln_stats(dve, ln[2], lambda q: y1[:, q * D:(q + 1) * D], t)
        if tail and s == 10:
            ln_variance(dve, ln[2], t)
        if tail and s == 12:
            ge(dve, t_pool, 2 * t)
            ge(dve, t_job, 4 * t - 1)
            ln_apply(dve, ln[2], lambda q: y1[:, q * D:(q + 1) * D], lambda q: n2[:, q, :], t).then_inc(n2_ready, 1)
        if tail and s == 15:
            ge(dve, t_job, 4 * t + 4)
            dve.tensor_tensor(lg[:, bass.ds(t * (QT * E0), QT * E0)].rearrange("p (q e) -> p q e", q=QT),
                              t_ps[:, 0:QT * E0].rearrange("p (q e) -> p q e", q=QT),
                              w["gb"].unsqueeze(1).to_broadcast([P, QT, E0]), ALU.add).then_inc(t_dve, 1)

    def dve_turn(dve, b, par, front, heads, tail):
        for s in range(n):
            if heads:
                dve_M(dve, b, s)
            if s == 1 and tail:
                rest(dve, b - 1, n - 2, p2_dve)
            if s >= LAG_R and (s - LAG_R) % 2 == 0 and heads:
                rest(dve, b, s - LAG_R, p2_dve)
            if s == G + LAG_PV and heads:
                dve_F(dve, b, par, 0)
            dve_side(dve, s, b, par, front, tail)

    def pool_turn(pool, b, par, front, heads, tail):
        f, t = b + 1, b - 1
        for s in range(n):
            if s < LAG_R and (s - LAG_R) % 2 == 1 and tail:
                rest(pool, b - 1, n + s - LAG_R, p2_pool)
            if s >= LAG_R and (s - LAG_R) % 2 == 1 and heads:
                rest(pool, b, s - LAG_R, p2_pool)
            if front and s == 0:
                ln_power(pool, ln[0], f)
            if front and s == 3:
                ln_power(pool, ln[1], f)
            if front and s in (7, 9):
                r, parts, c = (rq, qp, 0) if s == 7 else (rk, kp, 1)
                ge(pool, f_dve, 3 * f + c + 1)
                pool.tensor_tensor(pool_spare, m["power"][:, 0:1], m["power"][:, 0:1], ALU.mult)
                pool.tensor_copy(parts[1], r).then_inc(f_pool, 1)
                ge(pool, f_pool, 4 * f + 2 * c + 1)
                pool.tensor_tensor(parts[2], r, parts[1], ALU.subtract).then_inc(f_pool, 1)
            if tail and s == 10:
                ge(pool, t_dve, 2 * t + 1)
                pool.tensor_tensor(tile2(x, t), tile2(x, t), y1, ALU.add).then_inc(x_added, 1)
            if tail and s == 11:
                ln_power(pool, ln[2], t)
            if tail and s == 13:
                ge(pool, n2_ready, t + 1)
                pool.tensor_tensor(tmp, n2, w["ln2w"].unsqueeze(1).to_broadcast([P, QT, D]), ALU.mult).then_inc(t_pool, 1)
                ge(pool, t_pool, 2 * t + 1)
                pool.tensor_tensor(tile2(z, t).rearrange("p (q d) -> p q d", q=QT), tmp,
                                   w["ln2b"].unsqueeze(1).to_broadcast([P, QT, D]), ALU.add).then_inc(t_pool, 1)

    def sp_front(sp, f, par):
        def out_q(i, at):
            ge(sp, *at)
            sp.dma_start(qD[par, i].rearrange("d g n -> (d g) n"), qp[i]).then_inc(q_out, 16)

        def out_k(i, lo, rep, at):
            ge(sp, *at)
            sp.dma_start(kD[par, lo:lo + rep].rearrange("r d g n -> (d g) r n"),
                         kp[i].unsqueeze(1).to_broadcast([P, rep, 2 * S])).then_inc(k_out, 16)

        out_q(0, (f_act, 4 * f + 2))
        out_k(0, 0, 3, (f_act, 4 * f + 3))
        out_q(1, (f_pool, 4 * f + 1))
        out_q(2, (f_pool, 4 * f + 2))
        out_k(1, 3, 2, (f_pool, 4 * f + 3))
        out_k(2, 5, 1, (f_pool, 4 * f + 4))
        ge(sp, q_out, 48 * f + 48)
        ge(sp, k_out, 48 * f + 48)
        for i in range(2):
            ge(sp, s_full, n * (f - 1) + G * (i + 1))
            hs = slice(i * G, (i + 1) * G)
            for lo, cnt in ((0, 3), (3, 2), (5, 1)):
                sp.dma_start(qS[lo * DH1:(lo + cnt) * DH1, hs, :],
                             qD[par, 0:cnt, :, :, i * S:(i + 1) * S].rearrange("j d g n -> (j d) g n"))\
                    .then_inc(half_in[i], 16)
            sp.dma_start(kS[:, hs, :], kD[par, :, :, :, i * S:(i + 1) * S].rearrange("j d g n -> (j d) g n"))\
                .then_inc(half_in[i], 16)

    def turns(eng, turn):
        turn(eng, -1, 1, True, False, False)
        turn(eng, 0, 0, True, True, False)
        turn(eng, 1, 1, True, True, True)
        turn(eng, 2, 0, True, True, True)
        with eng.Fori(1, B // 2 - 1) as i:
            turn(eng, i * 2 + 1, 1, True, True, True)
            turn(eng, i * 2 + 2, 0, True, True, True)
        turn(eng, B - 1, 1, False, True, True)
        turn(eng, B, 0, False, False, True)

    with nc.Block() as block:
        @block.sync
        def _(sp):
            w2v = m["w2"][:, :].rearrange("p (e n) -> p e n", e=E0)
            for e in range(E0 // 2):
                sp.dma_start(w2v[:, e, :], a["w2"][e]).then_inc(m["w2_in"], 16)
            sp_front(sp, 0, 0)
            sp_front(sp, 1, 1)
            with sp.Fori(0, B // 2 - 1) as i:
                sp_front(sp, i * 2 + 2, 0)
                sp_front(sp, i * 2 + 3, 1)

        @block.gpsimd
        def _(pool):
            pool.memset(v1.rearrange("p a g w -> p (a g) w")[:, :, DH1:W], 1.0).then_inc(ones_set, 1)
            pool.memset(v2.rearrange("p a g w -> p (a g) w")[:, :, DH1:W], 0.0).then_inc(ones_set, 1)
            pool.wait_ge(m["w_self_in"], 16 * NW)
            pool.wait_ge(m["zero_fill"], 16 * 6)
            pool.nop().then_inc(ones_set, 1)
            turns(pool, pool_turn)

        @block.tensor
        def _(pe):
            pe.wait_ge(ones_set, 3)
            pe.wait_ge(m["w_self_in"], 16 * NW)
            turns(pe, pe_turn)

        @block.scalar
        def _(act):
            act.wait_ge(m["w_self_in"], 16 * NW)
            turns(act, act_turn)

        @block.vector
        def _(dve):
            dve.wait_ge(ones_set, 3)
            dve.wait_ge(m["w_self_in"], 16 * NW)
            turns(dve, dve_turn)



def route(nc, a, m, which):
    E, top, tiles = (E0, 1, TILES0) if which == 0 else (E1, TOP1, TILES1)
    tag = f"r{which}_"
    cv = Carve(m["r"], m["RW"])
    if which == 0:
        cv.at = 4000
    mask, rank, steps, jx = (cv.take(P, E, E), cv.take(P, E), cv.take(P, NC), cv.take(P, tiles))
    val, mx, eq, any_oh = cv.take(P, NT, E), cv.take(P, NT), cv.take(P, NT, E), cv.take(P, NT, E)
    oh = [cv.take(P, NT, E) for _ in range(top)]
    slotf, cnt, cmp, padded = cv.take(P, NT), cv.take(P, E), cv.take(P, E, NC), cv.take(P, E)
    lt, end, base = cv.take(P, E, E), cv.take(P, E), cv.take(P, E)
    own_cmp, own_f = cv.take(P, tiles, E), cv.take(P, tiles)
    sem = m["sem"]
    own, oh_ready, rank_ready = sem(tag + "own"), sem(tag + "oh_ready"), sem(tag + "rank_ready")
    mask_in, slots_ready, sent = sem(tag + "mask_in"), sem(tag + "slots_ready"), sem(tag + "sent")
    lg = m["logits"][:, 0:NT * E].rearrange("p (t e) -> p t e", t=NT)
    ohb = m["oh_bf"][:, 0:NT * E]
    ranks, counts = m["psum"][0][:, 0:NT * E], m["psum"][1][:, 0:NT * E]
    zs = m[f"zs{which}"]
    src = m["z"]
    if which == 1:
        w = ffn1_buffers(m)
        sw1, sw2, sb1, x3T, cs = w["sw1"], w["sw2"], w["sb1"], w["x3T"], w["carve"]
        shT, b2, cwT = cs.take(P, B, KD, S), cs.take(E1 + 1, D), cs.take(E1 + 1, NT, P)
        h_full, h_ready, cw_full, cwT_ready, y_full, y_added = (sem("s1_" + t) for t in (
            "h_full", "h_ready", "cw_full", "cwT_ready", "y_full", "y_added"))
        ps, x = m["psum"], m["x"]

    def over_e(v):
        return v.unsqueeze(2).to_broadcast([P, NT, E])

    def over_t(v):
        return v.unsqueeze(1).to_broadcast([P, NT, E])

    with nc.Block() as block:
        @block.sync
        def _(sp):
            for dst, name in ((mask, "incl"), (rank, "rank"), (steps, "steps"), (jx, "jx")):
                n = dst.free_size()
                flat = dst if len(dst.shape) == 2 else dst.rearrange("p a b -> p (a b)")
                sp.dma_start(flat, a[name + str(which)].partition_broadcast(P)).then_inc(mask_in, 16)
            if which == 1:
                sp.dma_start(b2, a["b2"]).then_inc(mask_in, 16)
            if which == 0:
                w2v = m["w2"][:, :].rearrange("p (e n) -> p e n", e=E0)
                for e in range(E0 // 2, E0):
                    sp.dma_start(w2v[:, e, :], a["w2"][e]).then_inc(m["w2_in"], 16)

        @block.tensor
        def _(pe):
            if which == 1:
                for b in range(B):
                    if b >= 2:
                        pe.wait_ge(h_ready, b - 1)
                    for i in range(KD):
                        for k in range(KD):
                            ins = pe.matmul(ps[2 + b % 2][:, i * S:(i + 1) * S], sw1[:, k, i * P:(i + 1) * P],
                                            x3T[:, k, b * S:(b + 1) * S], start=(k == 0), stop=(k == KD - 1))
                    ins.then_inc(h_full, 1)
            pe.wait_ge(oh_ready, 1)
            pe.matmul(ranks, m["upper"][:, :], ohb, start=True, stop=False)
            v = ranks.rearrange("p (t e) -> p t e", t=NT)
            for t in range(NT - 1):
                pe.matmul(v[:, t + 1:NT, :], m["ones"][:, :],
                          ohb[:, t * E:(t + 1) * E].unsqueeze(1).to_broadcast([P, NT - 1 - t, E]),
                          start=False, stop=(t == NT - 2))
            pe.matmul(counts, m["ones"][:, :], ohb, start=True, stop=True).then_inc(rank_ready, 1)
            if which == 1:
                pe.wait_ge(slots_ready, 1)
                for j in range(4):
                    for t in range(4):
                        ins = pe.transpose(ps[4 + j][0:E1 + 1, t * P:(t + 1) * P], m["cw"][:, 4 * j + t, :], m["ident"][:, :])
                    ins.then_inc(cw_full, 1)
                pe.wait_ge(mask_in, 80)
                pe.wait_ge(h_ready, B)
                for b in range(B):
                    pe.wait_ge(cwT_ready, b // 2 + 1)
                    if b >= 2:
                        pe.wait_ge(y_added, b - 1)
                    for q in range(QT):
                        y = ps[2 + b % 2][:, q * D:(q + 1) * D]
                        for k in range(KD):
                            pe.matmul(y, shT[:, b, k, q * P:(q + 1) * P], sw2[:, k, :], start=(k == 0), stop=False)
                        ins = pe.matmul(y, cwT[:, QT * b + q, :], b2, start=False, stop=True)
                    ins.then_inc(y_full, 1)

        @block.vector
        def _(dve):
            ch = Chain(dve, own, 0)

            def step(ins):
                ch.done(ins)
                ch.wait()

            dve.wait_ge(mask_in, 64 if which == 0 else 80)
            if which == 1:
                step(dve.tensor_reduce(mx, lg, AX, ALU.max))
                step(dve.tensor_tensor(val, lg, over_e(mx), ALU.subtract))
                dve.nop().then_inc(m["r1_shifted"], 1)
                dve.wait_ge(m["r1_exp"], 1)
                step(dve.tensor_reduce(mx, val, AX, ALU.add))
                step(dve.reciprocal(slotf, mx))
                step(dve.tensor_tensor(val, val, over_e(slotf), ALU.mult))
            else:
                step(dve.tensor_copy(val, lg))
            for k in range(top):
                step(dve.tensor_reduce(mx, val, AX, ALU.max))
                if which == 1:
                    step(dve.tensor_copy(m["top_p"][:, k, :], mx))
                step(dve.tensor_tensor(eq, val, over_e(mx), ALU.is_equal))
                step(dve.tensor_tensor(eq, eq, over_t(rank), ALU.mult))
                step(dve.tensor_reduce(mx, eq, AX, ALU.max))
                step(dve.tensor_tensor(oh[k], over_t(rank), over_e(mx), ALU.is_equal))
                if k + 1 < top:
                    step(dve.scalar_tensor_tensor(val, oh[k], -4.0, val, ALU.mult, ALU.add))
            total = oh[0]
            if which == 1:
                step(dve.tensor_tensor(any_oh, oh[0], oh[1], ALU.add))
                step(dve.tensor_tensor(any_oh, any_oh, oh[2], ALU.add))
                total = any_oh
                step(dve.scalar_tensor_tensor(val, oh[2], -4.0, val, ALU.mult, ALU.add))
                step(dve.scalar_tensor_tensor(val, any_oh, 4.0, val, ALU.mult, ALU.add))
                step(dve.tensor_tensor(m["cw"][:, :, 0:E], oh[0],
                                       over_e(m["top_p"][:, 0, :]), ALU.mult))
                for k in (1, 2):
                    step(dve.tensor_tensor(eq, oh[k], over_e(m["top_p"][:, k, :]), ALU.mult))
                    step(dve.tensor_tensor(m["cw"][:, :, 0:E], m["cw"][:, :, 0:E], eq, ALU.add))
            dve.tensor_copy(ohb, total.rearrange("p t e -> p (t e)")).then_inc(oh_ready, 1)
            dve.wait_ge(rank_ready, 1)
            step(dve.tensor_reduce(cnt, counts.rearrange("p (t e) -> p e t", t=NT), AX, ALU.add))
            step(dve.tensor_tensor(cmp, cnt.unsqueeze(2).to_broadcast([P, E, NC]),
                                   steps.unsqueeze(1).to_broadcast([P, E, NC]), ALU.is_gt))
            step(dve.tensor_reduce(padded, cmp, AX, ALU.add))
            step(dve.tensor_tensor(lt, mask, padded.unsqueeze(1).to_broadcast([P, E, E]), ALU.mult))
            step(dve.tensor_reduce(end, lt, AX, ALU.add))
            step(dve.tensor_tensor(base, end, padded, ALU.subtract))
            step(dve.scalar_tensor_tensor(eq, over_t(base), float(P), ranks.rearrange("p (t e) -> p t e", t=NT),
                                          ALU.mult, ALU.add))
            for k in range(top):
                step(dve.tensor_tensor(val, eq, oh[k], ALU.mult))
                step(dve.tensor_reduce(slotf, val, AX, ALU.add))
                step(dve.tensor_copy(m["slots"][:, k, :], slotf))
                dve.nop().then_inc(slots_ready, 1)
            step(dve.tensor_tensor(own_cmp, jx.unsqueeze(2).to_broadcast([P, tiles, E]),
                                   end.unsqueeze(1).to_broadcast([P, tiles, E]), ALU.is_ge))
            step(dve.tensor_reduce(own_f, own_cmp, AX, ALU.add))
            step(dve.tensor_scalar(own_f, own_f, float(E - 1), None, ALU.min))
            step(dve.tensor_copy(m["owner"][:, 0:tiles], own_f))
            if which == 1:
                for b in range(B):
                    dve.wait_ge(y_full, b + 1)
                    dve.tensor_tensor(tile2(x, b), tile2(x, b), ps[2 + b % 2][:, :], ALU.add).then_inc(y_added, 1)

        if which == 1:
            @block.scalar
            def _(act):
                act.wait_ge(m["r1_shifted"], 1)
                act.activation(val, val, ACT.Exp).then_inc(m["r1_exp"], 1)
                for b in range(B):
                    act.wait_ge(h_full, b + 1)
                    for i in range(KD):
                        ins = act.activation(shT[:, b, i, :], ps[2 + b % 2][:, i * S:(i + 1) * S], ACT.Relu,
                                             bias=sb1[:, i:i + 1])
                    ins.then_inc(h_ready, 1)
                for j in range(4):
                    act.wait_ge(cw_full, j + 1)
                    act.copy(cwT[:, 4 * j:4 * j + 4, :].rearrange("p t s -> p (t s)"), ps[4 + j][0:E1 + 1, :])\
                       .then_inc(cwT_ready, 1)

        @block.gpsimd
        def _(pool):
            pool.wait_ge(m["zero_fill"], 16 * 6)
            for k in range(top):
                pool.wait_ge(slots_ready, k + 1)
                for t in range(NT):
                    pool.indirect_dma_start(zs, bass.IndirectOffsetOnAxis(m["slots"][:, k, t:t + 1], 0),
                                            src[:, t * D:(t + 1) * D], None).then_inc(sent, 16)
            pool.wait_ge(sent, 16 * NT * top)



def moe(nc, a, m, which):
    E, HID, tiles = (E0, HID0, TILES0) if which == 0 else (E1, HID1, TILES1)
    MK = HID // P
    HB = (HID + 511) // 512
    HW = min(HID, 512)
    tag = f"m{which}_"
    cv = Carve(m["r"], m["RW"])
    zt = cv.take(P, U, D)
    zT = cv.take(P, 2, KD, P)
    hid = cv.take(P, 2, HID)
    hT = cv.take(P, 2, MK, P)
    y = cv.take(P, U, D)
    if which == 0:
        w1, w2 = m["w1"][:, 0:E * KD * HID], m["w2"][:, 0:E * MK * D]
    else:
        w1, w2 = m["w1"][:, 0:E * KD * HID], m["w1"][:, E * KD * HID:E * KD * HID + E * MK * D]
        b1T = cv.take(P, E, MK)
    sem = m["sem"]
    z_in = [sem(tag + f"z_in{i}") for i in range(U)]
    y_out = [sem(tag + f"y_out{i}") for i in range(U)]
    t_full, zT_ready, h_full, hid_ready, g_full, hT_ready, y_full, y_ready = (
        sem(tag + s) for s in ("t_full", "zT_ready", "h_full", "hid_ready", "g_full", "hT_ready", "y_full", "y_ready"))
    ps = m["psum"]
    t_ps, h_ps, g_ps, y_ps = ps[0], ps[1:3], ps[3:5], ps[5:7]
    zs, ys = m[f"zs{which}"], m[f"ys{which}"]


    def T(pe, j, u, behind):
        p = u % 2
        pe.wait_ge(z_in[u], 16 * ((j - u) // U) + 16 if isinstance(j, int) else j * (16 // U) + (16 - 16 // U * u))
        if behind:
            pe.wait_ge(zT_ready, j)
        for k in range(KD):
            ins = pe.transpose(t_ps[:, k * P:(k + 1) * P], zt[:, u, k * P:(k + 1) * P], m["ident"][:, :])
        ins.then_inc(t_full, 1)

    def owners(engine, j, n):
        return nc.values_load_multi_w_load_instructions(m["owner"][0:1, bass.ds(j, n)], engines=[engine],
                                                        min_val=0, max_val=E - 1)[1]

    def H(pe, j, u, behind, e):
        p = u % 2
        pe.wait_ge(zT_ready, j + 1)
        if behind:
            pe.wait_ge(hid_ready, j)
        for n in range(HB):
            for k in range(KD):
                ins = pe.matmul(h_ps[n][:, 0:HW], zT[:, p, k, :], w1[:, bass.ds(e * (KD * HID) + (k * HID + n * HW), HW)],
                                start=(k == 0), stop=(k == KD - 1))
        ins.then_inc(h_full, 1)

    def G(pe, j, u, behind):
        p = u % 2
        pe.wait_ge(hid_ready, j + 1)
        if behind:
            pe.wait_ge(hT_ready, j)
        for i in range(MK):
            ins = pe.transpose(g_ps[i // 4][:, i % 4 * P:(i % 4 + 1) * P], hid[:, p, i * P:(i + 1) * P], m["ident"][:, :])
        ins.then_inc(g_full, 1)

    def Y(pe, j, u, behind, e):
        p = u % 2
        pe.wait_ge(hT_ready, j + 1)
        if behind:
            pe.wait_ge(y_ready, j - 1)
        for i in range(MK):
            ins = pe.matmul(y_ps[p][:, 0:D], hT[:, p, i, :], w2[:, bass.ds(e * (MK * D) + i * D, D)],
                            start=(i == 0), stop=(i == MK - 1))
        ins.then_inc(y_full, 1)

    def act_T(act, j, u):
        p = u % 2
        act.wait_ge(t_full, j + 1)
        act.copy(zT[:, p, :, :].rearrange("p k s -> p (k s)"), t_ps[:, 0:KD * P]).then_inc(zT_ready, 1)

    def act_H(act, j, u):
        p = u % 2
        act.wait_ge(h_full, j + 1)
        for n in range(HB):
            ins = act.activation(hid[:, p, n * HW:(n + 1) * HW], h_ps[n][:, 0:HW],
                                 ACT.Gelu_apprx_tanh if which == 0 else ACT.Copy)
        ins.then_inc(hid_ready, 1)

    def dve_G(dve, j, u, e):
        p = u % 2
        dve.wait_ge(g_full, j + 1)
        if which == 0:
            for n in range(2):
                ins = dve.tensor_copy(hT[:, p, 4 * n:4 * n + 4, :].rearrange("p k s -> p (k s)"), g_ps[n][:, :])
        else:
            for i in range(MK):
                ins = dve.tensor_scalar(hT[:, p, i, :], g_ps[0][:, i * P:(i + 1) * P],
                                        b1T.rearrange("p e k -> p (e k)")[:, bass.ds(e * MK + i, 1)], 0.0,
                                        ALU.add, ALU.max)
        ins.then_inc(hT_ready, 1)

    def dve_Y(dve, j, u, behind):
        dve.wait_ge(y_full, j + 1)
        if behind:
            dve.wait_ge(y_out[u], (j - u) * (16 // U))
        dve.tensor_copy(y[:, u, :], y_ps[u % 2][:, 0:D]).then_inc(y_ready, 1)

    def load(sp, j, u):
        sp.dma_start(zt[:, u, :], zs[bass.ds(j * P, P), :]).then_inc(z_in[u], 16)

    def store(sp, j, u):
        sp.wait_ge(y_ready, j + 1)
        sp.dma_start(ys[bass.ds(j * P, P), :], y[:, u, :]).then_inc(y_out[u], 16)

    TURNS = (tiles - 3) // U
    AHEAD = U + 1

    def sp_step(sp, j, u, more):
        if more:
            sp.wait_ge(t_full, j + AHEAD - U + 1)
            load(sp, j + AHEAD, (u + AHEAD) % U)
        store(sp, j, u)

    def pe_step(pe, j, u, behind, e_h, e_y, left=4):
        if left > 3:
            T(pe, j + 3, (u + 3) % U, True)
        if left > 2:
            H(pe, j + 2, (u + 2) % U, True, e_h)
        if left > 1:
            G(pe, j + 1, (u + 1) % U, True)
        Y(pe, j, u, behind, e_y)

    def act_step(act, j, u, left=4):
        if left > 3:
            act_T(act, j + 3, (u + 3) % U)
        if left > 2:
            act_H(act, j + 2, (u + 2) % U)

    def dve_step(dve, j, u, behind, e, left=4):
        if left > 1:
            dve_G(dve, j + 1, (u + 1) % U, e)
        dve_Y(dve, j, u, behind)

    with nc.Block() as block:
        @block.sync
        def _(sp):
            if which == 1:
                sp.dma_start(b1T.rearrange("p e k -> p (e k)"), a["eb1T"]).then_inc(m["we_in"], 16)
            for j in range(U):
                load(sp, j, j)
            sp.wait_ge(t_full, 1)
            load(sp, U, 0)
            for j in range(U):
                sp_step(sp, j, j, True)
            with sp.Fori(1, TURNS - 1) as i:
                for u in range(U):
                    sp_step(sp, i * U + u, u, True)
            for j in range(U * (TURNS - 1), tiles):
                sp_step(sp, j, j % U, j + AHEAD < tiles)
            for u in range(U):
                sp.wait_ge(y_out[u], 16 * ((tiles + U - 1 - u) // U))

        @block.tensor
        def _(pe):
            if which == 0:
                pe.wait_ge(m["w1_in"], 16 * E0)
                pe.wait_ge(m["w2_in"], 16 * E0)
            else:
                pe.wait_ge(m["we_in"], 48)
            e = owners(mybir.EngineType.PE, 0, U + 2)
            T(pe, 0, 0, False)
            T(pe, 1, 1, True)
            H(pe, 0, 0, False, e[0])
            T(pe, 2, 2, True)
            H(pe, 1, 1, True, e[1])
            G(pe, 0, 0, False)
            for j in range(U):
                pe_step(pe, j, j, j >= 2, e[j + 2], e[j])
            with pe.Fori(1, TURNS) as i:
                e = owners(mybir.EngineType.PE, i * U, U + 2)
                for u in range(U):
                    pe_step(pe, i * U + u, u, True, e[u + 2], e[u])
            e = list(owners(mybir.EngineType.PE, U * TURNS, tiles - U * TURNS)) + 2 * [None]
            for j in range(U * TURNS, tiles):
                pe_step(pe, j, j % U, True, e[j + 2 - U * TURNS], e[j - U * TURNS], tiles - j)

        @block.scalar
        def _(act):
            act_T(act, 0, 0)
            act_T(act, 1, 1)
            act_H(act, 0, 0)
            act_T(act, 2, 2)
            act_H(act, 1, 1)
            with act.Fori(0, TURNS) as i:
                for u in range(U):
                    act_step(act, i * U + u, u)
            for j in range(U * TURNS, tiles):
                act_step(act, j, j % U, tiles - j)

        @block.vector
        def _(dve):
            if which == 1:
                dve.wait_ge(m["we_in"], 48)
            e = owners(mybir.EngineType.DVE, 0, U + 1)
            dve_G(dve, 0, 0, e[0])
            for j in range(U):
                dve_step(dve, j, j, False, e[j + 1])
            with dve.Fori(1, TURNS) as i:
                e = owners(mybir.EngineType.DVE, i * U, U + 1)
                for u in range(U):
                    dve_step(dve, i * U + u, u, True, e[u + 1])
            e = list(owners(mybir.EngineType.DVE, U * TURNS, tiles - U * TURNS)) + [None]
            for j in range(U * TURNS, tiles):
                dve_step(dve, j, j % U, True, e[j + 1 - U * TURNS], tiles - j)



def ffn1_buffers(m):
    cv = Carve(m["w2"], m["W1WORDS"])
    w = dict(sw1=cv.take(P, KD, D), sw2=cv.take(P, KD, D), sb1=cv.take(P, KD), x3T=cv.take(P, KD, B * S))
    w["carve"] = cv
    return w


ROW_GROUPS = ((0,), (1,), (2, 3), (4, 5, 6, 7))


def cross1(nc, a, m):
    w = ffn1_buffers(m)
    sw1, sw2, sb1, x3T, cv = w["sw1"], w["sw2"], w["sb1"], w["x3T"], w["carve"]
    got = Carve(m["r"], m["RW"]).take(P, NT, D)
    wq, wk, wv = cv.take(P, KD, D), cv.take(CP, KC, D), cv.take(CP, KC, D)
    rw, bqk, bqs, bv, rb = cv.take(P, KD, E1), cv.take(P, 2, KD), cv.take(P, KD), cv.take(P, D), cv.take(P, E1)
    ctxT, xn, xnT, n3 = cv.take(CP, 2, KC, S), cv.take(P, QT, D), cv.take(P, KD, S), cv.take(P, QT, D)
    qT, kT, v = cv.take(P, KD, S), cv.take(P, KD, S), cv.take(P, QT, D + 1)
    p, pT, x3_now = cv.take(P, QT, S), cv.take(P, QT, S), cv.take(P, KD, S)
    nmax, rec, spare, pool_spare = cv.take(P, QT), cv.take(P, QT), cv.take(P, 1), cv.take(P, 1)
    ln = [ln_buffers(m, cv, f"c1_ln{i}_") for i in range(2)]
    sem = m["sem"]
    (kvq_job, att_job, ffn_job, kvq_act, att_act, ffn_act, kvq_dve, att_max, rec_ready, x3_ready, ffn_dve, xn_ready,
     n3_ready, z_kept, ones_set, w_in) = (sem("c1_" + s) for s in (
         "kvq_job", "att_job", "ffn_job", "kvq_act", "att_act", "ffn_act", "kvq_dve", "att_max", "rec_ready", "x3_ready",
         "ffn_dve", "xn_ready", "n3_ready", "z_kept", "ones_set", "w_in"))
    ctx_in = [sem(f"c1_ctx_in{i}") for i in range(2)]
    row_in, x2_ready = [sem(f"c1_row_in{i}") for i in range(4)], sem("c1_x2_ready")
    m["r1_shifted"], m["r1_exp"] = sem("r1_shifted"), sem("r1_exp")
    ps, ident, x, z = m["psum"], m["ident"], m["x"], m["z"]
    s_ps, pt_ps, o_ps, kq_ps, vl_ps, xy_ps, xh_ps = ps[0], ps[1], ps[2:4], ps[4], ps[5], ps[6], ps[7]
    lg = m["logits"][:, 0:NT * E1]

    def transposes(pe, bank, src):
        for k in range(KD):
            for q in range(QT):
                ins = pe.transpose(bank[:, k * S + q * P:k * S + (q + 1) * P], src[:, q, k * P:(k + 1) * P], ident[:, :])
        return ins

    def product(pe, bank, width, lhsT, rhs, n):
        for i in range(2):
            for k in range(n):
                ins = pe.matmul(bank[:, i * width:(i + 1) * width], lhsT(i, k), rhs(i, k), start=(k == 0), stop=(k == n - 1))
        return ins

    def tile(t, i):
        return t[:, i * P:(i + 1) * P]

    def pe_turn(pe, b, par, first, second, third):
        f, t = b + 1, b - 1
        cx = ctxT[:, 1 - par]
        if second:
            ge(pe, kvq_act, 3 * b + 3)
            ge(pe, att_act, 2 * b - 1)
            product(pe, s_ps, S, lambda q, k: tile(qT[:, k], q), lambda q, k: kT[:, k, :], KD).then_inc(att_job, 1)
        if first:
            ge(pe, ctx_in[1 - par], 16 * ((f - (1 - par)) // 2) + 16 if isinstance(f, int) else 8 * (f - (1 - par)) + 16)
            ge(pe, kvq_act, 3 * f)
            product(pe, kq_ps, S, lambda i, k: tile(wk[:, k], i), lambda i, k: cx[:, k, :], KC).then_inc(kvq_job, 1)
        if third:
            ge(pe, n3_ready, t + 1)
            ge(pe, ffn_act, 2 * t)
            transposes(pe, xh_ps, n3).then_inc(ffn_job, 1)
        if second:
            ge(pe, att_act, 2 * b + 1)
            transposes(pe, pt_ps, p).then_inc(att_job, 1)
        if third:
            ge(pe, ffn_act, 2 * t + 1)
            ge(pe, kvq_dve, b + 1 if second else b)
            product(pe, vl_ps, E1, lambda q, k: tile(x3_now[:, k], q),
                    lambda q, k: rw[:, k, :], KD).then_inc(ffn_job, 1)
        if first:
            ge(pe, xn_ready, f + 1)
            ge(pe, kvq_act, 3 * f - 1)
            transposes(pe, xy_ps, xn).then_inc(kvq_job, 1)
        if second:
            ge(pe, att_act, 2 * b + 2)
            ge(pe, kvq_dve, b + 1)
            ge(pe, x3_ready, b)
            for q in range(QT):
                for kt in range(QT):
                    ins = pe.matmul(o_ps[q][:, 0:D + 1], tile(pT[:, kt], q), v[:, kt, :], start=(kt == 0), stop=(kt == QT - 1))
            ins.then_inc(att_job, 1)
        if first:
            ge(pe, ffn_dve, b)
            product(pe, vl_ps, D, lambda q, k: tile(cx[:, k], q), lambda q, k: wv[:, k, :], KC).then_inc(kvq_job, 1)
            ge(pe, kvq_act, 3 * f + 2)
            product(pe, kq_ps, S, lambda i, k: tile(wq[:, k], i), lambda i, k: xnT[:, k, :], KD).then_inc(kvq_job, 1)

    def act_turn(act, b, par, first, second, third):
        f, t = b + 1, b - 1
        if second:
            ge(act, att_max, b + 1)
            ge(act, att_job, 3 * b - 1)
            for q in range(QT):
                ins = act.activation(p[:, q, :], s_ps[:, q * S:(q + 1) * S], ACT.Exp, bias=nmax[:, q:q + 1])
            ins.then_inc(att_act, 1)
        if first:
            ge(act, kvq_job, 4 * f + 1)
            for i in range(KD):
                ins = act.activation(kT[:, i, :], kq_ps[:, i * S:(i + 1) * S], ACT.Identity, bias=bqk[:, 1, i:i + 1])
            ins.then_inc(kvq_act, 1)
        if third:
            ge(act, ffn_job, 2 * t + 1)
            act.copy(x3_now.rearrange("p k s -> p (k s)"), xh_ps[:, :]).then_inc(ffn_act, 1)
        if second:
            ge(act, att_job, 3 * b + 2)
            act.copy(pT.rearrange("p k s -> p (k s)"), pt_ps[:, :]).then_inc(att_act, 1)
        if third:
            act.copy(x3T[:, :, bass.ds(t * S, S)], xh_ps[:, :].rearrange("p (k s) -> p k s", k=KD)).then_inc(ffn_act, 1)
        if first:
            ge(act, kvq_job, 4 * f + 2)
            act.copy(xnT.rearrange("p k s -> p (k s)"), xy_ps[:, :]).then_inc(kvq_act, 1)
            ge(act, kvq_job, 4 * f + 4)
            for i in range(KD):
                ins = act.activation(qT[:, i, :], kq_ps[:, i * S:(i + 1) * S], ACT.Identity, bias=bqs[:, i:i + 1],
                                     scale=D ** -0.5)
            ins.then_inc(kvq_act, 1)

    def dve_turn(dve, b, par, first, second, third):
        f, t = b + 1, b - 1
        if second:
            ge(dve, att_job, 3 * b + 1)
            dve.tensor_reduce(nmax, s_ps[:, :].rearrange("p (q k) -> p q k", q=QT), AX, ALU.max, negate=True)\
               .then_inc(att_max, 1)
        if first:
            for i, group in enumerate(ROW_GROUPS):
                if f == group[0] if isinstance(f, int) else i == len(ROW_GROUPS) - 1:
                    ge(dve, row_in[i], 16 * QT * len(group))
            dve.tensor_tensor(tile2(x, f), tile2(x, f), got[:, bass.ds(f * QT, QT), :].rearrange("p q d -> p (q d)"),
                              ALU.add).then_inc(x2_ready, 1)
            ge(dve, x2_ready, f + 1)
            dve.memset(spare, 0.0)
            ln_stats(dve, ln[0], lambda q: tile1(x, f, q), f)
            ln_variance(dve, ln[0], f)
            ge(dve, kvq_job, 4 * f - 2)
            ln_apply(dve, ln[0], lambda q: tile1(x, f, q), lambda q: xn[:, q, :], f).then_inc(xn_ready, 1)
        if third:
            ge(dve, ffn_job, 2 * t + 2)
            dve.tensor_tensor(lg[:, bass.ds(t * (QT * E1), QT * E1)].rearrange("p (q e) -> p q e", q=QT),
                              vl_ps[:, 0:QT * E1].rearrange("p (q e) -> p q e", q=QT),
                              rb.unsqueeze(1).to_broadcast([P, QT, E1]), ALU.add).then_inc(ffn_dve, 1)
        if second:
            ge(dve, att_job, 3 * b + 3)
            for q in range(QT):
                ins = dve.reciprocal(rec[:, q:q + 1], o_ps[q][:, D:D + 1])
            ins.then_inc(rec_ready, 1)
            ge(dve, rec_ready, b + 1)
            for q in range(QT):
                ins = dve.scalar_tensor_tensor(tile1(x, b, q), o_ps[q][:, 0:D], rec[:, q:q + 1], tile1(x, b, q),
                                               ALU.mult, ALU.add)
            ins.then_inc(x3_ready, 1)
            ge(dve, x3_ready, b + 1)
            dve.memset(spare, 0.0)
            ln_stats(dve, ln[1], lambda q: tile1(x, b, q), b)
            ln_variance(dve, ln[1], b)
        if first:
            ge(dve, kvq_job, 4 * f + 3)
            dve.tensor_tensor(v[:, :, 0:D], vl_ps[:, :].rearrange("p (q d) -> p q d", q=QT),
                              bv.unsqueeze(1).to_broadcast([P, QT, D]), ALU.add).then_inc(kvq_dve, 1)
        if second:
            ge(dve, z_kept, b)
            ge(dve, ffn_job, 2 * b - 1)
            ln_apply(dve, ln[1], lambda q: tile1(x, b, q), lambda q: n3[:, q, :], b).then_inc(n3_ready, 1)

    def pool_turn(pool, b, par, first, second, third):
        if first:
            ln_power(pool, ln[0], b + 1)
        if second:
            ln_power(pool, ln[1], b)
            ge(pool, n3_ready, b + 1)
            pool.tensor_tensor(pool_spare, m["power"][:, 0:1], m["power"][:, 0:1], ALU.mult)
            pool.tensor_copy(tile2(z, b), n3.rearrange("p q d -> p (q d)")).then_inc(z_kept, 1)

    def turns(eng, turn):
        turn(eng, -1, 1, True, False, False)
        turn(eng, 0, 0, True, True, False)
        turn(eng, 1, 1, True, True, True)
        turn(eng, 2, 0, True, True, True)
        with eng.Fori(1, B // 2 - 1) as i:
            turn(eng, i * 2 + 1, 1, True, True, True)
            turn(eng, i * 2 + 2, 0, True, True, True)
        turn(eng, B - 1, 1, False, True, True)
        turn(eng, B, 0, False, False, True)

    with nc.Block() as block:
        @block.sync
        def _(sp):
            for dst, name in ((wk, "wk1"), (wv, "wv1"), (wq, "wq1"), (bqk, "bqk1"), (sw1, "sw1"), (sw2, "sw2"), (rw, "rw"),
                              (sb1, "sb1")):
                sp.dma_start(dst, a[name]).then_inc(w_in, 16)
            sp.dma_start(bv, a["bv1"].partition_broadcast(P)).then_inc(w_in, 16)
            sp.dma_start(rb, a["rb"].partition_broadcast(P)).then_inc(w_in, 16)
            for f in range(2):
                sp.dma_start(ctxT[:, f], a["ctxT"][f]).then_inc(ctx_in[f], 16)
            n = E1 * KD * HID1
            sp.dma_start(m["w1"][:, 0:n], a["ew1"]).then_inc(m["we_in"], 16)
            sp.dma_start(m["w1"][:, n:2 * n], a["ew2"]).then_inc(m["we_in"], 16)
            with sp.Fori(0, B // 2 - 1) as i:
                for par in range(2):
                    sp.wait_ge(kvq_job, i * 8 + (4 * par + 3))
                    sp.dma_start(ctxT[:, par], a["ctxT"][bass.ds(i * 2 + (par + 2), 1)].rearrange("o p k s -> (o p) k s"))\
                      .then_inc(ctx_in[par], 16)

        @block.gpsimd
        def _(pool):
            pool.memset(v[:, :, D:D + 1], 1.0).then_inc(ones_set, 1)
            for i, group in enumerate(ROW_GROUPS):
                for t in range(group[0] * QT, (group[-1] + 1) * QT):
                    pool.indirect_dma_start(got[:, t, :], None, m["ys0"],
                                            bass.IndirectOffsetOnAxis(m["slots"][:, 0, t:t + 1], 0)).then_inc(row_in[i], 16)
            turns(pool, pool_turn)

        @block.tensor
        def _(pe):
            pe.wait_ge(w_in, 160)
            pe.wait_ge(ones_set, 2)
            turns(pe, pe_turn)

        @block.scalar
        def _(act):
            act.wait_ge(w_in, 160)
            act.mul(bqs, bqk[:, 0, :], D ** -0.5).then_inc(ones_set, 1)
            turns(act, act_turn)

        @block.vector
        def _(dve):
            dve.wait_ge(w_in, 160)
            turns(dve, dve_turn)


def join1(nc, a, m, out):
    got = Carve(m["w2"], m["W1WORDS"]).take(P, TOP1, NT, D)
    sem = m["sem"]
    groups = [range(0, 6), range(6, 10), range(10, 14), range(14, NT)]
    row_in, joined, stored = [sem(f"j1_row_in{i}") for i in range(len(groups))], sem("j1_joined"), sem("j1_stored")
    x = m["x"]
    with nc.Block() as block:
        @block.sync
        def _(sp):
            for b in range(B):
                sp.wait_ge(joined, (QT * TOP1) * (b + 1))
                sp.dma_start(out[:, b * QT * D:(b + 1) * QT * D], tile2(x, b)).then_inc(stored, 16)
            sp.wait_ge(stored, 16 * B)

        @block.gpsimd
        def _(pool):
            for i, group in enumerate(groups):
                for t in group:
                    for k in range(TOP1):
                        pool.indirect_dma_start(got[:, k, t, :], None, m["ys1"],
                                                bass.IndirectOffsetOnAxis(m["slots"][:, k, t:t + 1], 0)).then_inc(row_in[i], 16)

        @block.vector
        def _(dve):
            for i, group in enumerate(groups):
                dve.wait_ge(row_in[i], 16 * TOP1 * len(group))
                for t0 in range(group[0], group[-1] + 1, QT):
                    for k in range(TOP1):
                        tiles = [t for t in (t0, t0 + 1) if t in group]
                        for t in tiles:
                            if k:
                                dve.wait_ge(joined, TOP1 * t0 + len(tiles) * (k - 1) + (t - t0) + 1)
                            dve.scalar_tensor_tensor(x[:, t * D:(t + 1) * D], got[:, k, t, :], m["top_p"][:, k, t:t + 1],
                                                     x[:, t * D:(t + 1) * D], ALU.mult, ALU.add).then_inc(joined, 1)



def kernel(**inputs):
    import numpy as np
    import concourse.bacc as bacc
    from concourse import mybir as mb
    from concourse.bass_utils import run_bass_kernel_spmd as run
    import ml_dtypes

    x = {k: np.asarray(v) for k, v in inputs.items()}

    def part(w, p=P):
        return np.ascontiguousarray(w.reshape(w.shape[0] // p, p, -1).transpose(1, 0, 2))

    def cols(v):
        return np.ascontiguousarray(v.reshape(-1, P).T)

    def spread_heads(w):
        return part(w.reshape(D, 2, H1 // 2, DH1).transpose(0, 1, 3, 2).reshape(D, D))

    qkv = x["L0_ffn_w_qkv"]
    arrays = {
        "x": part(x["x"].reshape(B * S, D)).reshape(P, NT * D),
        "ctxT": np.ascontiguousarray(x["ctx_768"].reshape(B, S, KC, CP).transpose(0, 3, 2, 1)),
        "wq0": part(x["L0_xattn_Wq"]), "wk0": part(x["L0_xattn_Wk"], CP), "wv0": part(x["L0_xattn_Wv"], CP),
        "wo0": part(x["L0_xattn_Wo"]), "bo0": x["L0_xattn_bo"],
        "s_wq": spread_heads(qkv[:, 0:D]), "s_wk": spread_heads(qkv[:, D:2 * D]), "s_wv": part(qkv[:, 2 * D:]),
        "s_wp": part(x["L0_ffn_w_proj"]),
        "s_ln1": np.ascontiguousarray(np.stack([cols(x["L0_ffn_ln1_w"]), cols(x["L0_ffn_ln1_b"])], axis=1)),
        "s_ln2": np.ascontiguousarray(np.stack([cols(x["L0_ffn_ln2_w"]), cols(x["L0_ffn_ln2_b"])], axis=1)),
        "s_ln2w": x["L0_ffn_ln2_w"], "s_ln2b": x["L0_ffn_ln2_b"],
        "s_gw": part(x["L0_ffn_gate_w"]), "s_gb": x["L0_ffn_gate_b"],
        "w1": np.stack([part(w).reshape(P, -1) for w in x["L0_ffn_w1"]]),
        "w2": np.stack([part(w).reshape(P, -1) for w in x["L0_ffn_w2"]]),
        "wq1": part(x["L1_xattn_Wq"]), "wk1": part(x["L1_xattn_Wk"], CP), "wv1": part(x["L1_xattn_Wv"], CP),
        "bqk1": np.ascontiguousarray(np.stack([cols(x["L1_xattn_bq"]), cols(x["L1_xattn_bk"])], axis=1)),
        "bv1": x["L1_xattn_bv"], "rw": part(x["L1_ffn_router_W"]), "rb": x["L1_ffn_router_b"],
        "sw1": part(x["L1_ffn_sW1"]), "sw2": part(x["L1_ffn_sW2"]), "sb1": cols(x["L1_ffn_sb1"]),
        "ew1": np.ascontiguousarray(np.stack([part(w).reshape(P, -1) for w in x["L1_ffn_eW1"]], axis=1)).reshape(P, -1),
        "ew2": np.ascontiguousarray(np.stack([part(w).reshape(P, -1) for w in x["L1_ffn_eW2"]], axis=1)).reshape(P, -1),
        "eb1T": np.ascontiguousarray(x["L1_ffn_eb1"].reshape(E1 * M1, P).T),
        "b2": np.ascontiguousarray(np.concatenate([x["L1_ffn_eb2"], x["L1_ffn_sb2"][None]], axis=0)),
        "ident": np.eye(P, dtype=np.float32),
        "upper": np.triu(np.ones((P, P)), 1).astype(ml_dtypes.bfloat16),
        "ones": np.ones((P, P)).astype(ml_dtypes.bfloat16),
    }
    for i, (e, tiles) in enumerate(((E0, TILES0), (E1, TILES1))):
        arrays[f"incl{i}"] = np.tril(np.ones((e, e), np.float32)).reshape(-1)
        arrays[f"rank{i}"] = (e - np.arange(e)).astype(np.float32)
        arrays[f"steps{i}"] = (P * np.arange(NC)).astype(np.float32)
        arrays[f"jx{i}"] = np.arange(tiles).astype(np.float32)

    nc = bacc.Bacc("TRN2", target_bir_lowering=False, num_devices=1)
    args = {k: nc.dram_tensor("in_" + k, v.shape, mb.dt.from_np(v.dtype), kind="ExternalInput").ap()
            for k, v in arrays.items()}
    out = nc.dram_tensor("out", (P, NT * D), mb.dt.float32, kind="ExternalOutput").ap()
    build(nc, args, out)
    r = run(nc, [{"in_" + k: v for k, v in arrays.items()}], core_ids=[0])
    got = np.asarray(r.results[0]["out"])
    return np.ascontiguousarray(got.reshape(P, NT, D).transpose(1, 0, 2)).reshape(B, S, D)
```

```python
from contextlib import ExitStack

import concourse.bass as bass
from concourse import mybir

F32 = mybir.dt.float32
BF16 = mybir.dt.bfloat16
F16 = mybir.dt.float16
I32 = mybir.dt.int32
ALU = mybir.AluOpType
ACT = mybir.ActivationFunctionType
AX = mybir.AxisListType.X

P = 128
B, S, D = 8, 256, 256
NT = B * S // P
QT = S // P
KD = D // P
CP, KC = 96, 2
H0, DH0 = 8, 64
H1, DH1 = 16, 16
EPS = 1e-5
E0, HID0 = 8, 1024
M0 = HID0 // P
E1, HID1, TOP1 = 15, 256, 3
M1 = HID1 // P
TILES0 = (NT * P + E0 * (P - 1)) // P
TILES1 = (TOP1 * NT * P + E1 * (P - 1)) // P
MOE_WORDS = 7200
U = 4
NC = 16


class Chain:

    def __init__(self, eng, sem, base):
        self.eng, self.sem, self.base, self.k = eng, sem, base, 0

    def done(self, ins):
        self.k += 1
        ins.then_inc(self.sem, 1)

    def wait(self):
        self.eng.wait_ge(self.sem, self.base + self.k)


def ge(eng, sem, value):
    if not isinstance(value, int) or value > 0:
        eng.wait_ge(sem, value)


class Carve:

    def __init__(self, region, words):
        self.region, self.words, self.at = region, words, 0

    def take(self, parts, *shape, dt=F32):
        n = 1
        for s in shape:
            n *= s
        w = n if dt in (F32, I32) else (n + 1) // 2
        v = self.region[0:parts, self.at:self.at + w]
        self.at += (w + 7) // 8 * 8
        assert self.at <= self.words, (self.at, self.words)
        if dt != F32:
            v = v.bitcast(dt)
        names = "abcd"[:len(shape)]
        if len(shape) > 1:
            v = v.rearrange("p (" + " ".join(names) + ") -> p " + " ".join(names), **dict(zip(names, shape)))
        return v


def tile2(t, b):
    return t[:, bass.ds(b * (QT * D), QT * D)]


def tile1(t, b, q):
    return t[:, bass.ds(b * (QT * D) + q * D, D)]



def ln_stats(dve, ln, src, nth):
    for q in range(QT):
        dve.bn_stats(ln["stats"][:, q, :], src(q)).then_inc(ln["own"], 1)


def ln_variance(dve, ln, nth):
    dve.wait_ge(ln["own"], nth * 4 + 2)
    dve.memset(ln["spare"], 0.0)
    for q in range(QT):
        dve.bn_aggr(ln["mv"][:, q, :], ln["stats"][:, q, :]).then_inc(ln["own"], 1)
    dve.wait_ge(ln["own"], nth * 4 + 4)
    dve.tensor_scalar(ln["var"], ln["mv"][:, :, 1], EPS, None, ALU.add).then_inc(ln["var_ready"], 1)


def ln_apply(dve, ln, src, dst, nth):
    dve.wait_ge(ln["rstd_ready"], nth + 1)
    for q in range(QT):
        ins = dve.tensor_scalar(dst(q), src(q), ln["mv"][:, q, 0:1], ln["rstd"][:, q:q + 1], ALU.subtract, ALU.mult)
    return ins


def ln_buffers(m, cv, tag):
    return dict(stats=cv.take(P, QT, 6), mv=cv.take(P, QT, 2), var=cv.take(P, QT), rstd=cv.take(P, QT),
                spare=cv.take(P, 1), power=m["power"][:, :], own=m["sem"](tag + "ln_own"),
                var_ready=m["sem"](tag + "var_ready"), rstd_ready=m["sem"](tag + "rstd_ready"))


def ln_power(pool, ln, nth):
    pool.wait_ge(ln["var_ready"], nth + 1)
    pool.tensor_tensor(ln["rstd"], ln["var"], ln["power"], ALU.pow).then_inc(ln["rstd_ready"], 1)


def build(nc, a, out):
    ctx = ExitStack()
    with ctx:
        def sb(name, shape, dt=F32):
            return ctx.enter_context(nc.sbuf_tensor(name, shape, dt))

        def sem(name):
            return ctx.enter_context(nc.semaphore(name))

        def scratch(name, shape):
            return nc.dram_tensor(name, shape, F32, kind="Internal").ap()

        m = {}
        m["x"] = sb("x_all", [P, NT * D])
        m["z"] = sb("z_all", [P, NT * D])
        W1WORDS = E0 * KD * HID0
        m["w1"] = sb("w1_all", [P, W1WORDS])
        m["w2"] = sb("w2_all", [P, W1WORDS])
        RW = 10580
        m["r"] = sb("r_all", [P, RW])
        m["RW"], m["W1WORDS"] = RW, W1WORDS
        m["ident"] = sb("ident", [P, P])
        m["power"] = sb("power", [P, QT])
        m["upper"] = sb("upper", [P, P], BF16)
        m["ones"] = sb("ones", [P, P], BF16)
        m["oh_bf"] = sb("oh_bf", [P, NT * E1], BF16)
        m["logits"] = sb("logits", [P, NT * 16])
        m["slots"] = sb("slots", [P, TOP1, NT], I32)
        m["owner"] = sb("owner", [P, 64], I32)
        m["top_p"] = sb("top_p", [P, TOP1, NT])
        m["cw"] = sb("cw", [P, NT, E1 + 1])
        m["route"] = []
        for i, (e, tiles) in enumerate(((E0, TILES0), (E1, TILES1))):
            m["route"].append([sb(f"route{i}_{name}", [P, n]) for name, n in (
                ("incl", e * e), ("rank", e), ("steps", NC), ("jx", tiles))])
        m["psum"] = [ctx.enter_context(nc.psum_tensor(f"bank{i}", [P, 512], F32)) for i in range(8)]
        m["q_parts"] = nc.dram_tensor("q_parts", [2, 3, DH1, H1 // 2, 2 * S], BF16, kind="Internal").ap()
        m["k_parts"] = nc.dram_tensor("k_parts", [2, 6, DH1, H1 // 2, 2 * S], BF16, kind="Internal").ap()
        m["zs0"] = scratch("zs0", [TILES0 * P, D])
        m["ys0"] = scratch("ys0", [TILES0 * P, D])
        m["zs1"] = scratch("zs1", [TILES1 * P, D])
        m["ys1"] = scratch("ys1", [TILES1 * P, D])
        for s in ("const_in", "w1_in", "w2_in", "w_self_in", "zero_fill", "we_in", "route_in"):
            m[s] = sem(s)
        m["c1_w_in"], m["c1_ctx_in"] = sem("c1_w_in"), [sem(f"c1_ctx_in{i}") for i in range(2)]
        m["sem"] = sem
        cross0(nc, a, m)
        self0(nc, a, m)
        route(nc, a, m, 0)
        moe(nc, a, m, 0)
        cross1(nc, a, m)
        route(nc, a, m, 1)
        moe(nc, a, m, 1)
        join1(nc, a, m, out)



def cross0(nc, a, m):
    cv, cr = Carve(m["w2"], m["W1WORDS"]), self0_weights(m)["carve"]
    n, W, FT = H0, DH0 + 1, H0 * DH0 // P
    wq, wo, bo = cv.take(P, KD, n * DH0), cv.take(P, FT, D), cv.take(P, D)
    wk, wv, ctxT = cv.take(CP, KC, n * DH0), cv.take(CP, KC, n * DH0), cv.take(CP, 2, KC, S)
    xn, xnT, qT, kT = cv.take(P, QT, D), cv.take(P, KD, S), cv.take(P, FT, S), cv.take(P, 2, FT, S)
    att, attT = cv.take(P, QT, n * DH0), cv.take(P, FT, S)
    p = cv.take(P, 2, QT, S)
    pT = cr.take(P, 2, QT * S)
    p1 = pT.rearrange("p s n -> p (s n)").bitcast(BF16).rearrange("p (s k n two) -> p s k n two", s=2, k=QT, two=2)
    p2 = cr.take(P, 2, QT * S, dt=F16)
    v1, v2 = cr.take(P, 2, QT * n, W, dt=BF16), cr.take(P, 2, QT * n, W, dt=F16)
    nmax, rec, spare = cr.take(P, 2, QT), cr.take(P, 2, QT * 2), cr.take(P, 1)
    ln = ln_buffers(m, cr, "c0_")
    sem = m["sem"]
    (s_full, max_done, exp_done, pt_full, pt_ev, p2_done, o_done, att_done, rec_ready, f_job, f_act, f_dve, t_job,
     t_dve, xn_ready, bo_added, start, kv_in, q_in, wo_in) = (sem("c0_" + s) for s in (
         "s_full", "max_done", "exp_done", "pt_full", "pt_ev", "p2_done", "o_done", "att_done", "rec_ready", "f_job",
         "f_act", "f_dve", "t_job", "t_dve", "xn_ready", "bo_added", "start", "kv_in", "q_in", "wo_in"))
    x_in = [sem(f"c0_x_in{i}") for i in range(2)]
    ctx_in = [sem(f"c0_ctx_in{i}") for i in range(2)]
    ps, x, ident = m["psum"], m["x"], m["ident"]
    s_ps, pt_ps, o_ps, f_ps, t_ps = ps[0:2], ps[2], ps[3:5], ps[5:7], ps[7]
    NF, NTL = 7, 3

    def transposes(pe, bank, src):
        for k in range(2):
            for q in range(QT):
                ins = pe.transpose(bank[:, k * S + q * P:k * S + (q + 1) * P], src(k, q), ident[:, :])
        return ins

    def project(pe, bank, w, kn, mt, xT):
        for i in range(2):
            for k in range(kn):
                ins = pe.matmul(bank[:, i * S:(i + 1) * S], w[:, k, (mt + i) * P:(mt + i + 1) * P], xT[:, k, :],
                                start=(k == 0), stop=(k == kn - 1))
        return ins

    def pe_S(pe, b, par, h):
        if h % 4 == 0:
            ge(pe, f_act, NF * b + 6 + h // 4)
        ge(pe, exp_done, n * b + h - 1)
        lo, mt = DH0 * (h % 2), h // 2
        for q in range(QT):
            ins = pe.matmul(s_ps[h % 2][:, q * S:(q + 1) * S], qT[lo:lo + DH0, mt, q * P:(q + 1) * P],
                            kT[lo:lo + DH0, par, mt, :], start=True, stop=True)
        ins.then_inc(s_full, 1)

    def pe_T(pe, b, h):
        ge(pe, exp_done, n * b + h + 1)
        ge(pe, pt_ev, n * b + h)
        transposes(pe, pt_ps, lambda kt, q: p[:, h % 2, q, kt * P:(kt + 1) * P]).then_inc(pt_full, 1)

    def pe_PV(pe, b, par, h):
        if h == 0:
            ge(pe, f_act, NF * b + 4)
            ge(pe, f_dve, 2 * b + 2)
        if h % 2 == 0:
            ge(pe, att_done, (n // 2) * b + h // 2 - 1)
        ge(pe, p2_done, n * b + h + 1)
        for q in range(QT):
            c = (q * 2 + h % 2) * W
            k = 0
            for kt in range(QT):
                for lhsT in (p1[:, h % 2, kt, q * P:(q + 1) * P, 1], p2[:, h % 2, kt * S + q * P:kt * S + (q + 1) * P]):
                    for v in (v1, v2):
                        ins = pe.matmul(o_ps[h // 2 % 2][:, c:c + W], lhsT, v[:, par, kt * n + h, :],
                                        start=(k == 0), stop=(k == 4 * QT - 1))
                        k += 1
        ins.then_inc(o_done, 1)

    def pe_side(pe, s, b, par, front, tail):
        f, t = b + 1, b - 1
        cx = ctxT[:, 1 - par]
        if front and s == 0:
            ge(pe, ctx_in[1 - par], 16 * ((f - (1 - par)) // 2) + 16 if isinstance(f, int) else 8 * (f - (1 - par)) + 16)
            ge(pe, f_act, NF * f)
            project(pe, f_ps[0], wk, KC, 0, cx).then_inc(f_job, 1)
        if front and s == 1:
            project(pe, f_ps[1], wk, KC, 2, cx).then_inc(f_job, 1)
        if front and s in (2, 3):
            ge(pe, f_act, NF * f + s - 1)
            for k in range(KC):
                ins = pe.matmul(f_ps[s - 2][:, :], cx[:, k, (s - 2) * P:(s - 1) * P], wv[:, k, :],
                                start=(k == 0), stop=(k == KC - 1))
            ins.then_inc(f_job, 1)
        if front and s == 5:
            if isinstance(b, int) and b < 0:
                ge(pe, q_in, 32)
            ge(pe, xn_ready, f + 1)
            ge(pe, f_act, NF * f + 3)
            ge(pe, f_dve, 2 * f + 1)
            transposes(pe, f_ps[0], lambda k, q: xn[:, q, k * P:(k + 1) * P]).then_inc(f_job, 1)
        if front and s in (6, 7):
            ge(pe, f_act, NF * f + 5)
            ge(pe, f_dve, 2 * f + 2)
            project(pe, f_ps[7 - s], wq, KD, 2 * (s - 6), xnT).then_inc(f_job, 1)
        if tail and s in (0, 2):
            ge(pe, att_done, (n // 2) * t + 2 + s)
            ge(pe, t_dve, NTL * t + s // 2)
            transposes(pe, t_ps, lambda k, q: att[:, q, (s + k) * P:(s + k + 1) * P]).then_inc(t_job, 1)
        if tail and s in (4, 5):
            if s == 4:
                if isinstance(t, int) and t == 0:
                    ge(pe, wo_in, 32)
                ge(pe, t_dve, NTL * t + 2)
            q = s - 4
            for k in range(FT):
                ins = pe.matmul(t_ps[:, q * D:(q + 1) * D], attT[:, k, q * P:(q + 1) * P], wo[:, k, :],
                                start=(k == 0), stop=(k == FT - 1))
            if s == 5:
                ins.then_inc(t_job, 1)

    def pe_turn(pe, b, par, front, heads, tail):
        for s in range(n):
            if heads:
                pe_S(pe, b, par, s)
            if s == 0 and tail:
                pe_T(pe, b - 1, n - 1)
            if s > 0 and heads:
                pe_T(pe, b, s - 1)
            if s < 2 and tail:
                pe_PV(pe, b - 1, 1 - par, n + s - 2)
            if s >= 2 and heads:
                pe_PV(pe, b, par, s - 2)
            pe_side(pe, s, b, par, front, tail)

    def act_E(act, b, h):
        ge(act, max_done, n * b + h + 1)
        ge(act, pt_full, n * b + h - 1)
        for q in range(QT):
            ins = act.activation(p[:, h % 2, q, :], s_ps[h % 2][:, q * S:(q + 1) * S], ACT.Exp,
                                 bias=nmax[:, h % 2, q:q + 1])
        ins.then_inc(exp_done, 1)

    def act_C(act, b, h):
        ge(act, pt_full, n * b + h + 1)
        ge(act, o_done, n * b + h - 1)
        act.copy(pT[:, h % 2, :], pt_ps[:, :]).then_inc(pt_ev, 1)

    def flat(t):
        return t.rearrange("p k s -> p (k s)")

    def act_side(act, s, b, par, front, heads):
        f = b + 1
        if heads and s == 0:
            ge(act, f_job, NF * b + 7)
            act.mul(flat(qT[:, 2:4, :]), f_ps[0][:, :], DH0 ** -0.5).then_inc(f_act, 1)
        if front and s in (1, 2):
            ge(act, f_job, NF * f + s)
            act.copy(flat(kT[:, 1 - par, 2 * (s - 1):2 * s, :]), f_ps[s - 1][:, :]).then_inc(f_act, 1)
        if front and s in (3, 4):
            ge(act, f_job, NF * f + s)
            act.copy(v1[:, 1 - par, (s - 3) * n:(s - 2) * n, 0:DH0],
                     f_ps[s - 3][:, :].rearrange("p (h w) -> p h w", h=n)).then_inc(f_act, 1)
        if front and s == 5:
            ge(act, f_job, NF * f + 5)
            act.copy(flat(xnT), f_ps[0][:, :]).then_inc(f_act, 1)
        if front and s == 7:
            ge(act, f_job, NF * f + 6)
            act.mul(flat(qT[:, 0:2, :]), f_ps[1][:, :], DH0 ** -0.5).then_inc(f_act, 1)

    def act_turn(act, b, par, front, heads, tail):
        for s in range(n):
            act_side(act, s, b, par, front, heads) if s < 5 else None
            if s == 0 and tail:
                act_C(act, b - 1, n - 1)
            if s > 0 and heads:
                act_C(act, b, s - 1)
            if heads:
                act_E(act, b, s)
            act_side(act, s, b, par, front, heads) if s >= 5 else None

    def dve_M(dve, b, h):
        ge(dve, s_full, n * b + h + 1)
        dve.tensor_reduce(nmax[:, h % 2, :], s_ps[h % 2][:, :].rearrange("p (q k) -> p q k", q=QT),
                          AX, ALU.max, negate=True).then_inc(max_done, 1)

    def dve_R(dve, b, h):
        ge(dve, pt_ev, n * b + h + 1)
        dve.tensor_tensor(p2[:, h % 2, :], pT[:, h % 2, :], p1[:, h % 2, :, :, 1].rearrange("p k n -> p (k n)"),
                          ALU.subtract).then_inc(p2_done, 1)

    def dve_F(dve, b, g):
        ge(dve, o_done, n * b + 2 * g + 2)
        ge(dve, t_job, NTL * (b - 1) + 1 + g // 2)
        o = o_ps[g % 2][:, 0:QT * 2 * W].rearrange("p (c w) -> p c w", w=W)
        dve.reciprocal(rec[:, g % 2, :], o[:, :, DH0]).then_inc(rec_ready, 1)
        ge(dve, rec_ready, (n // 2) * b + g + 1)
        for q in range(QT):
            ins = dve.tensor_tensor(att[:, q, g * P:(g + 1) * P].rearrange("p (h w) -> p h w", w=DH0),
                                    o[:, q * 2:(q + 1) * 2, 0:DH0],
                                    rec[:, g % 2, q * 2:(q + 1) * 2].unsqueeze(2).to_broadcast([P, 2, DH0]), ALU.mult)
        ins.then_inc(att_done, 1)

    def dve_side(dve, s, b, par, front, tail):
        f, t = b + 1, b - 1
        if front and s == 0:
            if isinstance(f, int) and f in (0, 2):
                ge(dve, x_in[f // 2], 16)
            ln_stats(dve, ln, lambda q: tile1(x, f, q), f)
            ln_variance(dve, ln, f)
        if front and s == 1:
            ge(dve, f_job, NF * f - 2)
            ln_apply(dve, ln, lambda q: tile1(x, f, q), lambda q: xn[:, q, :], f).then_inc(xn_ready, 1)
        if front and s in (3, 4):
            i = s - 3
            ge(dve, f_act, NF * f + s)
            dve.tensor_tensor(v2[:, 1 - par, i * n:(i + 1) * n, 0:DH0], f_ps[i][:, :].rearrange("p (h w) -> p h w", h=n),
                              v1[:, 1 - par, i * n:(i + 1) * n, 0:DH0], ALU.subtract).then_inc(f_dve, 1)
        if tail and s in (1, 3):
            ge(dve, t_job, NTL * t + 1 + s // 2)
            dve.tensor_scalar(flat(attT[:, s - 1:s + 1, :]), t_ps[:, :], 1.0, None, ALU.mult).then_inc(t_dve, 1)
        if tail and s == 6:
            ge(dve, t_job, NTL * t + 3)
            ge(dve, bo_added, t + 1)
            dve.tensor_tensor(tile2(x, t), t_ps[:, :], tile2(x, t), ALU.add).then_inc(t_dve, 1)

    def dve_turn(dve, b, par, front, heads, tail):
        for s in range(n):
            if heads:
                dve_M(dve, b, s)
            if s % 2 == 0 and s < 4 and tail:
                dve_F(dve, b - 1, 2 + s // 2)
            if s % 2 == 0 and s >= 4 and heads:
                dve_F(dve, b, s // 2 - 2)
            if s == 0 and tail:
                dve_R(dve, b - 1, n - 1)
            if s > 0 and heads:
                dve_R(dve, b, s - 1)
            dve_side(dve, s, b, par, front, tail)

    def zero_slots(pool):
        for name, tiles in (("zs0", TILES0), ("zs1", TILES1)):
            for t in range(0, tiles, NT):
                k = min(NT, tiles - t)
                pool.dma_start(m[name][t * P:(t + k) * P, :].rearrange("(t p) d -> p t d", p=P),
                               m["z"][:, 0:k * D].rearrange("p (t d) -> p t d", d=D))\
                    .then_inc(m["zero_fill"], 16)

    def pool_turn(pool, b, par, front, heads, tail):
        if front:
            ln_power(pool, ln, b + 1)
            if isinstance(b, int) and b < 0:
                ge(pool, wo_in, 32)
            ge(pool, xn_ready, b + 2)
            pool.tensor_tensor(tile2(x, b + 1).rearrange("p (q d) -> p q d", q=QT),
                               tile2(x, b + 1).rearrange("p (q d) -> p q d", q=QT),
                               bo.unsqueeze(1).to_broadcast([P, QT, D]), ALU.add).then_inc(bo_added, 1)
            if isinstance(b, int) and b == 1:
                zero_slots(pool)

    def turns(eng, turn):
        turn(eng, -1, 1, True, False, False)
        turn(eng, 0, 0, True, True, False)
        turn(eng, 1, 1, True, True, True)
        turn(eng, 2, 0, True, True, True)
        with eng.Fori(1, B // 2 - 1) as i:
            turn(eng, i * 2 + 1, 1, True, True, True)
            turn(eng, i * 2 + 2, 0, True, True, True)
        turn(eng, B - 1, 1, False, True, True)
        turn(eng, B, 0, False, False, True)

    with nc.Block() as block:
        @block.sync
        def _(sp):
            early = 2 * QT * D
            sp.dma_start(wk, a["wk0"]).then_inc(kv_in, 16)
            sp.dma_start(ctxT[:, 0], a["ctxT"][0]).then_inc(ctx_in[0], 16)
            sp.dma_start(wv, a["wv0"]).then_inc(kv_in, 16)
            sp.dma_start(x[:, 0:early], a["x"][:, 0:early]).then_inc(x_in[0], 16)
            sp.dma_start(m["ident"][:, :], a["ident"]).then_inc(q_in, 16)
            sp.dma_start(wq, a["wq0"]).then_inc(q_in, 16)
            sp.dma_start(bo, a["bo0"].partition_broadcast(P)).then_inc(wo_in, 16)
            sp.dma_start(wo, a["wo0"]).then_inc(wo_in, 16)
            sp.dma_start(ctxT[:, 1], a["ctxT"][1]).then_inc(ctx_in[1], 16)
            sp.dma_start(x[:, early:NT * D], a["x"][:, early:NT * D]).then_inc(x_in[1], 16)
            sp.dma_start(m["upper"][:, :], a["upper"]).then_inc(m["const_in"], 16)
            sp.dma_start(m["ones"][:, :], a["ones"]).then_inc(m["const_in"], 16)
            wself = self0_weights(m)
            for name in ("wq", "wk", "wv", "wp", "ln1", "ln2", "ln2w", "ln2b", "gw", "gb"):
                src = a["s_" + name]
                if name in ("ln2w", "ln2b", "gb"):
                    src = src.partition_broadcast(P)
                sp.dma_start(wself[name], src).then_inc(m["w_self_in"], 16)
            for i, consts in enumerate(m["route"]):
                for dst, name in zip(consts, ("incl", "rank", "steps", "jx")):
                    sp.dma_start(dst[:, :], a[name + str(i)].partition_broadcast(P)).then_inc(m["route_in"], 16)
            w1v = m["w1"][:, :].rearrange("p (e n) -> p e n", e=E0)
            for b in range(B):
                if b + 2 < B:
                    sp.wait_ge(f_job, NF * b + 4)
                    sp.dma_start(ctxT[:, b % 2], a["ctxT"][b + 2]).then_inc(ctx_in[b % 2], 16)
                sp.dma_start(w1v[:, b, :], a["w1"][b]).then_inc(m["w1_in"], 16)

        @block.gpsimd
        def _(pool):
            pool.memset(v1.rearrange("p a g w -> p (a g) w")[:, :, DH0:W], 1.0).then_inc(start, 1)
            pool.memset(v2.rearrange("p a g w -> p (a g) w")[:, :, DH0:W], 0.0).then_inc(start, 1)
            pool.memset(m["power"][:, :], -0.5).then_inc(start, 1)
            pool.memset(m["cw"][:, :, :], 1.0).then_inc(start, 1)
            pool.memset(m["z"][:, :], 0.0).then_inc(start, 1)
            pool.wait_ge(start, 5)
            turns(pool, pool_turn)

        @block.tensor
        def _(pe):
            pe.wait_ge(kv_in, 32)
            pe.wait_ge(start, 5)
            turns(pe, pe_turn)

        @block.scalar
        def _(act):
            turns(act, act_turn)

        @block.vector
        def _(dve):
            turns(dve, dve_turn)



def self0_weights(m):
    cv = Carve(m["r"], m["RW"])
    w = dict(wq=cv.take(P, KD, D), wk=cv.take(P, KD, D), wv=cv.take(P, KD, D), wp=cv.take(P, KD, D),
             ln1=cv.take(P, 2, KD), ln2=cv.take(P, 2, KD), ln2w=cv.take(P, D), ln2b=cv.take(P, D),
             gw=cv.take(P, KD, E0), gb=cv.take(P, E0))
    w["carve"] = cv
    return w


def self0(nc, a, m):
    w = self0_weights(m)
    cv, cw = w["carve"], Carve(m["w2"], m["W1WORDS"])
    cw.at = m["W1WORDS"] // 2
    G, W = H1 // 2, DH1 + 1
    TERMS = 6
    p = cv.take(P, 2, QT, S)
    pT = cv.take(P, 4, QT * S)
    p1 = pT.rearrange("p s n -> p (s n)").bitcast(BF16).rearrange("p (s k n two) -> p s k n two", s=4, k=QT, two=2)
    p2 = cv.take(P, 4, QT * S, dt=F16)
    v1 = cv.take(P, 2, QT * H1, W, dt=BF16)
    v2 = cv.take(P, 2, QT * H1, W, dt=F16)
    att = cv.take(P, 2, QT, D)
    xn, zT, attT = cv.take(P, QT, D), cv.take(P, KD, S), cv.take(P, KD, S)
    nmax, rec = cv.take(P, 2, QT), cv.take(P, 2, QT * G)
    z2T = attT
    qS, kS = cw.take(TERMS * DH1, H1, S, dt=BF16), cw.take(TERMS * DH1, H1, S, dt=BF16)
    qp, kp = [[cw.take(P, 2 * S, dt=BF16) for _ in range(3)] for _ in range(2)]
    rq, rk, y1, n2, tmp = cw.take(P, 2 * S), cw.take(P, 2 * S), cw.take(P, QT * D), cw.take(P, QT, D), cw.take(P, QT, D)
    sem = m["sem"]
    ln = [ln_buffers(m, cv, f"s0_ln{i}_") for i in range(3)]
    (s_full, max_done, exp_done, pt_full, pt_ev, p2_dve, p2_pool, o_done, att_done, rec_ready, ones_set,
     f_job, f_act, f_dve, f_pool, t_job, t_act, t_dve, y0_ready, xn_ready, n2_ready, x_added, t_pool) = (
        sem("s0_" + s) for s in (
            "s_full", "max_done", "exp_done", "pt_full", "pt_ev", "p2_dve", "p2_pool", "o_done", "att_done",
            "rec_ready", "ones_set", "f_job", "f_act", "f_dve", "f_pool", "t_job", "t_act", "t_dve", "y0_ready",
            "xn_ready", "n2_ready", "x_added", "t_pool"))
    q_out, k_out = sem("s0_q_out"), sem("s0_k_out")
    half_in = [sem(f"s0_half_in{i}") for i in range(2)]
    qD, kD = m["q_parts"], m["k_parts"]
    s_ps, pt_ps, o_ps, f_ps, t_ps = m["psum"][0:2], m["psum"][2:4], m["psum"][4:6], m["psum"][6], m["psum"][7]
    x, z, ident = m["x"], m["z"], m["ident"]
    lg = m["logits"][:, 0:NT * E0]
    NW = 10
    n = H1
    LAG_T, LAG_R, LAG_PV = 2, 3, 5


    def pe_S(pe, b, h):
        if h % G == 0:
            ge(pe, half_in[h // G], 64 * b + 64)
        ge(pe, exp_done, n * b + h - 1)
        for q in range(QT):
            ins = pe.matmul(s_ps[h % 2][:, q * S:(q + 1) * S], qS[:, h, q * P:(q + 1) * P], kS[:, h, :],
                            start=True, stop=True)
        ins.then_inc(s_full, 1)

    def pe_T(pe, b, h):
        ge(pe, exp_done, n * b + h + 1)
        ge(pe, pt_ev, n * b + h - 1)
        for kt in range(QT):
            for q in range(QT):
                at = kt * S + q * P
                ins = pe.transpose(pt_ps[h % 2][:, at:at + P], p[:, h % 2, q, kt * P:(kt + 1) * P], ident[:, :])
        ins.then_inc(pt_full, 1)

    def pe_PV(pe, b, par, h):
        if h == 0:
            ge(pe, f_act, 4 * b + 4)
            ge(pe, f_dve, 5 * b + 5)
        if h % G == 0:
            ge(pe, att_done, 2 * b + h // G - 1)
        if h % 2 == 0:
            ge(pe, p2_dve, (n // 2) * b + h // 2 + 1)
        else:
            ge(pe, p2_pool, (n // 2) * b + h // 2 + 1)
        for q in range(QT):
            o = o_ps[h // G][:, (q * G + h % G) * W:(q * G + h % G + 1) * W]
            k = 0
            for kt in range(QT):
                cols = slice(kt * S + q * P, kt * S + (q + 1) * P)
                for lhsT in (p1[:, h % 4, kt, q * P:(q + 1) * P, 1], p2[:, h % 4, cols]):
                    for v in (v1, v2):
                        ins = pe.matmul(o, lhsT, v[:, par, kt * H1 + h, :], start=(k == 0), stop=(k == 4 * QT - 1))
                        k += 1
        ins.then_inc(o_done, 1)

    def pe_side(pe, s, b, par, front, tail):
        f, t = b + 1, b - 1
        if front and s == 5:
            ge(pe, xn_ready, f + 1)
            ge(pe, f_act, 4 * f)
            ge(pe, f_dve, 5 * f)
            for k in range(KD):
                for q in range(QT):
                    ins = pe.transpose(f_ps[:, k * S + q * P:k * S + (q + 1) * P], xn[:, q, k * P:(k + 1) * P],
                                       ident[:, :])
            ins.then_inc(f_job, 1)
        if front and s in (6, 8):
            ge(pe, f_act, 4 * f + (1 if s == 6 else 2))
            if s == 8:
                ge(pe, f_dve, 5 * f + 1)
            wt = w["wq"] if s == 6 else w["wk"]
            for i in range(2):
                for k in range(KD):
                    ins = pe.matmul(f_ps[:, i * S:(i + 1) * S], wt[:, k, i * P:(i + 1) * P], zT[:, k, :],
                                    start=(k == 0), stop=(k == KD - 1))
            ins.then_inc(f_job, 1)
        if front and s == 10:
            ge(pe, f_act, 4 * f + 3)
            ge(pe, f_dve, 5 * f + 3)
            for q in range(QT):
                for k in range(KD):
                    ins = pe.matmul(f_ps[:, q * D:(q + 1) * D], zT[:, k, q * P:(q + 1) * P], w["wv"][:, k, :],
                                    start=(k == 0), stop=(k == KD - 1))
            ins.then_inc(f_job, 1)
        if tail and s == 6:
            ge(pe, att_done, 2 * t + 2)
            ge(pe, t_dve, 2 * t)
            for k in range(KD):
                for q in range(QT):
                    ins = pe.transpose(t_ps[:, k * S + q * P:k * S + (q + 1) * P],
                                       att[:, 1 - par, q, k * P:(k + 1) * P], ident[:, :])
            ins.then_inc(t_job, 1)
        if tail and s == 8:
            ge(pe, t_act, 2 * t + 1)
            for q in range(QT):
                for k in range(KD):
                    ins = pe.matmul(t_ps[:, q * D:(q + 1) * D], attT[:, k, q * P:(q + 1) * P], w["wp"][:, k, :],
                                    start=(k == 0), stop=(k == KD - 1))
            ins.then_inc(t_job, 1)
        if tail and s == 13:
            ge(pe, n2_ready, t + 1)
            ge(pe, t_dve, 2 * t + 1)
            for k in range(KD):
                for q in range(QT):
                    ins = pe.transpose(t_ps[:, k * S + q * P:k * S + (q + 1) * P], n2[:, q, k * P:(k + 1) * P],
                                       ident[:, :])
            ins.then_inc(t_job, 1)
        if tail and s == 15:
            ge(pe, t_act, 2 * t + 2)
            for q in range(QT):
                for k in range(KD):
                    ins = pe.matmul(t_ps[:, q * E0:(q + 1) * E0], z2T[:, k, q * P:(q + 1) * P], w["gw"][:, k, :],
                                    start=(k == 0), stop=(k == KD - 1))
            ins.then_inc(t_job, 1)

    def pe_turn(pe, b, par, pre, front, heads, tail):
        for s in range(n):
            if heads:
                pe_S(pe, b, s)
            if s < LAG_T and tail:
                pe_T(pe, b - 1, n + s - LAG_T)
            if s >= LAG_T and heads:
                pe_T(pe, b, s - LAG_T)
            if s < LAG_PV and tail:
                pe_PV(pe, b - 1, 1 - par, n + s - LAG_PV)
            if s >= LAG_PV and heads:
                pe_PV(pe, b, par, s - LAG_PV)
            pe_side(pe, s, b, par, front, tail)

    def act_E(act, b, h):
        ge(act, max_done, n * b + h + 1)
        ge(act, pt_full, n * b + h - 1)
        for q in range(QT):
            ins = act.activation(p[:, h % 2, q, :], s_ps[h % 2][:, q * S:(q + 1) * S], ACT.Exp,
                                 bias=nmax[:, h % 2, q:q + 1])
        ins.then_inc(exp_done, 1)

    def act_C(act, b, h):
        ge(act, pt_full, n * b + h + 1)
        ge(act, o_done, n * b + h - 3)
        act.copy(pT[:, h % 4, :], pt_ps[h % 2][:, :]).then_inc(pt_ev, 1)

    def act_side(act, s, b, par, front, tail):
        f, t = b + 1, b - 1
        if front and s == 5:
            ge(act, f_job, 4 * f + 1)
            for k in range(KD):
                ins = act.activation(zT[:, k, :], f_ps[:, k * S:(k + 1) * S], ACT.Identity,
                                     bias=w["ln1"][:, 1, k:k + 1], scale=w["ln1"][:, 0, k:k + 1])
            ins.then_inc(f_act, 1)
        if front and s == 6:
            ge(act, f_job, 4 * f + 2)
            ge(act, q_out, 48 * f)
            act.mul(qp[0], f_ps[:, :], DH1 ** -0.5).then_inc(f_act, 1)
        if front and s == 8:
            ge(act, f_job, 4 * f + 3)
            ge(act, k_out, 48 * f)
            act.copy(kp[0], f_ps[:, :]).then_inc(f_act, 1)
        if front and s == 10:
            ge(act, f_job, 4 * f + 4)
            ge(act, o_done, n * (f - 1))
            act.copy(v1[:, 1 - par, :, 0:DH1], f_ps[:, :].rearrange("p (g w) -> p g w", w=DH1)).then_inc(f_act, 1)
        if tail and s == 6:
            ge(act, t_job, 4 * t + 1)
            act.copy(attT.rearrange("p k s -> p (k s)"), t_ps[:, :]).then_inc(t_act, 1)
        if tail and s == 13:
            ge(act, t_job, 4 * t + 3)
            for k in range(KD):
                ins = act.activation(z2T[:, k, :], t_ps[:, k * S:(k + 1) * S], ACT.Identity,
                                     bias=w["ln2"][:, 1, k:k + 1], scale=w["ln2"][:, 0, k:k + 1])
            ins.then_inc(t_act, 1)

    def act_turn(act, b, par, pre, front, heads, tail):
        for s in range(n):
            if s < LAG_T and tail:
                act_C(act, b - 1, n + s - LAG_T)
            if s >= LAG_T and heads:
                act_C(act, b, s - LAG_T)
            if heads:
                act_E(act, b, s)
            act_side(act, s, b, par, front, tail)

    def dve_M(dve, b, h):
        ge(dve, s_full, n * b + h + 1)
        dve.tensor_reduce(nmax[:, h % 2, :], s_ps[h % 2][:, :].rearrange("p (q k) -> p q k", q=QT),
                          AX, ALU.max, negate=True).then_inc(max_done, 1)

    def rest(eng, b, h, done):
        ge(eng, pt_ev, n * b + h + 1)
        eng.tensor_tensor(p2[:, h % 4, :], pT[:, h % 4, :], p1[:, h % 4, :, :, 1].rearrange("p k n -> p (k n)"),
                          ALU.subtract).then_inc(done, 1)

    def dve_F(dve, b, par, g):
        ge(dve, o_done, n * b + G * (g + 1))
        if g == 0:
            ge(dve, t_job, 4 * (b - 2) + 1)
        o = o_ps[g][:, 0:QT * G * W].rearrange("p (c w) -> p c w", w=W)
        dve.reciprocal(rec[:, g, :], o[:, :, DH1]).then_inc(rec_ready, 1)
        ge(dve, rec_ready, 2 * b + g + 1)
        for q in range(QT):
            ins = dve.tensor_tensor(att[:, par, q, g * P:(g + 1) * P].rearrange("p (h w) -> p h w", w=DH1),
                                    o[:, q * G:(q + 1) * G, 0:DH1],
                                    rec[:, g, q * G:(q + 1) * G].unsqueeze(2).to_broadcast([P, G, DH1]), ALU.mult)
        ins.then_inc(att_done, 1)

    def dve_first_stats(dve, f):
        ln_stats(dve, ln[0], lambda q: tile1(x, f, q), f)
        ln_variance(dve, ln[0], f)

    def dve_first_norm(dve, f):
        ln_apply(dve, ln[0], lambda q: tile1(x, f, q), lambda q: tile1(z, f, q), f).then_inc(y0_ready, 1)

    def dve_side(dve, s, b, par, pre, front, tail):
        f, t = b + 1, b - 1
        if pre and s == 13:
            dve_first_stats(dve, f + 1)
        if pre and s == 15:
            dve_first_norm(dve, f + 1)
        if front and s == 0:
            ge(dve, y0_ready, f + 1)
            dve.memset(ln[1]["spare"], 0.0)
            ln_stats(dve, ln[1], lambda q: tile1(z, f, q), f)
        if front and s == 1:
            ln_variance(dve, ln[1], f)
        if front and s == 2:
            ge(dve, f_job, 4 * f - 3)
            ln_apply(dve, ln[1], lambda q: tile1(z, f, q), lambda q: xn[:, q, :], f).then_inc(xn_ready, 1)
        if front and s == 6:
            ge(dve, f_act, 4 * f + 2)
            ge(dve, f_pool, 2 * f - 1)
            dve.scalar_tensor_tensor(rq, f_ps[:, :], DH1 ** -0.5, qp[0], ALU.mult, ALU.subtract).then_inc(f_dve, 1)
            ge(dve, f_dve, 5 * f + 1)
            dve.tensor_copy(qp[1], rq).then_inc(f_dve, 1)
        if front and s == 8:
            ge(dve, f_act, 4 * f + 3)
            ge(dve, f_pool, 2 * f)
            dve.tensor_tensor(rk, f_ps[:, :], kp[0], ALU.subtract).then_inc(f_dve, 1)
            ge(dve, f_dve, 5 * f + 3)
            dve.tensor_copy(kp[1], rk).then_inc(f_dve, 1)
        if front and s == 10:
            ge(dve, f_act, 4 * f + 4)
            dve.tensor_tensor(v2[:, 1 - par, :, 0:DH1], f_ps[:, :].rearrange("p (g w) -> p g w", w=DH1),
                              v1[:, 1 - par, :, 0:DH1], ALU.subtract).then_inc(f_dve, 1)
        if tail and s == 5:
            dve_F(dve, t, 1 - par, 1)
        if tail and s == 8:
            ge(dve, t_job, 4 * t + 2)
            ge(dve, x_added, t)
            dve.tensor_tensor(y1, t_ps[:, :], tile2(z, t), ALU.add).then_inc(t_dve, 1)
        if tail and s == 9:
            ge(dve, t_dve, 2 * t + 1)
            dve.memset(ln[1]["spare"], 0.0)
            ln_stats(dve, ln[2], lambda q: y1[:, q * D:(q + 1) * D], t)
        if tail and s == 10:
            ln_variance(dve, ln[2], t)
        if tail and s == 12:
            ge(dve, t_pool, 2 * t)
            ge(dve, t_job, 4 * t - 1)
            ln_apply(dve, ln[2], lambda q: y1[:, q * D:(q + 1) * D], lambda q: n2[:, q, :], t).then_inc(n2_ready, 1)
        if tail and s == 15:
            ge(dve, t_job, 4 * t + 4)
            dve.tensor_tensor(lg[:, bass.ds(t * (QT * E0), QT * E0)].rearrange("p (q e) -> p q e", q=QT),
                              t_ps[:, 0:QT * E0].rearrange("p (q e) -> p q e", q=QT),
                              w["gb"].unsqueeze(1).to_broadcast([P, QT, E0]), ALU.add).then_inc(t_dve, 1)

    def dve_turn(dve, b, par, pre, front, heads, tail):
        for s in range(n):
            if heads:
                dve_M(dve, b, s)
            if s == 1 and tail:
                rest(dve, b - 1, n - 2, p2_dve)
            if s >= LAG_R and (s - LAG_R) % 2 == 0 and heads:
                rest(dve, b, s - LAG_R, p2_dve)
            if s == G + LAG_PV and heads:
                dve_F(dve, b, par, 0)
            dve_side(dve, s, b, par, pre, front, tail)

    def pool_turn(pool, b, par, pre, front, heads, tail):
        f, t = b + 1, b - 1
        for s in range(n):
            if s < LAG_R and (s - LAG_R) % 2 == 1 and tail:
                rest(pool, b - 1, n + s - LAG_R, p2_pool)
            if s >= LAG_R and (s - LAG_R) % 2 == 1 and heads:
                rest(pool, b, s - LAG_R, p2_pool)
            if pre and s == 14:
                ln_power(pool, ln[0], f + 1)
            if front and s == 1:
                ln_power(pool, ln[1], f)
            if front and s in (7, 9):
                r, parts, c = (rq, qp, 0) if s == 7 else (rk, kp, 1)
                ge(pool, f_dve, 5 * f + 2 * c + 2)
                pool.tensor_tensor(parts[2], r, parts[1], ALU.subtract).then_inc(f_pool, 1)
            if tail and s == 10:
                ge(pool, t_dve, 2 * t + 1)
                pool.tensor_tensor(tile2(x, t), tile2(x, t), y1, ALU.add).then_inc(x_added, 1)
            if tail and s == 11:
                ln_power(pool, ln[2], t)
            if tail and s == 13:
                ge(pool, n2_ready, t + 1)
                pool.tensor_tensor(tmp, n2, w["ln2w"].unsqueeze(1).to_broadcast([P, QT, D]), ALU.mult).then_inc(t_pool, 1)
                ge(pool, t_pool, 2 * t + 1)
                pool.tensor_tensor(tile2(z, t).rearrange("p (q d) -> p q d", q=QT), tmp,
                                   w["ln2b"].unsqueeze(1).to_broadcast([P, QT, D]), ALU.add).then_inc(t_pool, 1)

    def sp_front(sp, f, par):
        def out_q(i, at):
            ge(sp, *at)
            sp.dma_start(qD[par, i].rearrange("d g n -> (d g) n"), qp[i]).then_inc(q_out, 16)

        def out_k(i, lo, rep, at):
            ge(sp, *at)
            sp.dma_start(kD[par, lo:lo + rep].rearrange("r d g n -> (d g) r n"),
                         kp[i].unsqueeze(1).to_broadcast([P, rep, 2 * S])).then_inc(k_out, 16)

        out_q(0, (f_act, 4 * f + 2))
        out_k(0, 0, 3, (f_act, 4 * f + 3))
        out_q(1, (f_dve, 5 * f + 2))
        out_q(2, (f_pool, 2 * f + 1))
        out_k(1, 3, 2, (f_dve, 5 * f + 4))
        out_k(2, 5, 1, (f_pool, 2 * f + 2))
        ge(sp, q_out, 48 * f + 48)
        ge(sp, k_out, 48 * f + 48)
        for i in range(2):
            ge(sp, s_full, n * (f - 1) + G * (i + 1))
            hs = slice(i * G, (i + 1) * G)
            for lo, cnt in ((0, 3), (3, 2), (5, 1)):
                sp.dma_start(qS[lo * DH1:(lo + cnt) * DH1, hs, :],
                             qD[par, 0:cnt, :, :, i * S:(i + 1) * S].rearrange("j d g n -> (j d) g n"))\
                    .then_inc(half_in[i], 16)
            sp.dma_start(kS[:, hs, :], kD[par, :, :, :, i * S:(i + 1) * S].rearrange("j d g n -> (j d) g n"))\
                .then_inc(half_in[i], 16)

    def turns(eng, turn):
        turn(eng, -1, 1, True, True, False, False)
        turn(eng, 0, 0, True, True, True, False)
        turn(eng, 1, 1, True, True, True, True)
        with eng.Fori(1, B // 2 - 1) as i:
            turn(eng, i * 2, 0, True, True, True, True)
            turn(eng, i * 2 + 1, 1, True, True, True, True)
        turn(eng, B - 2, 0, False, True, True, True)
        turn(eng, B - 1, 1, False, False, True, True)
        turn(eng, B, 0, False, False, False, True)

    with nc.Block() as block:
        @block.sync
        def _(sp):
            w2v = m["w2"][:, :].rearrange("p (e n) -> p e n", e=E0)
            for e in range(E0 // 2):
                sp.dma_start(w2v[:, e, :], a["w2"][e]).then_inc(m["w2_in"], 16)
            sp_front(sp, 0, 0)
            sp_front(sp, 1, 1)
            with sp.Fori(0, B // 2 - 1) as i:
                sp_front(sp, i * 2 + 2, 0)
                sp_front(sp, i * 2 + 3, 1)

        @block.gpsimd
        def _(pool):
            pool.memset(v1.rearrange("p a g w -> p (a g) w")[:, :, DH1:W], 1.0).then_inc(ones_set, 1)
            pool.memset(v2.rearrange("p a g w -> p (a g) w")[:, :, DH1:W], 0.0).then_inc(ones_set, 1)
            pool.wait_ge(m["w_self_in"], 16 * NW)
            pool.wait_ge(m["zero_fill"], 16 * 6)
            pool.nop().then_inc(ones_set, 1)
            ln_power(pool, ln[0], 0)
            turns(pool, pool_turn)

        @block.tensor
        def _(pe):
            pe.wait_ge(ones_set, 3)
            pe.wait_ge(m["w_self_in"], 16 * NW)
            turns(pe, pe_turn)

        @block.scalar
        def _(act):
            act.wait_ge(m["w_self_in"], 16 * NW)
            turns(act, act_turn)

        @block.vector
        def _(dve):
            dve.wait_ge(ones_set, 3)
            dve.wait_ge(m["w_self_in"], 16 * NW)
            dve_first_stats(dve, 0)
            dve_first_norm(dve, 0)
            turns(dve, dve_turn)



def route(nc, a, m, which):
    E, top, tiles = (E0, 1, TILES0) if which == 0 else (E1, TOP1, TILES1)
    tag = f"r{which}_"
    cv = Carve(m["r"], m["RW"])
    if which == 0:
        cv.at = 4000
    mask, rank, steps, jx = (v[:, :] for v in m["route"][which])
    mask = mask.rearrange("p (a b) -> p a b", a=E)
    val, mx, eq, any_oh = cv.take(P, NT, E), cv.take(P, NT), cv.take(P, NT, E), cv.take(P, NT, E)
    oh = [cv.take(P, NT, E) for _ in range(top)]
    slotf, cnt, cmp, padded = cv.take(P, NT), cv.take(P, E), cv.take(P, E, NC), cv.take(P, E)
    lt, end, base = cv.take(P, E, E), cv.take(P, E), cv.take(P, E)
    own_cmp, own_f = cv.take(P, tiles, E), cv.take(P, tiles)
    sem = m["sem"]
    own, oh_ready, rank_ready = sem(tag + "own"), sem(tag + "oh_ready"), sem(tag + "rank_ready")
    slots_ready, sent = sem(tag + "slots_ready"), sem(tag + "sent")
    lg = m["logits"][:, 0:NT * E].rearrange("p (t e) -> p t e", t=NT)
    ohb = m["oh_bf"][:, 0:NT * E]
    ranks, counts = m["psum"][0][:, 0:NT * E], m["psum"][1][:, 0:NT * E]
    zs = m[f"zs{which}"]
    src = m["z"]
    if which == 1:
        w = ffn1_buffers(m)
        sw1, sw2, sb1, x3T, cs = w["sw1"], w["sw2"], w["sb1"], w["x3T"], w["carve"]
        shT, b2, cwT = cs.take(P, B, KD, S), cs.take(E1 + 1, D), cs.take(E1 + 1, NT, P)
        h_full, h_ready, cw_full, cwT_ready, y_full, y_added, b2_in = (sem("s1_" + t) for t in (
            "h_full", "h_ready", "cw_full", "cwT_ready", "y_full", "y_added", "b2_in"))
        ps, x = m["psum"], m["x"]

    def over_e(v):
        return v.unsqueeze(2).to_broadcast([P, NT, E])

    def over_t(v):
        return v.unsqueeze(1).to_broadcast([P, NT, E])

    with nc.Block() as block:
        @block.sync
        def _(sp):
            if which == 1:
                sp.dma_start(b2, a["b2"]).then_inc(b2_in, 16)
            if which == 0:
                w2v = m["w2"][:, :].rearrange("p (e n) -> p e n", e=E0)
                for e in range(E0 // 2, E0):
                    sp.dma_start(w2v[:, e, :], a["w2"][e]).then_inc(m["w2_in"], 16)

        @block.tensor
        def _(pe):
            if which == 1:
                for b in range(B):
                    if b >= 2:
                        pe.wait_ge(h_ready, b - 1)
                    for i in range(KD):
                        for k in range(KD):
                            ins = pe.matmul(ps[2 + b % 2][:, i * S:(i + 1) * S], sw1[:, k, i * P:(i + 1) * P],
                                            x3T[:, k, b * S:(b + 1) * S], start=(k == 0), stop=(k == KD - 1))
                    ins.then_inc(h_full, 1)
            if which == 0:
                pe.wait_ge(m["const_in"], 32)
            pe.wait_ge(oh_ready, 1)
            pe.matmul(ranks, m["upper"][:, :], ohb, start=True, stop=False)
            v = ranks.rearrange("p (t e) -> p t e", t=NT)
            for t in range(NT - 1):
                pe.matmul(v[:, t + 1:NT, :], m["ones"][:, :],
                          ohb[:, t * E:(t + 1) * E].unsqueeze(1).to_broadcast([P, NT - 1 - t, E]),
                          start=False, stop=(t == NT - 2))
            pe.matmul(counts, m["ones"][:, :], ohb, start=True, stop=True).then_inc(rank_ready, 1)
            if which == 1:
                pe.wait_ge(slots_ready, 1)
                for j in range(4):
                    for t in range(4):
                        ins = pe.transpose(ps[4 + j][0:E1 + 1, t * P:(t + 1) * P], m["cw"][:, 4 * j + t, :],
                                           m["ident"][:, :])
                    ins.then_inc(cw_full, 1)
                pe.wait_ge(b2_in, 16)
                pe.wait_ge(h_ready, B)
                for b in range(B):
                    pe.wait_ge(cwT_ready, b // 2 + 1)
                    if b >= 2:
                        pe.wait_ge(y_added, b - 1)
                    for q in range(QT):
                        y = ps[2 + b % 2][:, q * D:(q + 1) * D]
                        for k in range(KD):
                            pe.matmul(y, shT[:, b, k, q * P:(q + 1) * P], sw2[:, k, :], start=(k == 0), stop=False)
                        ins = pe.matmul(y, cwT[:, QT * b + q, :], b2, start=False, stop=True)
                    ins.then_inc(y_full, 1)

        @block.vector
        def _(dve):
            ch = Chain(dve, own, 0)

            def step(ins):
                ch.done(ins)
                ch.wait()

            dve.wait_ge(m["route_in"], 16 * 8)
            if which == 1:
                step(dve.tensor_reduce(mx, lg, AX, ALU.max))
                step(dve.tensor_tensor(val, lg, over_e(mx), ALU.subtract))
                dve.nop().then_inc(m["r1_shifted"], 1)
                dve.wait_ge(m["r1_exp"], 1)
                step(dve.tensor_reduce(mx, val, AX, ALU.add))
                step(dve.reciprocal(slotf, mx))
                step(dve.tensor_tensor(val, val, over_e(slotf), ALU.mult))
            else:
                step(dve.tensor_copy(val, lg))
            for k in range(top):
                step(dve.tensor_reduce(mx, val, AX, ALU.max))
                if which == 1:
                    step(dve.tensor_copy(m["top_p"][:, k, :], mx))
                step(dve.tensor_tensor(eq, val, over_e(mx), ALU.is_equal))
                step(dve.tensor_tensor(eq, eq, over_t(rank), ALU.mult))
                step(dve.tensor_reduce(mx, eq, AX, ALU.max))
                step(dve.tensor_tensor(oh[k], over_t(rank), over_e(mx), ALU.is_equal))
                if k + 1 < top:
                    step(dve.scalar_tensor_tensor(val, oh[k], -4.0, val, ALU.mult, ALU.add))
            total = oh[0]
            if which == 1:
                step(dve.tensor_tensor(any_oh, oh[0], oh[1], ALU.add))
                step(dve.tensor_tensor(any_oh, any_oh, oh[2], ALU.add))
                total = any_oh
            dve.tensor_copy(ohb, total.rearrange("p t e -> p (t e)")).then_inc(oh_ready, 1)
            if which == 1:
                step(dve.tensor_tensor(m["cw"][:, :, 0:E], oh[0],
                                       over_e(m["top_p"][:, 0, :]), ALU.mult))
                for k in (1, 2):
                    step(dve.tensor_tensor(eq, oh[k], over_e(m["top_p"][:, k, :]), ALU.mult))
                    step(dve.tensor_tensor(m["cw"][:, :, 0:E], m["cw"][:, :, 0:E], eq, ALU.add))
            dve.wait_ge(rank_ready, 1)
            step(dve.tensor_reduce(cnt, counts.rearrange("p (t e) -> p e t", t=NT), AX, ALU.add))
            step(dve.tensor_tensor(cmp, cnt.unsqueeze(2).to_broadcast([P, E, NC]),
                                   steps.unsqueeze(1).to_broadcast([P, E, NC]), ALU.is_gt))
            step(dve.tensor_reduce(padded, cmp, AX, ALU.add))
            step(dve.tensor_tensor(lt, mask, padded.unsqueeze(1).to_broadcast([P, E, E]), ALU.mult))
            step(dve.tensor_reduce(end, lt, AX, ALU.add))
            step(dve.tensor_tensor(base, end, padded, ALU.subtract))
            step(dve.scalar_tensor_tensor(eq, over_t(base), float(P), ranks.rearrange("p (t e) -> p t e", t=NT),
                                          ALU.mult, ALU.add))
            for k in range(top):
                step(dve.tensor_tensor(val, eq, oh[k], ALU.mult))
                step(dve.tensor_reduce(slotf, val, AX, ALU.add))
                step(dve.tensor_copy(m["slots"][:, k, :], slotf))
                dve.nop().then_inc(slots_ready, 1)
            step(dve.tensor_tensor(own_cmp, jx.unsqueeze(2).to_broadcast([P, tiles, E]),
                                   end.unsqueeze(1).to_broadcast([P, tiles, E]), ALU.is_ge))
            step(dve.tensor_reduce(own_f, own_cmp, AX, ALU.add))
            step(dve.tensor_scalar(own_f, own_f, float(E - 1), None, ALU.min))
            step(dve.tensor_copy(m["owner"][:, 0:tiles], own_f))
            if which == 1:
                for b in range(B):
                    dve.wait_ge(y_full, b + 1)
                    dve.tensor_tensor(tile2(x, b), tile2(x, b), ps[2 + b % 2][:, :], ALU.add).then_inc(y_added, 1)

        if which == 1:
            @block.scalar
            def _(act):
                act.wait_ge(m["r1_shifted"], 1)
                act.activation(val, val, ACT.Exp).then_inc(m["r1_exp"], 1)
                for b in range(B):
                    act.wait_ge(h_full, b + 1)
                    for i in range(KD):
                        ins = act.activation(shT[:, b, i, :], ps[2 + b % 2][:, i * S:(i + 1) * S], ACT.Relu,
                                             bias=sb1[:, i:i + 1])
                    ins.then_inc(h_ready, 1)
                for j in range(4):
                    act.wait_ge(cw_full, j + 1)
                    act.copy(cwT[:, 4 * j:4 * j + 4, :].rearrange("p t s -> p (t s)"), ps[4 + j][0:E1 + 1, :])\
                       .then_inc(cwT_ready, 1)

        @block.gpsimd
        def _(pool):
            pool.wait_ge(m["zero_fill"], 16 * 6)
            for k in range(top):
                pool.wait_ge(slots_ready, k + 1)
                for t in range(NT):
                    pool.indirect_dma_start(zs, bass.IndirectOffsetOnAxis(m["slots"][:, k, t:t + 1], 0),
                                            src[:, t * D:(t + 1) * D], None).then_inc(sent, 16)
            pool.wait_ge(sent, 16 * NT * top)



def moe(nc, a, m, which):
    E, HID, tiles = (E0, HID0, TILES0) if which == 0 else (E1, HID1, TILES1)
    MK = HID // P
    HB = (HID + 511) // 512
    HW = min(HID, 512)
    tag = f"m{which}_"
    cv = Carve(m["r"], m["RW"])
    zt = cv.take(P, U, D)
    zT = cv.take(P, 2, KD, P)
    hid = cv.take(P, 2, HID)
    hT = cv.take(P, 2, MK, P)
    y = cv.take(P, U, D)
    if which == 0:
        w1, w2 = m["w1"][:, 0:E * KD * HID], m["w2"][:, 0:E * MK * D]
    else:
        w1, w2 = m["w1"][:, 0:E * KD * HID], m["w1"][:, E * KD * HID:E * KD * HID + E * MK * D]
        b1T = cv.take(P, E, MK)
    assert cv.at <= MOE_WORDS
    sem = m["sem"]
    z_in = [sem(tag + f"z_in{i}") for i in range(U)]
    y_out = [sem(tag + f"y_out{i}") for i in range(U)]
    t_full, zT_ready, h_full, hid_ready, g_full, hT_ready, y_full, y_ready = (
        sem(tag + s) for s in ("t_full", "zT_ready", "h_full", "hid_ready", "g_full", "hT_ready", "y_full", "y_ready"))
    ps = m["psum"]
    t_ps, h_ps, g_ps, y_ps = ps[0], ps[1:3], ps[3:5], ps[5:7]
    zs, ys = m[f"zs{which}"], m[f"ys{which}"]


    def T(pe, j, u, behind):
        p = u % 2
        pe.wait_ge(z_in[u], 16 * ((j - u) // U) + 16 if isinstance(j, int) else j * (16 // U) + (16 - 16 // U * u))
        if behind:
            pe.wait_ge(zT_ready, j)
        for k in range(KD):
            ins = pe.transpose(t_ps[:, k * P:(k + 1) * P], zt[:, u, k * P:(k + 1) * P], m["ident"][:, :])
        ins.then_inc(t_full, 1)

    def owners(engine, j, n):
        return nc.values_load_multi_w_load_instructions(m["owner"][0:1, bass.ds(j, n)], engines=[engine],
                                                        min_val=0, max_val=E - 1)[1]

    def H(pe, j, u, behind, e):
        p = u % 2
        pe.wait_ge(zT_ready, j + 1)
        if behind:
            pe.wait_ge(hid_ready, j)
        for n in range(HB):
            for k in range(KD):
                ins = pe.matmul(h_ps[n][:, 0:HW], zT[:, p, k, :], w1[:, bass.ds(e * (KD * HID) + (k * HID + n * HW), HW)],
                                start=(k == 0), stop=(k == KD - 1))
        ins.then_inc(h_full, 1)

    def G(pe, j, u, behind):
        p = u % 2
        pe.wait_ge(hid_ready, j + 1)
        if behind:
            pe.wait_ge(hT_ready, j)
        for i in range(MK):
            ins = pe.transpose(g_ps[i // 4][:, i % 4 * P:(i % 4 + 1) * P], hid[:, p, i * P:(i + 1) * P], m["ident"][:, :])
        ins.then_inc(g_full, 1)

    def Y(pe, j, u, behind, e):
        p = u % 2
        pe.wait_ge(hT_ready, j + 1)
        if behind:
            pe.wait_ge(y_ready, j - 1)
        for i in range(MK):
            ins = pe.matmul(y_ps[p][:, 0:D], hT[:, p, i, :], w2[:, bass.ds(e * (MK * D) + i * D, D)],
                            start=(i == 0), stop=(i == MK - 1))
        ins.then_inc(y_full, 1)

    def act_T(act, j, u):
        p = u % 2
        act.wait_ge(t_full, j + 1)
        act.copy(zT[:, p, :, :].rearrange("p k s -> p (k s)"), t_ps[:, 0:KD * P]).then_inc(zT_ready, 1)

    def act_H(act, j, u):
        p = u % 2
        act.wait_ge(h_full, j + 1)
        for n in range(HB):
            ins = act.activation(hid[:, p, n * HW:(n + 1) * HW], h_ps[n][:, 0:HW],
                                 ACT.Gelu_apprx_tanh if which == 0 else ACT.Copy)
        ins.then_inc(hid_ready, 1)

    def dve_G(dve, j, u, e):
        p = u % 2
        dve.wait_ge(g_full, j + 1)
        if which == 0:
            for n in range(2):
                ins = dve.tensor_copy(hT[:, p, 4 * n:4 * n + 4, :].rearrange("p k s -> p (k s)"), g_ps[n][:, :])
        else:
            for i in range(MK):
                ins = dve.tensor_scalar(hT[:, p, i, :], g_ps[0][:, i * P:(i + 1) * P],
                                        b1T.rearrange("p e k -> p (e k)")[:, bass.ds(e * MK + i, 1)], 0.0,
                                        ALU.add, ALU.max)
        ins.then_inc(hT_ready, 1)

    def dve_Y(dve, j, u, behind):
        dve.wait_ge(y_full, j + 1)
        if behind:
            dve.wait_ge(y_out[u], (j - u) * (16 // U))
        dve.tensor_copy(y[:, u, :], y_ps[u % 2][:, 0:D]).then_inc(y_ready, 1)

    def load(sp, j, u):
        sp.dma_start(zt[:, u, :], zs[bass.ds(j * P, P), :]).then_inc(z_in[u], 16)

    def store(sp, j, u):
        sp.wait_ge(y_ready, j + 1)
        sp.dma_start(ys[bass.ds(j * P, P), :], y[:, u, :]).then_inc(y_out[u], 16)

    V = U
    TURNS = (tiles - 3) // V
    AHEAD = U + 1

    def sp_step(sp, j, u, more):
        if more:
            sp.wait_ge(t_full, j + AHEAD - U + 1)
            load(sp, j + AHEAD, (u + AHEAD) % U)
        store(sp, j, u)

    def pe_step(pe, j, u, behind, e_h, e_y, left=4):
        if left > 3:
            T(pe, j + 3, (u + 3) % U, True)
        if left > 2:
            H(pe, j + 2, (u + 2) % U, True, e_h)
        if left > 1:
            G(pe, j + 1, (u + 1) % U, True)
        Y(pe, j, u, behind, e_y)

    def act_step(act, j, u, left=4):
        if left > 3:
            act_T(act, j + 3, (u + 3) % U)
        if left > 2:
            act_H(act, j + 2, (u + 2) % U)

    def dve_step(dve, j, u, behind, e, left=4):
        if left > 1:
            dve_G(dve, j + 1, (u + 1) % U, e)
        dve_Y(dve, j, u, behind)

    with nc.Block() as block:
        @block.sync
        def _(sp):
            if which == 1:
                sp.dma_start(b1T.rearrange("p e k -> p (e k)"), a["eb1T"]).then_inc(m["we_in"], 16)
            for j in range(U):
                load(sp, j, j)
            if which == 0:
                for dst, name in cross1_weights(m):
                    if name == "ctxT":
                        for f in range(2):
                            sp.dma_start(dst[:, f], a[name][f]).then_inc(m["c1_ctx_in"][f], 16)
                    else:
                        src = a[name].partition_broadcast(P) if name in ("bv1", "rb") else a[name]
                        sp.dma_start(dst, src).then_inc(m["c1_w_in"], 16)
            sp.wait_ge(t_full, 1)
            load(sp, U, 0)
            for j in range(V):
                sp_step(sp, j, j % U, True)
            with sp.Fori(1, TURNS - 1) as i:
                for u in range(V):
                    sp_step(sp, i * V + u, u % U, True)
            for j in range(V * (TURNS - 1), tiles):
                sp_step(sp, j, j % U, j + AHEAD < tiles)
            for u in range(U):
                sp.wait_ge(y_out[u], 16 * ((tiles + U - 1 - u) // U))

        @block.tensor
        def _(pe):
            if which == 0:
                pe.wait_ge(m["w1_in"], 16 * E0)
                pe.wait_ge(m["w2_in"], 16 * E0)
            else:
                pe.wait_ge(m["we_in"], 16 * (2 * (B - 2) + 1))
            e = owners(mybir.EngineType.PE, 0, V + 2)
            T(pe, 0, 0, False)
            T(pe, 1, 1, True)
            H(pe, 0, 0, False, e[0])
            T(pe, 2, 2, True)
            H(pe, 1, 1, True, e[1])
            G(pe, 0, 0, False)
            for j in range(V):
                pe_step(pe, j, j % U, j >= 2, e[j + 2], e[j])
            with pe.Fori(1, TURNS) as i:
                e = owners(mybir.EngineType.PE, i * V, V + 2)
                for u in range(V):
                    pe_step(pe, i * V + u, u % U, True, e[u + 2], e[u])
            e = list(owners(mybir.EngineType.PE, V * TURNS, tiles - V * TURNS)) + 2 * [None]
            for j in range(V * TURNS, tiles):
                pe_step(pe, j, j % U, True, e[j + 2 - V * TURNS], e[j - V * TURNS], tiles - j)

        @block.scalar
        def _(act):
            act_T(act, 0, 0)
            act_T(act, 1, 1)
            act_H(act, 0, 0)
            act_T(act, 2, 2)
            act_H(act, 1, 1)
            with act.Fori(0, TURNS) as i:
                for u in range(V):
                    act_step(act, i * V + u, u % U)
            for j in range(V * TURNS, tiles):
                act_step(act, j, j % U, tiles - j)

        @block.vector
        def _(dve):
            if which == 1:
                dve.wait_ge(m["we_in"], 16 * (2 * (B - 2) + 1))
            e = owners(mybir.EngineType.DVE, 0, V + 1)
            dve_G(dve, 0, 0, e[0])
            for j in range(V):
                dve_step(dve, j, j % U, j >= U, e[j + 1])
            with dve.Fori(1, TURNS) as i:
                e = owners(mybir.EngineType.DVE, i * V, V + 1)
                for u in range(V):
                    dve_step(dve, i * V + u, u % U, True, e[u + 1])
            e = list(owners(mybir.EngineType.DVE, V * TURNS, tiles - V * TURNS)) + [None]
            for j in range(V * TURNS, tiles):
                dve_step(dve, j, j % U, True, e[j + 1 - V * TURNS], tiles - j)



def cross1_weights(m):
    cv = Carve(m["r"], m["RW"])
    cv.at = MOE_WORDS
    return [(cv.take(P, KD, D), "wq1"), (cv.take(CP, KC, D), "wk1"), (cv.take(CP, KC, D), "wv1"),
            (cv.take(P, KD, E1), "rw"), (cv.take(P, 2, KD), "bqk1"), (cv.take(P, D), "bv1"), (cv.take(P, E1), "rb"),
            (cv.take(CP, 2, KC, S), "ctxT")]


def ffn1_buffers(m):
    cv = Carve(m["w2"], m["W1WORDS"])
    w = dict(sw1=cv.take(P, KD, D), sw2=cv.take(P, KD, D), sb1=cv.take(P, KD), x3T=cv.take(P, KD, B * S))
    w["carve"] = cv
    return w


ROW_GROUPS = ((0,), (1,), (2, 3), (4, 5, 6, 7))


def cross1(nc, a, m):
    w = ffn1_buffers(m)
    sw1, sw2, sb1, x3T, cv = w["sw1"], w["sw2"], w["sb1"], w["x3T"], w["carve"]
    got = Carve(m["r"], m["RW"]).take(P, NT, D)
    wq, wk, wv, rw, bqk, bv, rb, ctxT = (v for v, _ in cross1_weights(m))
    bqs, xn, xnT, n3 = cv.take(P, KD), cv.take(P, QT, D), cv.take(P, KD, S), cv.take(P, QT, D)
    qT, kT, v = cv.take(P, KD, S), cv.take(P, KD, S), cv.take(P, QT, D + 1)
    p, pT, x3_now = cv.take(P, QT, S), cv.take(P, QT, S), cv.take(P, KD, S)
    nmax, rec, spare, pool_spare = cv.take(P, QT), cv.take(P, QT), cv.take(P, 1), cv.take(P, 1)
    ln = [ln_buffers(m, cv, f"c1_ln{i}_") for i in range(2)]
    sem = m["sem"]
    (kvq_job, att_job, ffn_job, kvq_act, att_act, ffn_act, kvq_dve, att_max, rec_ready, x3_ready, ffn_dve, xn_ready,
     n3_ready, z_kept, ones_set, w_in) = (sem("c1_" + s) for s in (
         "kvq_job", "att_job", "ffn_job", "kvq_act", "att_act", "ffn_act", "kvq_dve", "att_max", "rec_ready", "x3_ready",
         "ffn_dve", "xn_ready", "n3_ready", "z_kept", "ones_set", "ffn_w_in"))
    ctx_in = m["c1_ctx_in"]
    row_in, x2_ready = [sem(f"c1_row_in{i}") for i in range(4)], sem("c1_x2_ready")
    m["r1_shifted"], m["r1_exp"] = sem("r1_shifted"), sem("r1_exp")
    ps, ident, x, z = m["psum"], m["ident"], m["x"], m["z"]
    s_ps, pt_ps, o_ps, kq_ps, vl_ps, xy_ps, xh_ps = ps[0], ps[1], ps[2:4], ps[4], ps[5], ps[6], ps[7]
    lg = m["logits"][:, 0:NT * E1]

    def transposes(pe, bank, src):
        for k in range(KD):
            for q in range(QT):
                ins = pe.transpose(bank[:, k * S + q * P:k * S + (q + 1) * P], src[:, q, k * P:(k + 1) * P], ident[:, :])
        return ins

    def product(pe, bank, width, lhsT, rhs, n):
        for i in range(2):
            for k in range(n):
                ins = pe.matmul(bank[:, i * width:(i + 1) * width], lhsT(i, k), rhs(i, k), start=(k == 0), stop=(k == n - 1))
        return ins

    def tile(t, i):
        return t[:, i * P:(i + 1) * P]

    def pe_turn(pe, b, par, first, second, third):
        f, t = b + 1, b - 1
        cx = ctxT[:, 1 - par]
        if second:
            ge(pe, kvq_act, 3 * b + 3)
            ge(pe, att_act, 2 * b - 1)
            product(pe, s_ps, S, lambda q, k: tile(qT[:, k], q), lambda q, k: kT[:, k, :], KD).then_inc(att_job, 1)
        if first:
            ge(pe, ctx_in[1 - par], 16 * ((f - (1 - par)) // 2) + 16 if isinstance(f, int) else 8 * (f - (1 - par)) + 16)
            ge(pe, kvq_act, 3 * f)
            product(pe, kq_ps, S, lambda i, k: tile(wk[:, k], i), lambda i, k: cx[:, k, :], KC).then_inc(kvq_job, 1)
        if third:
            ge(pe, n3_ready, t + 1)
            ge(pe, ffn_act, 2 * t)
            transposes(pe, xh_ps, n3).then_inc(ffn_job, 1)
        if second:
            ge(pe, att_act, 2 * b + 1)
            transposes(pe, pt_ps, p).then_inc(att_job, 1)
        if third:
            ge(pe, ffn_act, 2 * t + 1)
            ge(pe, kvq_dve, b + 1 if second else b)
            product(pe, vl_ps, E1, lambda q, k: tile(x3_now[:, k], q),
                    lambda q, k: rw[:, k, :], KD).then_inc(ffn_job, 1)
        if first:
            ge(pe, xn_ready, f + 1)
            ge(pe, kvq_act, 3 * f - 1)
            transposes(pe, xy_ps, xn).then_inc(kvq_job, 1)
        if second:
            ge(pe, att_act, 2 * b + 2)
            ge(pe, kvq_dve, b + 1)
            ge(pe, x3_ready, b)
            for q in range(QT):
                for kt in range(QT):
                    ins = pe.matmul(o_ps[q][:, 0:D + 1], tile(pT[:, kt], q), v[:, kt, :],
                                    start=(kt == 0), stop=(kt == QT - 1))
            ins.then_inc(att_job, 1)
        if first:
            ge(pe, kvq_act, 3 * f + 2)
            product(pe, kq_ps, S, lambda i, k: tile(wq[:, k], i), lambda i, k: xnT[:, k, :], KD).then_inc(kvq_job, 1)
            ge(pe, ffn_dve, b)
            product(pe, vl_ps, D, lambda q, k: tile(cx[:, k], q), lambda q, k: wv[:, k, :], KC).then_inc(kvq_job, 1)

    def act_turn(act, b, par, first, second, third):
        f, t = b + 1, b - 1
        if second:
            ge(act, att_max, b + 1)
            ge(act, att_job, 3 * b - 1)
            for q in range(QT):
                ins = act.activation(p[:, q, :], s_ps[:, q * S:(q + 1) * S], ACT.Exp, bias=nmax[:, q:q + 1])
            ins.then_inc(att_act, 1)
        if first:
            ge(act, kvq_job, 4 * f + 1)
            for i in range(KD):
                ins = act.activation(kT[:, i, :], kq_ps[:, i * S:(i + 1) * S], ACT.Identity, bias=bqk[:, 1, i:i + 1])
            ins.then_inc(kvq_act, 1)
        if third:
            ge(act, ffn_job, 2 * t + 1)
            act.copy(x3_now.rearrange("p k s -> p (k s)"), xh_ps[:, :]).then_inc(ffn_act, 1)
        if second:
            ge(act, att_job, 3 * b + 2)
            act.copy(pT.rearrange("p k s -> p (k s)"), pt_ps[:, :]).then_inc(att_act, 1)
        if third:
            act.copy(x3T[:, :, bass.ds(t * S, S)], xh_ps[:, :].rearrange("p (k s) -> p k s", k=KD)).then_inc(ffn_act, 1)
        if first:
            ge(act, kvq_job, 4 * f + 2)
            act.copy(xnT.rearrange("p k s -> p (k s)"), xy_ps[:, :]).then_inc(kvq_act, 1)
            ge(act, kvq_job, 4 * f + 3)
            for i in range(KD):
                ins = act.activation(qT[:, i, :], kq_ps[:, i * S:(i + 1) * S], ACT.Identity, bias=bqs[:, i:i + 1],
                                     scale=D ** -0.5)
            ins.then_inc(kvq_act, 1)

    def dve_turn(dve, b, par, first, second, third):
        f, t = b + 1, b - 1
        if second:
            ge(dve, att_job, 3 * b + 1)
            dve.tensor_reduce(nmax, s_ps[:, :].rearrange("p (q k) -> p q k", q=QT), AX, ALU.max, negate=True)\
               .then_inc(att_max, 1)
        if first:
            for i, group in enumerate(ROW_GROUPS):
                if f == group[0] if isinstance(f, int) else i == len(ROW_GROUPS) - 1:
                    ge(dve, row_in[i], 16 * QT * len(group))
            dve.tensor_tensor(tile2(x, f), tile2(x, f), got[:, bass.ds(f * QT, QT), :].rearrange("p q d -> p (q d)"),
                              ALU.add).then_inc(x2_ready, 1)
            ge(dve, x2_ready, f + 1)
            dve.memset(spare, 0.0)
            ln_stats(dve, ln[0], lambda q: tile1(x, f, q), f)
            ln_variance(dve, ln[0], f)
            ge(dve, kvq_job, 4 * f - 2)
            ln_apply(dve, ln[0], lambda q: tile1(x, f, q), lambda q: xn[:, q, :], f).then_inc(xn_ready, 1)
        if third:
            ge(dve, ffn_job, 2 * t + 2)
            dve.tensor_tensor(lg[:, bass.ds(t * (QT * E1), QT * E1)].rearrange("p (q e) -> p q e", q=QT),
                              vl_ps[:, 0:QT * E1].rearrange("p (q e) -> p q e", q=QT),
                              rb.unsqueeze(1).to_broadcast([P, QT, E1]), ALU.add).then_inc(ffn_dve, 1)
        if second:
            ge(dve, att_job, 3 * b + 3)
            for q in range(QT):
                ins = dve.reciprocal(rec[:, q:q + 1], o_ps[q][:, D:D + 1])
            ins.then_inc(rec_ready, 1)
            ge(dve, rec_ready, b + 1)
            for q in range(QT):
                ins = dve.scalar_tensor_tensor(tile1(x, b, q), o_ps[q][:, 0:D], rec[:, q:q + 1], tile1(x, b, q),
                                               ALU.mult, ALU.add)
            ins.then_inc(x3_ready, 1)
            ge(dve, x3_ready, b + 1)
            dve.memset(spare, 0.0)
            ln_stats(dve, ln[1], lambda q: tile1(x, b, q), b)
            ln_variance(dve, ln[1], b)
        if first:
            ge(dve, kvq_job, 4 * f + 4)
            dve.tensor_tensor(v[:, :, 0:D], vl_ps[:, :].rearrange("p (q d) -> p q d", q=QT),
                              bv.unsqueeze(1).to_broadcast([P, QT, D]), ALU.add).then_inc(kvq_dve, 1)
        if second:
            ge(dve, z_kept, b)
            ge(dve, ffn_job, 2 * b - 1)
            ln_apply(dve, ln[1], lambda q: tile1(x, b, q), lambda q: n3[:, q, :], b).then_inc(n3_ready, 1)

    def rows(pool, i):
        for t in range(ROW_GROUPS[i][0] * QT, (ROW_GROUPS[i][-1] + 1) * QT):
            pool.indirect_dma_start(got[:, t, :], None, m["ys0"],
                                    bass.IndirectOffsetOnAxis(m["slots"][:, 0, t:t + 1], 0)).then_inc(row_in[i], 16)

    def pool_turn(pool, b, par, first, second, third):
        if first:
            ln_power(pool, ln[0], b + 1)
        if isinstance(b, int) and b in (-1, 0):
            rows(pool, b + 3)
        if second:
            ln_power(pool, ln[1], b)
            ge(pool, n3_ready, b + 1)
            pool.tensor_tensor(pool_spare, m["power"][:, 0:1], m["power"][:, 0:1], ALU.mult)
            pool.tensor_copy(tile2(z, b), n3.rearrange("p q d -> p (q d)")).then_inc(z_kept, 1)

    def turns(eng, turn):
        turn(eng, -1, 1, True, False, False)
        turn(eng, 0, 0, True, True, False)
        turn(eng, 1, 1, True, True, True)
        turn(eng, 2, 0, True, True, True)
        with eng.Fori(1, B // 2 - 1) as i:
            turn(eng, i * 2 + 1, 1, True, True, True)
            turn(eng, i * 2 + 2, 0, True, True, True)
        turn(eng, B - 1, 1, False, True, True)
        turn(eng, B, 0, False, False, True)

    with nc.Block() as block:
        @block.sync
        def _(sp):
            for dst, name in ((sw1, "sw1"), (sw2, "sw2"), (sb1, "sb1")):
                sp.dma_start(dst, a[name]).then_inc(w_in, 16)
            with sp.Fori(0, B // 2 - 1) as i:
                for par in range(2):
                    sp.wait_ge(kvq_job, i * 8 + (4 * par + 4))
                    sp.dma_start(ctxT[:, par], a["ctxT"][bass.ds(i * 2 + (par + 2), 1)].rearrange("o p k s -> (o p) k s"))\
                      .then_inc(ctx_in[par], 16)
                    words = E1 * KD * HID1
                    part = words // (B - 2)
                    for j, name in enumerate(("ew1", "ew2")):
                        sp.dma_start(m["w1"][:, bass.ds(i * (2 * part) + (par * part + j * words), part)],
                                     a[name][:, bass.ds(i * (2 * part) + par * part, part)]).then_inc(m["we_in"], 16)
            sp.wait_ge(w_in, 48)

        @block.gpsimd
        def _(pool):
            pool.memset(v[:, :, D:D + 1], 1.0).then_inc(ones_set, 1)
            rows(pool, 0)
            rows(pool, 1)
            turns(pool, pool_turn)

        @block.tensor
        def _(pe):
            pe.wait_ge(m["c1_w_in"], 16 * 7)
            pe.wait_ge(ones_set, 2)
            turns(pe, pe_turn)

        @block.scalar
        def _(act):
            act.wait_ge(m["c1_w_in"], 16 * 7)
            act.mul(bqs, bqk[:, 0, :], D ** -0.5).then_inc(ones_set, 1)
            turns(act, act_turn)

        @block.vector
        def _(dve):
            dve.wait_ge(m["c1_w_in"], 16 * 7)
            turns(dve, dve_turn)


def join1(nc, a, m, out):
    got = Carve(m["w2"], m["W1WORDS"]).take(P, TOP1, NT, D)
    sem = m["sem"]
    groups = [range(0, 6), range(6, 10), range(10, 14), range(14, NT)]
    row_in, joined, stored = [sem(f"j1_row_in{i}") for i in range(len(groups))], sem("j1_joined"), sem("j1_stored")
    x = m["x"]
    with nc.Block() as block:
        @block.sync
        def _(sp):
            for b in range(B):
                sp.wait_ge(joined, (QT * TOP1) * (b + 1))
                sp.dma_start(out[:, b * QT * D:(b + 1) * QT * D], tile2(x, b)).then_inc(stored, 16)
            sp.wait_ge(stored, 16 * B)

        @block.gpsimd
        def _(pool):
            for i, group in enumerate(groups):
                for t in group:
                    for k in range(TOP1):
                        pool.indirect_dma_start(got[:, k, t, :], None, m["ys1"],
                                                bass.IndirectOffsetOnAxis(m["slots"][:, k, t:t + 1], 0))\
                            .then_inc(row_in[i], 16)

        @block.vector
        def _(dve):
            for i, group in enumerate(groups):
                dve.wait_ge(row_in[i], 16 * TOP1 * len(group))
                for t0 in range(group[0], group[-1] + 1, QT):
                    for k in range(TOP1):
                        tiles = [t for t in (t0, t0 + 1) if t in group]
                        for t in tiles:
                            if k:
                                dve.wait_ge(joined, TOP1 * t0 + len(tiles) * (k - 1) + (t - t0) + 1)
                            dve.scalar_tensor_tensor(x[:, t * D:(t + 1) * D], got[:, k, t, :], m["top_p"][:, k, t:t + 1],
                                                     x[:, t * D:(t + 1) * D], ALU.mult, ALU.add).then_inc(joined, 1)



def kernel(**inputs):
    import numpy as np
    import concourse.bacc as bacc
    from concourse import mybir as mb
    from concourse.bass_utils import run_bass_kernel_spmd as run
    import ml_dtypes

    x = {k: np.asarray(v) for k, v in inputs.items()}

    def part(w, p=P):
        return np.ascontiguousarray(w.reshape(w.shape[0] // p, p, -1).transpose(1, 0, 2))

    def cols(v):
        return np.ascontiguousarray(v.reshape(-1, P).T)

    def spread_heads(w):
        return part(w.reshape(D, 2, H1 // 2, DH1).transpose(0, 1, 3, 2).reshape(D, D))

    qkv = x["L0_ffn_w_qkv"]
    arrays = {
        "x": part(x["x"].reshape(B * S, D)).reshape(P, NT * D),
        "ctxT": np.ascontiguousarray(x["ctx_768"].reshape(B, S, KC, CP).transpose(0, 3, 2, 1)),
        "wq0": part(x["L0_xattn_Wq"]), "wk0": part(x["L0_xattn_Wk"], CP), "wv0": part(x["L0_xattn_Wv"], CP),
        "wo0": part(x["L0_xattn_Wo"]), "bo0": x["L0_xattn_bo"],
        "s_wq": spread_heads(qkv[:, 0:D]), "s_wk": spread_heads(qkv[:, D:2 * D]), "s_wv": part(qkv[:, 2 * D:]),
        "s_wp": part(x["L0_ffn_w_proj"]),
        "s_ln1": np.ascontiguousarray(np.stack([cols(x["L0_ffn_ln1_w"]), cols(x["L0_ffn_ln1_b"])], axis=1)),
        "s_ln2": np.ascontiguousarray(np.stack([cols(x["L0_ffn_ln2_w"]), cols(x["L0_ffn_ln2_b"])], axis=1)),
        "s_ln2w": x["L0_ffn_ln2_w"], "s_ln2b": x["L0_ffn_ln2_b"],
        "s_gw": part(x["L0_ffn_gate_w"]), "s_gb": x["L0_ffn_gate_b"],
        "w1": np.stack([part(w).reshape(P, -1) for w in x["L0_ffn_w1"]]),
        "w2": np.stack([part(w).reshape(P, -1) for w in x["L0_ffn_w2"]]),
        "wq1": part(x["L1_xattn_Wq"]), "wk1": part(x["L1_xattn_Wk"], CP), "wv1": part(x["L1_xattn_Wv"], CP),
        "bqk1": np.ascontiguousarray(np.stack([cols(x["L1_xattn_bq"]), cols(x["L1_xattn_bk"])], axis=1)),
        "bv1": x["L1_xattn_bv"], "rw": part(x["L1_ffn_router_W"]), "rb": x["L1_ffn_router_b"],
        "sw1": part(x["L1_ffn_sW1"]), "sw2": part(x["L1_ffn_sW2"]), "sb1": cols(x["L1_ffn_sb1"]),
        "ew1": np.ascontiguousarray(np.stack([part(w).reshape(P, -1) for w in x["L1_ffn_eW1"]], axis=1)).reshape(P, -1),
        "ew2": np.ascontiguousarray(np.stack([part(w).reshape(P, -1) for w in x["L1_ffn_eW2"]], axis=1)).reshape(P, -1),
        "eb1T": np.ascontiguousarray(x["L1_ffn_eb1"].reshape(E1 * M1, P).T),
        "b2": np.ascontiguousarray(np.concatenate([x["L1_ffn_eb2"], x["L1_ffn_sb2"][None]], axis=0)),
        "ident": np.eye(P, dtype=np.float32),
        "upper": np.triu(np.ones((P, P)), 1).astype(ml_dtypes.bfloat16),
        "ones": np.ones((P, P)).astype(ml_dtypes.bfloat16),
    }
    for i, (e, tiles) in enumerate(((E0, TILES0), (E1, TILES1))):
        arrays[f"incl{i}"] = np.tril(np.ones((e, e), np.float32)).reshape(-1)
        arrays[f"rank{i}"] = (e - np.arange(e)).astype(np.float32)
        arrays[f"steps{i}"] = (P * np.arange(NC)).astype(np.float32)
        arrays[f"jx{i}"] = np.arange(tiles).astype(np.float32)

    nc = bacc.Bacc("TRN2", target_bir_lowering=False, num_devices=1)
    args = {k: nc.dram_tensor("in_" + k, v.shape, mb.dt.from_np(v.dtype), kind="ExternalInput").ap()
            for k, v in arrays.items()}
    out = nc.dram_tensor("out", (P, NT * D), mb.dt.float32, kind="ExternalOutput").ap()
    build(nc, args, out)
    r = run(nc, [{"in_" + k: v for k, v in arrays.items()}], core_ids=[0])
    got = np.asarray(r.results[0]["out"])
    return np.ascontiguousarray(got.reshape(P, NT, D).transpose(1, 0, 2)).reshape(B, S, D)
```
